# Optimizing a Trainium2 kernel written in Bass

```python
import numpy as np
import jax
import jax.numpy as jnp

def _softmax(x, axis=-1):
    return jax.nn.softmax(x, axis=axis)

def _gelu(x):
    return jax.nn.gelu(x, approximate=True)

def _silu(x):
    return jax.nn.silu(x)

def _sigmoid(x):
    return jax.nn.sigmoid(x)

def _layernorm(x, axis=-1, eps=1e-05):
    m = jnp.mean(x, axis=axis, keepdims=True)
    v = jnp.var(x, axis=axis, keepdims=True)
    return (x - m) / jnp.sqrt(v + eps)

def _scatter_add(tgt, idx, src, axis=0):
    return tgt.at[idx].add(src)

def _segment_sum(src, seg, n):
    return jax.ops.segment_sum(src, seg, n)
kernel_name = 'mk_xattn_ffn_d4_seqx_r8_bd74b4'

def setup_inputs(seed: int=0):
    np.random.seed(seed)
    _w = jnp.asarray

    def _rec_inputs():
        import jax
        import jax.numpy as jnp
        _rk = jax.random.key(seed)
        x = -0.0003929 + 0.9999 * jax.random.normal(jax.random.fold_in(_rk, 1), (16, 128, 128), jnp.float32)
        _lenS = 128 - jax.random.randint(jax.random.fold_in(_rk, 7), (16,), 0, max(1, 128 // 4) + 1, jnp.int32)
        _lenS2 = 77 - jax.random.randint(jax.random.fold_in(_rk, 8), (16,), 0, max(1, 77 // 4) + 1, jnp.int32)
        _ctx_1024P = jax.random.normal(jax.random.fold_in(_rk, 11), (16, 16, 128), jnp.float32)
        _ctx_1024c = jax.random.dirichlet(jax.random.fold_in(_rk, 511), 0.3 * jnp.ones((16,), jnp.float32), (16, 77))
        _ctx_1024t = jnp.einsum('bsk,bkd->bsd', _ctx_1024c, _ctx_1024P)
        _ctx_1024t = _ctx_1024t * jax.lax.rsqrt(jnp.mean(jnp.square(_ctx_1024t)) + 1e-12) * 0.953939
        ctx_1024 = 2.81802e-05 + 1.00001 * (_ctx_1024t + 0.3 * jax.random.normal(jax.random.fold_in(_rk, 611), (16, 77, 128), jnp.float32))
        _validS = jnp.arange(128)[None, :] < _lenS[:, None]
        _validS2 = jnp.arange(77)[None, :] < _lenS2[:, None]
        _causal = jnp.tril(jnp.ones((128, 128), dtype=bool))
        mask_BxSxS2_ik0 = jnp.where(jnp.broadcast_to(_validS2[:, None, :], (16, 128, 77)), 0, 1).astype(jnp.int32)
        mask_BxS2_bk0 = jnp.logical_not(jnp.broadcast_to(_validS2[:, :], (16, 77)))
        return (x, ctx_1024, mask_BxSxS2_ik0, mask_BxS2_bk0)
    x, ctx_1024, mask_BxSxS2_ik0, mask_BxS2_bk0 = _rec_inputs()

    def _L0_xattn_setup():
        import jax, jax.numpy as jnp
        import numpy as np
        NEG = -1000000.0
        key = jax.random.key(seed)
        k1, k2, k3, k4, k5 = jax.random.split(key, 5)
        B, Lq, Lm, Din, Dout = (8, 256, 256, 128, 128)
        query = jax.random.normal(k1, (B, Lq, Din), dtype=jnp.float32)
        memories = jax.random.normal(k2, (B, Lm, Dout), dtype=jnp.float32)
        mask = jax.random.randint(k3, (B, Lq, Lm), 0, 2, dtype=jnp.int32)
        bound = 1.0 / np.sqrt(Din)
        W = jax.random.uniform(k4, (Dout, Din), minval=-bound, maxval=bound, dtype=jnp.float32)
        b = jax.random.uniform(k5, (Dout,), minval=-bound, maxval=bound, dtype=jnp.float32)
        return {'query': query, 'memories': memories, 'mask': mask, 'W': W, 'b': b}
    _L0_xattn_all = _L0_xattn_setup()
    _L0_xattn_in = {k: v for k, v in _L0_xattn_all.items() if k in ('W', 'b')}
    del _L0_xattn_all

    def _L0_ffn_setup():
        import jax, jax.numpy as jnp
        import numpy as np
        H = 128
        I = 128
        E = 8
        key = jax.random.key(seed)
        ks = jax.random.split(key, 8)
        s = 0.02
        x = jax.random.normal(ks[0], (4, 256, H), dtype=jnp.float32)
        Wg = jax.random.normal(ks[1], (H, E), dtype=jnp.float32) * s
        bg = jnp.zeros((E,), dtype=jnp.float32)
        W1 = jax.random.normal(ks[2], (E, H, I), dtype=jnp.float32) * s
        b1 = jnp.zeros((E, I), dtype=jnp.float32)
        W2 = jax.random.normal(ks[3], (E, I, H), dtype=jnp.float32) * s
        b2 = jnp.zeros((E, H), dtype=jnp.float32)
        return {'x': x, 'Wg': Wg, 'bg': bg, 'W1': W1, 'b1': b1, 'W2': W2, 'b2': b2}
    _L0_ffn_all = _L0_ffn_setup()
    _L0_ffn_in = {k: v for k, v in _L0_ffn_all.items() if k in ('Wg', 'bg', 'W1', 'b1', 'W2', 'b2')}
    del _L0_ffn_all

    def _L1_xattn_setup():
        import jax, jax.numpy as jnp
        import numpy as np
        B, S, D, H, DK = (4, 256, 128, 16, 64)

        def _proj(x, W, b):
            y = jnp.einsum('bsd,ed->bse', x, W) + b
            return y.reshape(x.shape[0], x.shape[1], H, DK).transpose(0, 2, 1, 3)
        key = jax.random.key(seed)
        ks = jax.random.split(key, 10)
        scale = 1.0 / np.sqrt(D)
        return {'input_Q': jax.random.normal(ks[0], (B, S, D), jnp.float32), 'input_K': jax.random.normal(ks[1], (B, S, D), jnp.float32), 'input_V': jax.random.normal(ks[2], (B, S, D), jnp.float32), 'Wq': jax.random.normal(ks[3], (H * DK, D), jnp.float32) * scale, 'bq': jax.random.normal(ks[4], (H * DK,), jnp.float32) * scale, 'Wk': jax.random.normal(ks[5], (H * DK, D), jnp.float32) * scale, 'bk': jax.random.normal(ks[6], (H * DK,), jnp.float32) * scale, 'Wv': jax.random.normal(ks[7], (H * DK, D), jnp.float32) * scale, 'bv': jax.random.normal(ks[8], (H * DK,), jnp.float32) * scale, 'Wo': jax.random.normal(ks[9], (D, H * DK), jnp.float32) * scale}
    _L1_xattn_all = _L1_xattn_setup()
    _L1_xattn_in = {k: v for k, v in _L1_xattn_all.items() if k in ('Wq', 'bq', 'Wk', 'bk', 'Wv', 'bv', 'Wo')}
    del _L1_xattn_all

    def _L1_ffn_setup():
        import jax, jax.numpy as jnp
        import numpy as np
        E = 8
        TOP_K = 2
        H = 128
        F = 512
        LN_EPS = 1e-12
        key = jax.random.key(seed)
        ks = jax.random.split(key, 9)
        s = lambda k, shape, scale: jax.random.normal(k, shape, dtype=jnp.float32) * scale
        return {'hidden_states': s(ks[0], (4, 256, H), 1.0), 'Wr': s(ks[1], (E, H), 0.02), 'br': jnp.zeros((E,), jnp.float32), 'W1': s(ks[2], (E, F, H), 0.02), 'b1': jnp.zeros((E, F), jnp.float32), 'W2': s(ks[3], (E, H, F), 0.02), 'b2': jnp.zeros((E, H), jnp.float32), 'ln_w': jnp.ones((H,), jnp.float32), 'ln_b': jnp.zeros((H,), jnp.float32)}
    _L1_ffn_all = _L1_ffn_setup()
    _L1_ffn_in = {k: v for k, v in _L1_ffn_all.items() if k in ('Wr', 'br', 'W1', 'b1', 'W2', 'b2', 'ln_w', 'ln_b')}
    del _L1_ffn_all

    def _L2_xattn_setup():
        import jax, jax.numpy as jnp
        import numpy as np
        import math
        B, SQ, SK, D = (4, 256, 256, 128)
        key = jax.random.key(seed)
        ks = jax.random.split(key, 9)
        s = 1.0 / math.sqrt(D)
        return {'q': jax.random.normal(ks[0], (B, SQ, D), jnp.float32), 'k': jax.random.normal(ks[1], (B, SK, D), jnp.float32), 'v': jax.random.normal(ks[2], (B, SK, D), jnp.float32), 'Wq': jax.random.normal(ks[3], (D, D), jnp.float32) * s, 'bq': jax.random.normal(ks[4], (D,), jnp.float32) * s, 'Wk': jax.random.normal(ks[5], (D, D), jnp.float32) * s, 'bk': jax.random.normal(ks[6], (D,), jnp.float32) * s, 'Wv': jax.random.normal(ks[7], (D, D), jnp.float32) * s, 'bv': jax.random.normal(ks[8], (D,), jnp.float32) * s}
    _L2_xattn_all = _L2_xattn_setup()
    _L2_xattn_in = {k: v for k, v in _L2_xattn_all.items() if k in ('Wq', 'bq', 'Wk', 'bk', 'Wv', 'bv')}
    del _L2_xattn_all

    def _L2_ffn_setup():
        import jax, jax.numpy as jnp
        import numpy as np
        D_MODEL, D_FF, RANK = (128, 512, 32)
        B, S = (4, 512)
        key = jax.random.key(seed)
        ks = jax.random.split(key, 7)
        return {'x': jax.random.normal(ks[0], (B, S, D_MODEL), dtype=jnp.float32), 'U1': jax.random.normal(ks[1], (D_MODEL, RANK), dtype=jnp.float32) * 0.02, 'V1': jax.random.normal(ks[2], (RANK, D_FF), dtype=jnp.float32) * 0.02, 'b1': jnp.zeros((D_FF,), dtype=jnp.float32), 'U2': jax.random.normal(ks[3], (D_FF, RANK), dtype=jnp.float32) * 0.02, 'V2': jax.random.normal(ks[4], (RANK, D_MODEL), dtype=jnp.float32) * 0.02, 'b2': jnp.zeros((D_MODEL,), dtype=jnp.float32)}
    _L2_ffn_all = _L2_ffn_setup()
    _L2_ffn_in = {k: v for k, v in _L2_ffn_all.items() if k in ('U1', 'V1', 'b1', 'U2', 'V2', 'b2')}
    del _L2_ffn_all

    def _L3_xattn_setup():
        import jax, jax.numpy as jnp
        import numpy as np
        HEADS = 8
        DIM_HEAD = 64
        SCALE = DIM_HEAD ** (-0.5)
        LN_EPS = 1e-05
        NEG_INF = -1e+30

        def layernorm(x, gamma, beta):
            mu = jnp.mean(x, axis=-1, keepdims=True)
            var = jnp.var(x, axis=-1, keepdims=True)
            return (x - mu) * jax.lax.rsqrt(var + LN_EPS) * gamma + beta
        key = jax.random.key(seed)
        ks = jax.random.split(key, 8)
        b, f, n, d, inner = (8, 1024, 64, 128, HEADS * DIM_HEAD)
        x = jax.random.normal(ks[0], (b, f, d), dtype=jnp.float32)
        latents = jax.random.normal(ks[1], (b, n, d), dtype=jnp.float32)
        key_padding_mask = jax.random.randint(ks[2], (b, f), 0, 2) > 0
        s = 0.02
        return {'x': x, 'latents': latents, 'key_padding_mask': key_padding_mask, 'kv_gate': jnp.float32(-4.0), 'gamma_media': jnp.ones((d,), jnp.float32), 'beta_media': jnp.zeros((d,), jnp.float32), 'gamma_lat': jnp.ones((d,), jnp.float32), 'beta_lat': jnp.zeros((d,), jnp.float32), 'Wq': jax.random.normal(ks[3], (d, inner), jnp.float32) * s, 'Wk': jax.random.normal(ks[4], (d, inner), jnp.float32) * s, 'Wv': jax.random.normal(ks[5], (d, inner), jnp.float32) * s, 'Wout': jax.random.normal(ks[6], (inner, d), jnp.float32) * s}
    _L3_xattn_all = _L3_xattn_setup()
    _L3_xattn_in = {k: v for k, v in _L3_xattn_all.items() if k in ('kv_gate', 'gamma_media', 'beta_media', 'gamma_lat', 'beta_lat', 'Wq', 'Wk', 'Wv', 'Wout')}
    del _L3_xattn_all

    def _L3_ffn_setup():
        import jax, jax.numpy as jnp
        import numpy as np
        B, S, H, NH, E, F = (4, 128, 128, 16, 8, 512)
        D = H // NH
        EPS = 1e-05

        def _layernorm(x, g, b):
            mu = jnp.mean(x, axis=-1, keepdims=True)
            var = jnp.var(x, axis=-1, keepdims=True)
            return (x - mu) * jax.lax.rsqrt(var + EPS) * g + b
        key = jax.random.key(seed)
        ks = jax.random.split(key, 16)
        s = 0.02
        return {'x': jax.random.normal(ks[0], (B, S, H), jnp.float32), 'ln1_g': jnp.ones((H,), jnp.float32), 'ln1_b': jnp.zeros((H,), jnp.float32), 'ln2_g': jnp.ones((H,), jnp.float32), 'ln2_b': jnp.zeros((H,), jnp.float32), 'wq': jax.random.normal(ks[1], (H, H), jnp.float32) * s, 'bq': jnp.zeros((H,), jnp.float32), 'wk': jax.random.normal(ks[2], (H, H), jnp.float32) * s, 'bk': jnp.zeros((H,), jnp.float32), 'wv': jax.random.normal(ks[3], (H, H), jnp.float32) * s, 'bv': jnp.zeros((H,), jnp.float32), 'wo': jax.random.normal(ks[4], (H, H), jnp.float32) * s, 'bo': jnp.zeros((H,), jnp.float32), 'gate_w': jax.random.normal(ks[5], (H, E), jnp.float32) * s, 'gate_b': jnp.zeros((E,), jnp.float32), 'w1': jax.random.normal(ks[6], (E, H, F), jnp.float32) * s, 'b1': jnp.zeros((E, F), jnp.float32), 'w2': jax.random.normal(ks[7], (E, F, H), jnp.float32) * s, 'b2': jnp.zeros((E, H), jnp.float32)}
    _L3_ffn_all = _L3_ffn_setup()
    _L3_ffn_in = {k: v for k, v in _L3_ffn_all.items() if k in ('ln1_g', 'ln1_b', 'ln2_g', 'ln2_b', 'wq', 'bq', 'wk', 'bk', 'wv', 'bv', 'wo', 'bo', 'gate_w', 'gate_b', 'w1', 'b1', 'w2', 'b2')}
    del _L3_ffn_all
    return {'x': x, 'ctx_1024': ctx_1024, 'mask_BxSxS2_ik0': mask_BxSxS2_ik0, 'mask_BxS2_bk0': mask_BxS2_bk0, 'L0_xattn_W': _L0_xattn_in['W'], 'L0_xattn_b': _L0_xattn_in['b'], 'L0_ffn_Wg': _L0_ffn_in['Wg'], 'L0_ffn_bg': _L0_ffn_in['bg'], 'L0_ffn_W1': _L0_ffn_in['W1'], 'L0_ffn_b1': _L0_ffn_in['b1'], 'L0_ffn_W2': _L0_ffn_in['W2'], 'L0_ffn_b2': _L0_ffn_in['b2'], 'L1_xattn_Wq': _L1_xattn_in['Wq'], 'L1_xattn_bq': _L1_xattn_in['bq'], 'L1_xattn_Wk': _L1_xattn_in['Wk'], 'L1_xattn_bk': _L1_xattn_in['bk'], 'L1_xattn_Wv': _L1_xattn_in['Wv'], 'L1_xattn_bv': _L1_xattn_in['bv'], 'L1_xattn_Wo': _L1_xattn_in['Wo'], 'L1_ffn_Wr': _L1_ffn_in['Wr'], 'L1_ffn_br': _L1_ffn_in['br'], 'L1_ffn_W1': _L1_ffn_in['W1'], 'L1_ffn_b1': _L1_ffn_in['b1'], 'L1_ffn_W2': _L1_ffn_in['W2'], 'L1_ffn_b2': _L1_ffn_in['b2'], 'L1_ffn_ln_w': _L1_ffn_in['ln_w'], 'L1_ffn_ln_b': _L1_ffn_in['ln_b'], 'L2_xattn_Wq': _L2_xattn_in['Wq'], 'L2_xattn_bq': _L2_xattn_in['bq'], 'L2_xattn_Wk': _L2_xattn_in['Wk'], 'L2_xattn_bk': _L2_xattn_in['bk'], 'L2_xattn_Wv': _L2_xattn_in['Wv'], 'L2_xattn_bv': _L2_xattn_in['bv'], 'L2_ffn_U1': _L2_ffn_in['U1'], 'L2_ffn_V1': _L2_ffn_in['V1'], 'L2_ffn_b1': _L2_ffn_in['b1'], 'L2_ffn_U2': _L2_ffn_in['U2'], 'L2_ffn_V2': _L2_ffn_in['V2'], 'L2_ffn_b2': _L2_ffn_in['b2'], 'L3_xattn_kv_gate': _L3_xattn_in['kv_gate'], 'L3_xattn_gamma_media': _L3_xattn_in['gamma_media'], 'L3_xattn_beta_media': _L3_xattn_in['beta_media'], 'L3_xattn_gamma_lat': _L3_xattn_in['gamma_lat'], 'L3_xattn_beta_lat': _L3_xattn_in['beta_lat'], 'L3_xattn_Wq': _L3_xattn_in['Wq'], 'L3_xattn_Wk': _L3_xattn_in['Wk'], 'L3_xattn_Wv': _L3_xattn_in['Wv'], 'L3_xattn_Wout': _L3_xattn_in['Wout'], 'L3_ffn_ln1_g': _L3_ffn_in['ln1_g'], 'L3_ffn_ln1_b': _L3_ffn_in['ln1_b'], 'L3_ffn_ln2_g': _L3_ffn_in['ln2_g'], 'L3_ffn_ln2_b': _L3_ffn_in['ln2_b'], 'L3_ffn_wq': _L3_ffn_in['wq'], 'L3_ffn_bq': _L3_ffn_in['bq'], 'L3_ffn_wk': _L3_ffn_in['wk'], 'L3_ffn_bk': _L3_ffn_in['bk'], 'L3_ffn_wv': _L3_ffn_in['wv'], 'L3_ffn_bv': _L3_ffn_in['bv'], 'L3_ffn_wo': _L3_ffn_in['wo'], 'L3_ffn_bo': _L3_ffn_in['bo'], 'L3_ffn_gate_w': _L3_ffn_in['gate_w'], 'L3_ffn_gate_b': _L3_ffn_in['gate_b'], 'L3_ffn_w1': _L3_ffn_in['w1'], 'L3_ffn_b1': _L3_ffn_in['b1'], 'L3_ffn_w2': _L3_ffn_in['w2'], 'L3_ffn_b2': _L3_ffn_in['b2']}

def reference(x, ctx_1024, mask_BxSxS2_ik0, mask_BxS2_bk0, L0_xattn_W, L0_xattn_b, L0_ffn_Wg, L0_ffn_bg, L0_ffn_W1, L0_ffn_b1, L0_ffn_W2, L0_ffn_b2, L1_xattn_Wq, L1_xattn_bq, L1_xattn_Wk, L1_xattn_bk, L1_xattn_Wv, L1_xattn_bv, L1_xattn_Wo, L1_ffn_Wr, L1_ffn_br, L1_ffn_W1, L1_ffn_b1, L1_ffn_W2, L1_ffn_b2, L1_ffn_ln_w, L1_ffn_ln_b, L2_xattn_Wq, L2_xattn_bq, L2_xattn_Wk, L2_xattn_bk, L2_xattn_Wv, L2_xattn_bv, L2_ffn_U1, L2_ffn_V1, L2_ffn_b1, L2_ffn_U2, L2_ffn_V2, L2_ffn_b2, L3_xattn_kv_gate, L3_xattn_gamma_media, L3_xattn_beta_media, L3_xattn_gamma_lat, L3_xattn_beta_lat, L3_xattn_Wq, L3_xattn_Wk, L3_xattn_Wv, L3_xattn_Wout, L3_ffn_ln1_g, L3_ffn_ln1_b, L3_ffn_ln2_g, L3_ffn_ln2_b, L3_ffn_wq, L3_ffn_bq, L3_ffn_wk, L3_ffn_bk, L3_ffn_wv, L3_ffn_bv, L3_ffn_wo, L3_ffn_bo, L3_ffn_gate_w, L3_ffn_gate_b, L3_ffn_w1, L3_ffn_b1, L3_ffn_w2, L3_ffn_b2):
    import jax
    import jax.numpy as jnp

    def _L0_xattn_ref(query, memories, mask, W, b):
        import jax, jax.numpy as jnp
        import numpy as np
        NEG = -1000000.0
        q = jnp.einsum('bqi,oi->bqo', query, W) + b
        add_mask = (1.0 - mask.astype(q.dtype)) * NEG
        logits = jnp.einsum('bqd,bmd->bqm', q, memories) + add_mask
        weights = jax.nn.softmax(logits, axis=-1)
        out = jnp.einsum('bqm,bmd->bqd', weights, memories)
        return out

    def _L0_ffn_ref(x, Wg, bg, W1, b1, W2, b2):
        import jax, jax.numpy as jnp
        import numpy as np
        H = 128
        I = 128
        E = 8
        B, S, Hd = x.shape
        xf = x.reshape(-1, Hd)
        logits = xf @ Wg + bg
        gates = jax.nn.softmax(logits, axis=-1)
        idx = jnp.argmax(gates, axis=-1)
        h = jax.nn.gelu(jnp.einsum('th,ehi->tei', xf, W1) + b1, approximate=False)
        y = jnp.einsum('tei,eih->teh', h, W2) + b2
        out = jnp.take_along_axis(y, idx[:, None, None], axis=1)[:, 0, :]
        return out.reshape(B, S, Hd)

    def _L1_xattn_ref(input_Q, input_K, input_V, Wq, bq, Wk, bk, Wv, bv, Wo):
        import jax, jax.numpy as jnp
        import numpy as np
        B, S, D, H, DK = (4, 256, 128, 16, 64)

        def _proj(x, W, b):
            y = jnp.einsum('bsd,ed->bse', x, W) + b
            return y.reshape(x.shape[0], x.shape[1], H, DK).transpose(0, 2, 1, 3)
        Q = _proj(input_Q, Wq, bq)
        K = _proj(input_K, Wk, bk)
        V = _proj(input_V, Wv, bv)
        scores = jnp.einsum('bhqd,bhkd->bhqk', Q, K) / np.sqrt(DK).astype(np.float32)
        attn = jax.nn.softmax(scores, axis=-1)
        context = jnp.einsum('bhqk,bhkd->bhqd', attn, V)
        context = context.transpose(0, 2, 1, 3).reshape(input_Q.shape[0], -1, H * DK)
        return jnp.einsum('bse,de->bsd', context, Wo)

    def _L1_ffn_ref(hidden_states, Wr, br, W1, b1, W2, b2, ln_w, ln_b):
        import jax, jax.numpy as jnp
        import numpy as np
        E = 8
        TOP_K = 2
        H = 128
        F = 512
        LN_EPS = 1e-12
        bsz, seqlen, h = hidden_states.shape
        x = hidden_states.reshape(-1, h)
        logits = x @ Wr.T + br
        topk_vals, topk_idx = jax.lax.top_k(logits, TOP_K)
        topk_w = jax.nn.softmax(topk_vals, axis=-1)
        out = jnp.zeros_like(x)
        for e in range(E):
            cw = jnp.sum(topk_w * (topk_idx == e), axis=-1)
            y = jax.nn.gelu(x @ W1[e].T + b1[e], approximate=False) @ W2[e].T + b2[e]
            out = out + cw[:, None] * y
        z = out + x
        mu = jnp.mean(z, axis=-1, keepdims=True)
        var = jnp.mean(jnp.square(z - mu), axis=-1, keepdims=True)
        z = (z - mu) * jax.lax.rsqrt(var + LN_EPS) * ln_w + ln_b
        return z.reshape(bsz, seqlen, h)

    def _L2_xattn_ref(q, k, v, Wq, bq, Wk, bk, Wv, bv):
        import jax, jax.numpy as jnp
        import numpy as np
        import math
        B, SQ, SK, D = (4, 256, 256, 128)
        qp = jnp.einsum('bsd,ed->bse', q, Wq) + bq
        kp = jnp.einsum('bsd,ed->bse', k, Wk) + bk
        vp = jnp.einsum('bsd,ed->bse', v, Wv) + bv
        scale = 1.0 / jnp.sqrt(jnp.asarray(kp.shape[-1], qp.dtype))
        scores = jnp.einsum('bqd,bkd->bqk', qp, kp) * scale
        attn = jax.nn.softmax(scores, axis=-1)
        return jnp.einsum('bqk,bkd->bqd', attn, vp)

    def _L2_ffn_ref(x, U1, V1, b1, U2, V2, b2):
        import jax, jax.numpy as jnp
        import numpy as np
        D_MODEL, D_FF, RANK = (128, 512, 32)
        B, S = (4, 512)
        P = jnp.einsum('bsd,dr->bsr', x, U1)
        H = jax.nn.gelu(jnp.einsum('bsr,rf->bsf', P, V1) + b1)
        Q = jnp.einsum('bsf,fr->bsr', H, U2)
        return jnp.einsum('bsr,rd->bsd', Q, V2) + b2

    def _L3_xattn_ref(x, latents, key_padding_mask, kv_gate, gamma_media, beta_media, gamma_lat, beta_lat, Wq, Wk, Wv, Wout):
        import jax, jax.numpy as jnp
        import numpy as np
        HEADS = 8
        DIM_HEAD = 64
        SCALE = DIM_HEAD ** (-0.5)
        LN_EPS = 1e-05
        NEG_INF = -1e+30

        def layernorm(x, gamma, beta):
            mu = jnp.mean(x, axis=-1, keepdims=True)
            var = jnp.var(x, axis=-1, keepdims=True)
            return (x - mu) * jax.lax.rsqrt(var + LN_EPS) * gamma + beta
        b, f, d = x.shape
        n = latents.shape[1]
        x = layernorm(x, gamma_media, beta_media)
        latents = layernorm(latents, gamma_lat, beta_lat)
        kv = jnp.concatenate((x, latents * kv_gate), axis=1)
        q = (latents @ Wq).reshape(b, n, HEADS, DIM_HEAD)
        k = (kv @ Wk).reshape(b, f + n, HEADS, DIM_HEAD)
        v = (kv @ Wv).reshape(b, f + n, HEADS, DIM_HEAD)
        sim = jnp.einsum('bqhd,bkhd->bhqk', q * SCALE, k)
        sim = sim - jax.lax.stop_gradient(jnp.max(sim, axis=-1, keepdims=True))
        valid_feat = ~key_padding_mask
        valid_full = jnp.concatenate((valid_feat, jnp.ones((b, n), dtype=bool)), axis=1)
        sim = jnp.where(valid_full[:, None, None, :], sim, NEG_INF)
        attn = jax.nn.softmax(sim, axis=-1)
        out = jnp.einsum('bhqk,bkhd->bqhd', attn, v).reshape(b, n, HEADS * DIM_HEAD)
        return out @ Wout

    def _L3_ffn_ref(x, ln1_g, ln1_b, ln2_g, ln2_b, wq, bq, wk, bk, wv, bv, wo, bo, gate_w, gate_b, w1, b1, w2, b2):
        import jax, jax.numpy as jnp
        import numpy as np
        B, S, H, NH, E, F = (4, 128, 128, 16, 8, 512)
        D = H // NH
        EPS = 1e-05

        def _layernorm(x, g, b):
            mu = jnp.mean(x, axis=-1, keepdims=True)
            var = jnp.var(x, axis=-1, keepdims=True)
            return (x - mu) * jax.lax.rsqrt(var + EPS) * g + b
        b, s, h = x.shape
        hn = _layernorm(x, ln1_g, ln1_b)
        q = (hn @ wq + bq).reshape(b, s, NH, D).transpose(0, 2, 1, 3)
        k = (hn @ wk + bk).reshape(b, s, NH, D).transpose(0, 2, 1, 3)
        v = (hn @ wv + bv).reshape(b, s, NH, D).transpose(0, 2, 1, 3)
        scores = jnp.einsum('bhqd,bhkd->bhqk', q, k) / jnp.sqrt(jnp.float32(D))
        attn = jax.nn.softmax(scores, axis=-1)
        o = jnp.einsum('bhqk,bhkd->bhqd', attn, v)
        o = o.transpose(0, 2, 1, 3).reshape(b, s, h)
        x = x + (o @ wo + bo)
        hn2 = _layernorm(x, ln2_g, ln2_b).reshape(-1, h)
        logits = hn2 @ gate_w + gate_b
        idx = jnp.argmax(logits, axis=-1)
        mid = jax.nn.relu(jnp.einsum('th,ehf->etf', hn2, w1) + b1[:, None, :])
        y = jnp.einsum('etf,efh->eth', mid, w2) + b2[:, None, :]
        moe = y[idx, jnp.arange(hn2.shape[0])]
        return x + moe.reshape(b, s, h)
    x = x + _L0_xattn_ref(_layernorm(x, axis=-1), ctx_1024, mask_BxSxS2_ik0, L0_xattn_W, L0_xattn_b)
    x = x + _L0_ffn_ref(_layernorm(x, axis=-1), L0_ffn_Wg, L0_ffn_bg, L0_ffn_W1, L0_ffn_b1, L0_ffn_W2, L0_ffn_b2)
    x = x + _L1_xattn_ref(_layernorm(x, axis=-1), ctx_1024, ctx_1024, L1_xattn_Wq, L1_xattn_bq, L1_xattn_Wk, L1_xattn_bk, L1_xattn_Wv, L1_xattn_bv, L1_xattn_Wo)
    x = x + _L1_ffn_ref(_layernorm(x, axis=-1), L1_ffn_Wr, L1_ffn_br, L1_ffn_W1, L1_ffn_b1, L1_ffn_W2, L1_ffn_b2, L1_ffn_ln_w, L1_ffn_ln_b)
    x = x + _L2_xattn_ref(_layernorm(x, axis=-1), ctx_1024, ctx_1024, L2_xattn_Wq, L2_xattn_bq, L2_xattn_Wk, L2_xattn_bk, L2_xattn_Wv, L2_xattn_bv)
    x = x + _L2_ffn_ref(_layernorm(x, axis=-1), L2_ffn_U1, L2_ffn_V1, L2_ffn_b1, L2_ffn_U2, L2_ffn_V2, L2_ffn_b2)
    x = x + _L3_xattn_ref(ctx_1024, _layernorm(x, axis=-1), mask_BxS2_bk0, L3_xattn_kv_gate, L3_xattn_gamma_media, L3_xattn_beta_media, L3_xattn_gamma_lat, L3_xattn_beta_lat, L3_xattn_Wq, L3_xattn_Wk, L3_xattn_Wv, L3_xattn_Wout)
    x = x + _L3_ffn_ref(_layernorm(x, axis=-1), L3_ffn_ln1_g, L3_ffn_ln1_b, L3_ffn_ln2_g, L3_ffn_ln2_b, L3_ffn_wq, L3_ffn_bq, L3_ffn_wk, L3_ffn_bk, L3_ffn_wv, L3_ffn_bv, L3_ffn_wo, L3_ffn_bo, L3_ffn_gate_w, L3_ffn_gate_b, L3_ffn_w1, L3_ffn_b1, L3_ffn_w2, L3_ffn_b2)
    return x

_drawn_inputs = setup_inputs


def setup_inputs(seed=0):
    import zlib

    import numpy as np

    out = dict(_drawn_inputs(seed))
    spreads = {'L0_ffn_bg': (0.0, 0.1),
     'L0_ffn_b1': (0.0, 0.8),
     'L0_ffn_b2': (0.0, 0.1),
     'L1_ffn_br': (0.0, 0.522),
     'L1_ffn_b1': (0.0, 0.8),
     'L1_ffn_b2': (0.0, 0.333),
     'L1_ffn_ln_w': (1.0, 0.2),
     'L1_ffn_ln_b': (0.0, 0.1),
     'L2_ffn_b1': (0.0, 0.8),
     'L2_ffn_b2': (0.0, 0.315),
     'L3_xattn_gamma_media': (1.0, 0.6),
     'L3_xattn_beta_media': (0.0, 0.8),
     'L3_xattn_gamma_lat': (1.0, 0.6),
     'L3_xattn_beta_lat': (0.0, 0.8),
     'L3_ffn_ln1_g': (1.0, 0.6),
     'L3_ffn_ln1_b': (0.0, 0.8),
     'L3_ffn_ln2_g': (1.0, 0.6),
     'L3_ffn_ln2_b': (0.0, 0.8),
     'L3_ffn_bq': (0.0, 0.8),
     'L3_ffn_bk': (0.0, 2.0),
     'L3_ffn_bv': (0.0, 0.8),
     'L3_ffn_bo': (0.0, 0.284),
     'L3_ffn_gate_b': (0.0, 0.337),
     'L3_ffn_b1': (0.0, 0.8),
     'L3_ffn_b2': (0.0, 0.336)}
    factors = {'L0_ffn_W1': 3.885,
     'L0_ffn_W2': 3.586,
     'L1_xattn_bk': 64.0,
     'L1_ffn_W1': 4.558,
     'L1_ffn_W2': 4.155,
     'L2_xattn_bq': 8.0,
     'L2_xattn_bk': 64.0,
     'L2_ffn_U1': 8.0,
     'L2_ffn_V1': 8.0,
     'L2_ffn_U2': 8.0,
     'L2_ffn_V2': 8.0,
     'L3_xattn_Wq': 8.0,
     'L3_xattn_Wk': 8.0,
     'L3_ffn_wq': 8.0,
     'L3_ffn_wk': 8.0,
     'L3_ffn_wv': 4.982,
     'L3_ffn_wo': 4.223,
     'L3_ffn_w1': 3.778,
     'L3_ffn_w2': 2.92}
    for name, (base, spread) in spreads.items():
        noise = np.random.default_rng([zlib.crc32(name.encode()), seed]).standard_normal(out[name].shape)
        drawn = base * np.exp(spread * noise) if base else spread * noise
        out[name] = jnp.asarray(drawn.astype(out[name].dtype))
    for name, factor in factors.items():
        out[name] = (out[name] * factor).astype(out[name].dtype)
    return out
```

```python
from contextlib import ExitStack

import numpy as np

import concourse.bass as bass
from concourse import mybir

F32 = mybir.dt.float32
I32 = mybir.dt.int32
U8 = mybir.dt.uint8
ALU = mybir.AluOpType
ACT = mybir.ActivationFunctionType
AX = mybir.AxisListType

P = 128
T = 16
J = 4
G = T // J
GT = J * P
KC = 77
E = 8
F = 512
FC = F // P
H1, D1 = 16, 64
C1 = H1 * D1 // P
H3, D3 = 8, 64
C3 = H3 * D3 // P
K3 = KC + P
HS, DS = 16, 8
RANK = 32
EPS = 1e-5
EPS_POST = 1e-12
NEG0 = -1000000.0
NEG3 = -1e30
STOP = 9

W_SMALL = [("ident", P), ("headmask", HS), ("l0_w", P), ("l0_b", 1), ("f0_wg", E), ("f0_bg", 1), ("f0_b1", E),
           ("f0_b2", P), ("l1_bq", C1), ("l1_bk", C1), ("f1_wr", E), ("f1_br", 1), ("f1_b1", E * FC), ("f1_b2", P),
           ("l2_wq", P), ("l2_bq", 1), ("l2_wk", P), ("l2_bk", 1), ("l2_wv", P),
           ("f2_u1", RANK), ("f2_v1", F), ("f2_b1", FC), ("f2_u2", FC * RANK), ("f2_v2", P),
           ("l3_gm", 1), ("l3_bm", 1), ("l3_gl", 1), ("l3_bl", 1), ("l3_gate", 1),
           ("s_g1", 1), ("s_b1", 1), ("s_g2", 1), ("s_b2", 1), ("s_wq", P), ("s_bq", 1), ("s_wk", P), ("s_bk", 1),
           ("s_wv", P), ("s_wo", P), ("f3_wg", E), ("f3_bg", 1), ("f3_b1", E * FC), ("f3_b2", P)]
W_ROWS = [("l1_bv", H1 * D1), ("f1_lnw", P), ("f1_lnb", P), ("l2_bv", P), ("f2_b2", P), ("s_bv", P), ("s_bo", P)]


def columns(table):
    at, out = 0, {}
    for name, width in table:
        out[name] = (at, at + width)
        at += width
    return out, at


SMALL, N_SMALL = columns(W_SMALL)
ROWS, N_ROWS = columns(W_ROWS)


class Chain:

    def __init__(self, eng, sem):
        self.eng, self.sem, self.n = eng, sem, 0

    def link(self, ins):
        ins.then_inc(self.sem, 1)
        self.n += 1

    def after(self):
        self.eng.wait_ge(self.sem, self.n)

    def restart(self):
        self.after()
        self.eng.sem_clear(self.sem)
        self.n = 0


def build(nc, x_d, ctx_d, ctxT_d, mask0_d, mask3_d, small_d, rows_d, f0_d, l1_d, f1_d, l3_d, f3_d, out_d):
    with ExitStack() as ctx:
        def sb(name, shape, dt=F32):
            return ctx.enter_context(nc.sbuf_tensor(name, shape, dt))

        def sem(name):
            return ctx.enter_context(nc.semaphore(name))

        x_res = sb("x_res", [P, T * P])
        xl_res = sb("xl_res", [P, T * P])
        xnT = sb("xnT", [P, T * P])
        ctx_sb = sb("ctx_sb", [KC, T * (P + 1)])
        ctxT_sb = sb("ctxT_sb", [P, T * KC])
        mask0_sb = sb("mask0_sb", [P, T * KC], I32)
        mask3_sb = sb("mask3_sb", [P, T * KC], U8)
        small = sb("small", [P, N_SMALL])
        rows = sb("rows", [P, N_ROWS])
        f0_sb = sb("f0_sb", [P, 2 * E * P])
        w16_sb = sb("w16_sb", [P, 4 * 1024])
        w32_sb = sb("w32_sb", [P, 2 * E * F])
        cw = sb("cw", [P, T * E])

        big = sb("big", [P, 2 * FC * GT])
        kT = sb("kT", [P, C3 * J * K3])
        kv = sb("kv", [P, J * H1 * (D1 + 1)])
        gT_sb = kv[0:E, 0:T * P]
        pT = sb("pT", [P, H1 * P])
        ebuf = sb("ebuf", [P, 2 * 1024])
        ob = sb("ob", [P, 1024])
        oT = sb("oT", [P, 1024])
        ctxTg = sb("ctxTg", [P, J * KC])
        xnG = sb("xnG", [P, GT])
        tmp = sb("tmp", [P, GT])
        acc = sb("acc", [P, GT])
        madd = sb("madd", [P, J * KC])
        mask3_f = sb("mask3_f", [P, T * KC])
        cwg = sb("cwg", [P, J * E])
        cwT = sb("cwT", [E, GT])
        st = sb("st", [P, J, 6])
        mv = sb("mv", [P, J, 2])
        ve = sb("ve", [P, J])
        rstd = sb("rstd", [P, J])
        mhalf = sb("mhalf", [P, J])
        euler = sb("euler", [P, T])
        mx = sb("mx", [P, 32])
        rs = sb("rs", [P, 32])
        rt = [sb(f"rt{i}", [P, T * E]) for i in range(4)]
        rank8 = sb("rank8", [P, T * E])
        rv = [sb(f"rv{i}", [P, T]) for i in range(5)]

        psum = ctx.enter_context(nc.psum_tensor("psum", [P, 8 * 512], F32))
        bank = [psum[:, i * 512:(i + 1) * 512] for i in range(8)]

        def W(name, rows_=P):
            a, b = SMALL[name]
            return small[0:rows_, a:b]

        def R(name):
            a, b = ROWS[name]
            return rows[:, a:b]

        ident = W("ident")
        unmask_f = mask0_sb[:, :].bitcast(F32)

        in_small, in_ctx, in_rows, in_masks = sem("in_small"), sem("in_ctx"), sem("in_rows"), sem("in_masks")
        in_x = [sem(f"in_x{q}") for q in range(G)]
        in_mask3 = sem("in_mask3")
        in_f0, in_w16, in_w32 = sem("in_f0"), sem("in_w16"), sem("in_w32")
        out_done = sem("out_done")
        consts_ready = sem("consts_ready")
        dve_order = sem("dve_order")
        pool_order = sem("pool_order")
        var_ready, rstd_ready = sem("var_ready"), sem("rstd_ready")
        xn_ready, xnt_psum, xnT_ready = sem("xn_ready"), sem("xnt_psum"), sem("xnT_ready")
        x_final = sem("x_final")
        madd_ready = sem("madd_ready")

        LN_PER = [1, 1, 1, 1, 2, 1, 2, 2, 1]
        LN_BASE = [G * sum(LN_PER[:i]) for i in range(len(LN_PER) + 1)]

        def toks(t, n=P):
            return bass.ds(t * n, n)

        def grp(t):
            return t.rearrange("p (j d) -> p j d", j=J)

        block = ctx.enter_context(nc.Block())

        def ln_dve(dve, ch, src, dst, eps, n, used=None):
            for j in range(J):
                ch.link(dve.bn_stats(st[:, j, :], src[:, j, :]))
            ch.after()
            for j in range(J):
                ch.link(dve.bn_aggr(mv[:, j, :], st[:, j, :]))
            ch.after()
            dve.tensor_scalar(ve[:, :], mv[:, :, 1], eps, None, ALU.add).then_inc(var_ready, 1)
            dve.wait_ge(rstd_ready, n + 1)
            if used is not None:
                dve.wait_ge(xnt_psum, used)
            for j in range(J):
                ch.link(dve.tensor_scalar(dst[:, j, :], src[:, j, :], mv[:, j, 0:1], rstd[:, j:j + 1],
                                          ALU.subtract, ALU.mult))
            ch.after()

        def ln_pool(pool, n):
            pool.wait_ge(var_ready, n + 1)
            pool.tensor_tensor(rstd[:, :], ve[:, :], mhalf[:, :], ALU.pow).then_inc(rstd_ready, 1)

        def tail_dve(dve, ch, p, g):
            x_g = grp(x_res[:, toks(g, GT)])
            xl_g = grp(xl_res[:, toks(g, GT)])
            n = LN_BASE[p] + g * LN_PER[p]
            used = G * p + g + 1
            if p in (6, 7):
                ln_dve(dve, ch, x_g, xl_g, EPS, n)
                ln_dve(dve, ch, xl_g, grp(xnG[:, :]), EPS, n + 1, used)
            elif p == 8:
                ln_dve(dve, ch, xl_g, grp(xnG[:, :]), EPS, n, used)
            else:
                ln_dve(dve, ch, x_g, grp(xnG[:, :]), EPS, n + LN_PER[p] - 1, used)
            if p == 3:
                ch.link(dve.tensor_copy(xl_res[:, toks(g, GT)], xnG[:, :]))
                ch.after()
            dve.sem_inc(xn_ready, 1)

        def tail_pool(pool, p, g):
            for i in range(LN_PER[p]):
                ln_pool(pool, LN_BASE[p] + g * LN_PER[p] + i)

        def tail_pe(pe, p, g):
            pe.wait_ge(xn_ready, G * p + g + 1)
            pe.wait_ge(xnT_ready, G * p + g + 1)
            for j in range(J):
                ins = pe.transpose(bank[7][:, j * P:(j + 1) * P], xnG[:, j * P:(j + 1) * P], ident)
            ins.then_inc(xnt_psum, 1)

        def tail_act(act, p, g):
            act.wait_ge(xnt_psum, G * p + g + 2)
            gain = {6: "l3_gl", 7: "s_g1", 8: "s_g2"}.get(p)
            if gain:
                shift = {6: "l3_bl", 7: "s_b1", 8: "s_b2"}[p]
                ins = act.activation(xnT[:, toks(g, GT)], bank[7][:, :], ACT.Identity, bias=W(shift), scale=W(gain))
            else:
                ins = act.copy(xnT[:, toks(g, GT)], bank[7][:, :])
            ins.then_inc(xnT_ready, 1)

        def enter_phase(eng, p):
            eng.wait_ge(xnT_ready, G * (p + 1) + 1)

        class OneHead:
            def __init__(s, tag, p):
                s.tag, s.p = tag, p
                s.q_psum, s.q_ready = sem(f"{tag}_q_psum"), sem(f"{tag}_q_ready")
                s.k_psum, s.k_ready = sem(f"{tag}_k_psum"), sem(f"{tag}_k_ready")
                s.v_psum, s.v_ready = sem(f"{tag}_v_psum"), sem(f"{tag}_v_ready")
                s.s_psum, s.shift_ready, s.exp_ready = sem(f"{tag}_s_psum"), sem(f"{tag}_shift_ready"), sem(f"{tag}_exp_ready")
                s.pt_psum, s.pt_ready, s.o_psum = sem(f"{tag}_pt_psum"), sem(f"{tag}_pt_ready"), sem(f"{tag}_o_psum")
                s.ct_ready = sem(f"{tag}_ct_ready")

        A0 = OneHead("l0", 0)
        A2 = OneHead("l2", 4)
        qT1 = big[:, 0:GT]

        def vrow(t, n):
            return ctx_sb[:, bass.ds(t * (P + 1), n)]

        def onehead_pe(pe, A, g):
            first = A is A0
            rhs = xnT[:, toks(g, GT)]
            pe.matmul(bank[0][:, :], W("l0_w") if first else W("l2_wq"), rhs, start=True, stop=True).then_inc(A.q_psum, 1)
            if not first:
                pe.wait_ge(A.ct_ready, g + 1)
                pe.matmul(bank[2][:, 0:J * KC], W("l2_wk"), ctxTg[:, :], start=True, stop=True).then_inc(A.k_psum, 1)
                for j in range(J):
                    ins = pe.matmul(bank[3][0:KC, j * P:(j + 1) * P], ctxTg[:, j * KC:(j + 1) * KC], W("l2_wv"),
                                    start=True, stop=True)
                ins.then_inc(A.v_psum, 1)
                pe.wait_ge(A.k_ready, g + 1)
            pe.wait_ge(A.q_ready, g + 1)
            for j in range(J):
                keys = ctxT_sb[:, bass.ds((g * J + j) * KC, KC)] if first else kT[:, j * KC:(j + 1) * KC]
                ins = pe.matmul(bank[1][:, j * KC:(j + 1) * KC], qT1[:, j * P:(j + 1) * P], keys, start=True, stop=True)
            ins.then_inc(A.s_psum, 1)
            pe.wait_ge(A.exp_ready, g + 1)
            for j in range(J):
                ins = pe.transpose(bank[4][0:KC, j * P:(j + 1) * P], ebuf[:, j * KC:(j + 1) * KC], ident)
            ins.then_inc(A.pt_psum, 1)
            pe.wait_ge(A.pt_ready, g + 1)
            if not first:
                pe.wait_ge(A.v_ready, g + 1)
            for j in range(J):
                vals = ctx_sb[0:KC, bass.ds((g * J + j) * (P + 1), P + 1)] if first else kv[0:KC, j * (P + 1):(j + 1) * (P + 1)]
                ins = pe.matmul(bank[5 + j // 2][:, (j % 2) * 256:(j % 2) * 256 + P + 1], pT[0:KC, j * P:(j + 1) * P], vals,
                                start=True, stop=True)
            ins.then_inc(A.o_psum, 1)

        def onehead_act(act, A, g):
            first = A is A0
            act.wait_ge(A.q_psum, g + 1)
            act.activation(qT1, bank[0][:, :], ACT.Identity, bias=W("l0_b") if first else W("l2_bq")).then_inc(A.q_ready, 1)
            if not first:
                act.wait_ge(A.k_psum, g + 1)
                act.activation(kT[:, 0:J * KC], bank[2][:, 0:J * KC], ACT.Identity, bias=W("l2_bk")).then_inc(A.k_ready, 1)
            act.wait_ge(A.shift_ready, g + 1)
            act.activation(ebuf[:, 0:J * KC], madd[:, :] if first else tmp[:, 0:J * KC], ACT.Exp,
                           scale=1.0 if first else float(P) ** -0.5).then_inc(A.exp_ready, 1)
            act.wait_ge(A.pt_psum, g + 1)
            act.copy(pT[0:KC, 0:GT], bank[4][0:KC, :]).then_inc(A.pt_ready, 1)

        def onehead_dve(dve, ch, A, g):
            first = A is A0
            if not first:
                dve.wait_ge(A.v_psum, g + 1)
                vals = kv[0:KC, 0:J * (P + 1)].rearrange("p (j d) -> p j d", j=J)
                ch.link(dve.memset(vals[:, :, P:P + 1], 1.0))
                dve.tensor_tensor(vals[:, :, 0:P], grp(bank[3][0:KC, :]),
                                  R("l2_bv")[0:KC, None, :].to_broadcast((KC, J, P)), ALU.add).then_inc(A.v_ready, 1)
            dve.wait_ge(A.s_psum, g + 1)
            s_ps = bank[1][:, 0:J * KC]
            if first:
                ch.link(dve.scalar_tensor_tensor(out=tmp[:, 0:J * KC], in0=unmask_f[:, bass.ds(g * J * KC, J * KC)],
                                                 scalar=NEG0, in1=s_ps,
                                                 op0=ALU.mult, op1=ALU.add))
                ch.after()
                src = tmp[:, 0:J * KC]
            else:
                src = s_ps
            src = src.rearrange("p (j k) -> p j k", j=J)
            ch.link(dve.tensor_reduce(mx[:, 0:J], src, AX.X, ALU.max))
            ch.after()
            dst = (madd[:, :] if first else tmp[:, 0:J * KC]).rearrange("p (j k) -> p j k", j=J)
            dve.tensor_tensor(dst, src, mx[:, 0:J, None].to_broadcast((P, J, KC)), ALU.subtract).then_inc(A.shift_ready, 1)
            dve.wait_ge(A.o_psum, g + 1)
            for i in range(2):
                o = bank[5 + i][:, :].rearrange("p (j d) -> p j d", j=2)
                ch.link(dve.reciprocal(rs[:, 2 * i:2 * i + 2, None], o[:, :, P:P + 1]))
            ch.after()
            for j in range(J):
                xt = x_res[:, toks(g * J + j)]
                ch.link(dve.scalar_tensor_tensor(out=xt, in0=bank[5 + j // 2][:, (j % 2) * 256:(j % 2) * 256 + P],
                                                 scalar=rs[:, j:j + 1], in1=xt, op0=ALU.mult, op1=ALU.add))
            ch.after()

        def onehead_pool(pool, A, g):
            if A is A2:
                pool.wait_ge(ct_used, g + 1)
                pool.tensor_copy(ctxTg[:, :], ctxT_sb[:, bass.ds(g * J * KC, J * KC)]).then_inc(A.ct_ready, 1)

        gl_psum, gl_ready, g_psum, cw_ready = sem("gl_psum"), sem("gl_ready"), sem("g_psum"), sem("cw_ready")
        gap_ready, gexp_ready = sem("gap_ready"), sem("gexp_ready")
        h_psum, hT_ready, y_psum, y_used = sem("h_psum"), sem("hT_ready"), sem("y_psum"), sem("y_used")
        cwg_ready, cwt_psum, cwT_ready = sem("cwg_ready"), sem("cwt_psum"), sem("cwT_ready")
        H_BANKS, Y_BANKS = 4, 2

        class Experts:
            def __init__(s, k, p, fc, func, w, wg, bg, b1, b2, top):
                s.k, s.p, s.fc, s.func, s.w, s.wg, s.bg, s.b1, s.b2, s.top = k, p, fc, func, w, wg, bg, b1, b2, top

            def w1(s, e, c):
                return s.w[:, (e * s.fc + c) * P:(e * s.fc + c + 1) * P]

            def w2(s, e, c):
                at = E * s.fc + e * s.fc + c
                return s.w[:, at * P:(at + 1) * P]

        M0 = Experts(0, 1, 1, ACT.Gelu, f0_sb, "f0_wg", "f0_bg", "f0_b1", "f0_b2", 1)
        M1 = Experts(1, 3, FC, ACT.Gelu, w32_sb, "f1_wr", "f1_br", "f1_b1", "f1_b2", 2)
        M3 = Experts(2, 8, FC, ACT.Relu, w32_sb, "f3_wg", "f3_bg", "f3_b1", "f3_b2", 1)
        HT_BASE = {0: H_BANKS, 1: H_BANKS + G * E, 2: H_BANKS + G * E + G * E * FC}
        YJ = E + 1

        def route_pe(pe, M):
            for g in range(G):
                pe.matmul(bank[4 + g][0:E, :], W(M.wg), xnT[:, g * GT:(g + 1) * GT], start=True, stop=True).then_inc(gl_psum, 1)
            pe.wait_ge(gl_ready, G * (M.k + 1))
            for t in range(T):
                ins = pe.transpose(bank[4][:, t * E:(t + 1) * E], gT_sb[:, t * P:(t + 1) * P], ident[0:E, 0:E])
            ins.then_inc(g_psum, 1)

        def route_act(act, M):
            for g in range(G):
                act.wait_ge(gl_psum, G * M.k + g + 1)
                act.activation(gT_sb[:, g * GT:(g + 1) * GT], bank[4 + g][0:E, :], ACT.Identity,
                               bias=W(M.bg, E)).then_inc(gl_ready, 1)

        def route_dve(dve, ch, M):
            def te(t):
                return t[:, :].rearrange("p (t e) -> p t e", t=T)

            def wide(v):
                return v[:, :, None].to_broadcast((P, T, E))

            def first_of_greatest(src, hot, top, scratch, at):
                ch.link(dve.tensor_reduce(top[:, :], te(src), AX.X, ALU.max))
                ch.after()
                ch.link(dve.tensor_tensor(te(scratch), te(src), wide(top), ALU.is_ge))
                ch.after()
                ch.link(dve.tensor_tensor(te(scratch), te(scratch), te(rank8), ALU.mult))
                ch.after()
                ch.link(dve.tensor_reduce(at[:, :], te(scratch), AX.X, ALU.max))
                ch.after()
                ch.link(dve.tensor_tensor(te(hot), te(scratch), wide(at), ALU.is_equal))
                ch.after()

            dve.wait_ge(g_psum, M.k + 1)
            ch.link(dve.tensor_copy(rt[0][:, :], bank[4][:, 0:T * E]))
            ch.after()
            if M.top == 1:
                first_of_greatest(rt[0], cw, rv[0], rt[1], rv[1])
            else:
                first_of_greatest(rt[0], rt[2], rv[0], rt[1], rv[1])
                ch.link(dve.scalar_tensor_tensor(out=rt[0][:, :], in0=rt[2][:, :], scalar=NEG3, in1=rt[0][:, :],
                                                 op0=ALU.mult, op1=ALU.add))
                ch.after()
                first_of_greatest(rt[0], rt[3], rv[2], rt[1], rv[1])
                dve.tensor_tensor(rv[2][:, :], rv[2][:, :], rv[0][:, :], ALU.subtract).then_inc(gap_ready, 1)
                dve.wait_ge(gexp_ready, 1)
                ch.link(dve.tensor_scalar(rv[0][:, :], rv[3][:, :], 1.0, None, ALU.add))
                ch.after()
                ch.link(dve.reciprocal(rv[0][:, :], rv[0][:, :]))
                ch.after()
                ch.link(dve.tensor_tensor(rv[1][:, :], rv[3][:, :], rv[0][:, :], ALU.mult))
                ch.after()
                ch.link(dve.tensor_tensor(te(rt[2]), te(rt[2]), wide(rv[0]), ALU.mult))
                ch.link(dve.tensor_tensor(te(rt[3]), te(rt[3]), wide(rv[1]), ALU.mult))
                ch.after()
                ch.link(dve.tensor_tensor(cw[:, :], rt[2][:, :], rt[3][:, :], ALU.add))
                ch.after()
            ch.restart()

        def route_pool(pool):
            pool.wait_ge(gap_ready, 1)
            pool.tensor_tensor(rv[3][:, :], euler[:, :], rv[2][:, :], ALU.pow).then_inc(gexp_ready, 1)

        def experts_pe(pe, M, g):
            rhs = xnT[:, toks(g, GT)]
            n = E * M.fc

            def hidden(e):
                for c in range(M.fc):
                    k = e * M.fc + c
                    pe.wait_ge(hT_ready, HT_BASE[M.k] + g * n + k - H_BANKS + 1)
                    pe.matmul(bank[k % H_BANKS][:, :], M.w1(e, c), rhs, start=True, stop=True).then_inc(h_psum, 1)

            def y_job(i):
                pe.wait_ge(y_used, Y_BANKS + G * YJ * M.k + g * YJ + (i - 1 if i else 0))
                return bank[5 + i % 2]

            def biases():
                y = y_job(0)
                pe.wait_ge(cwT_ready, G * M.k + g + 1)
                for j in range(J):
                    ins = pe.matmul(y[:, j * P:(j + 1) * P], cwT[:, j * P:(j + 1) * P], W(M.b2, E), start=True, stop=True)
                ins.then_inc(y_psum, 1)

            def out(e):
                y = y_job(e + 1)
                pe.wait_ge(hT_ready, HT_BASE[M.k] + g * n + (e + 1) * M.fc)
                for j in range(J):
                    for c in range(M.fc):
                        at = ((e % 2) * M.fc + c) * GT + j * P
                        ins = pe.matmul(y[:, j * P:(j + 1) * P], big[:, at:at + P], M.w2(e, c),
                                        start=(c == 0), stop=(c == M.fc - 1))
                ins.then_inc(y_psum, 1)

            hidden(0)
            pe.wait_ge(cwg_ready, G * M.k + g + 1)
            if M is not M3:
                pe.wait_ge(xnT_ready, G * (M.p + 1) + g + 1)
            for j in range(J):
                ins = pe.transpose(bank[7][0:E, j * P:(j + 1) * P], cwg[:, j * E:(j + 1) * E], ident)
            ins.then_inc(cwt_psum, 1)
            hidden(1)
            biases()
            for e in range(E):
                out(e)
                if e + 2 < E:
                    hidden(e + 2)

        def experts_act(act, M, g):
            n = E * M.fc

            def hidden(e):
                for c in range(M.fc):
                    k = e * M.fc + c
                    act.wait_ge(h_psum, HT_BASE[M.k] - H_BANKS + g * n + k + 1)
                    if c == 0:
                        act.wait_ge(y_psum, Y_BANKS + G * YJ * M.k + g * YJ + (e if e >= 2 else e - 1))
                    at = ((e % 2) * M.fc + c) * GT
                    act.activation(big[:, at:at + GT], bank[k % H_BANKS][:, :], M.func,
                                   bias=W(M.b1)[:, k:k + 1]).then_inc(hT_ready, 1)

            hidden(0)
            act.wait_ge(cwt_psum, G * M.k + g + 2)
            act.copy(cwT[:, :], bank[7][0:E, :]).then_inc(cwT_ready, 1)
            for e in range(1, E):
                hidden(e)

        def experts_dve(dve, ch, M, g):
            dve.wait_ge(cwt_psum, G * M.k + g + 1)
            dve.tensor_copy(cwg[:, :], cw[:, bass.ds(g * J * E, J * E)]).then_inc(cwg_ready, 1)
            w = cwg[:, :].rearrange("p (j e) -> p j e", j=J)
            for i in range(YJ):
                dve.wait_ge(y_psum, Y_BANKS + G * YJ * M.k + g * YJ + i + 1)
                y = bank[5 + i % 2]
                if i == 0:
                    dve.tensor_copy(acc[:, :], y[:, :]).then_inc(y_used, 1)
                    dve.wait_ge(y_used, Y_BANKS + G * YJ * M.k + g * YJ + i + 1)
                    continue
                dve.tensor_tensor(grp(tmp[:, :]), grp(y[:, :]), w[:, :, i - 1:i].to_broadcast((P, J, P)),
                                  ALU.mult).then_inc(y_used, 1)
                dve.wait_ge(y_used, Y_BANKS + G * YJ * M.k + g * YJ + i + 1)
                ch.link(dve.tensor_tensor(acc[:, :], acc[:, :], tmp[:, :], ALU.add))
                ch.after()
            x_g = x_res[:, toks(g, GT)]
            xl_g = xl_res[:, toks(g, GT)]
            if M is M1:
                ch.link(dve.tensor_tensor(acc[:, :], acc[:, :], xl_g, ALU.add))
                ch.after()
                ln_dve(dve, ch, grp(acc[:, :]), grp(tmp[:, :]), EPS_POST, LN_BASE[4] + g * LN_PER[4])
                for name, op in (("f1_lnw", ALU.mult), ("f1_lnb", ALU.add)):
                    ch.link(dve.tensor_tensor(grp(tmp[:, :]), grp(tmp[:, :]), R(name)[:, None, :].to_broadcast((P, J, P)), op))
                    ch.after()
                ch.link(dve.tensor_tensor(x_g, x_g, tmp[:, :], ALU.add))
                ch.after()
            else:
                ch.link(dve.tensor_tensor(x_g, x_g, acc[:, :], ALU.add))
                ch.after()
                if M is M3:
                    ch.link(dve.tensor_tensor(x_g, x_g, xl_g, ALU.add))
                    ch.after()

        s_psum, shift_ready, exp_ready = sem("s_psum"), sem("shift_ready"), sem("exp_ready")
        pt_psum, pt_ready = sem("pt_psum"), sem("pt_ready")
        o_psum, o_ready, ot_psum, ot_ready = sem("o_psum"), sem("o_ready"), sem("ot_psum"), sem("ot_ready")
        w_psum, w_used = sem("w_psum"), sem("w_used")
        NJ = 2 * J

        class Heads:
            def __init__(s, k, p, nh, d, nk, scale, wo):
                s.k, s.p, s.nh, s.d, s.nk, s.scale, s.wo = k, p, nh, d, nk, scale, wo
                s.jh = nh // 2
                s.sl = s.jh // 2
                s.ob = 2 if s.jh * (d + 1) > 512 else 1
                s.oc = nh * d // P

        HL1 = Heads(0, 2, H1, D1, KC, D1 ** -0.5, lambda c: w16_sb[:, 3072 + c * P:3072 + (c + 1) * P])
        HL3 = Heads(1, 6, H3, D3, K3, D3 ** -0.5, lambda c: w16_sb[:, 1536 + c * P:1536 + (c + 1) * P])
        HLS = Heads(2, 7, HS, DS, P, DS ** -0.5, lambda c: W("s_wo"))

        def banked(A, ap, width):
            return ap.rearrange("p (b r) -> p b r", b=2)[:, :, 0:A.sl * width].rearrange("p b (s k) -> p b s k", s=A.sl)

        def e_slot(A, i):
            return ebuf[:, (i % 2) * 1024:(i % 2) * 1024 + A.jh * A.nk]

        def e_head(A, i, u):
            at = (i % 2) * 1024 + ((u % 2) * A.sl + u // 2) * A.nk
            return ebuf[:, at:at + A.nk]

        def o_cols(A, u):
            w = A.d + 1
            if A.ob == 2:
                return bank[6 + u % 2][:, (u // 2) * w:(u // 2) * w + w]
            at = ((u % 2) * A.sl + u // 2) * w
            return bank[6][:, at:at + w]

        def heads_pe(pe, A, g):
            nb = NJ * (G * A.k + g)
            tb = J * (G * A.k + g)

            def scores(i):
                j, hh = i // 2, i % 2
                if A is HLS:
                    pe.wait_ge(kx_ready, J * g + j + 1)
                for u in range(A.jh):
                    h = hh * A.jh + u
                    out = bank[2 * (i % 2) + u % 2][:, (u // 2) * A.nk:(u // 2 + 1) * A.nk]
                    if A is HLS:
                        lhsT = kT[:, GT + j * P:GT + (j + 1) * P]
                        rhs = big[:, (j % 2) * 2048 + h * P:(j % 2) * 2048 + (h + 1) * P]
                    else:
                        a = (h % 2) * 64
                        c = h // 2
                        kc = c * J * A.nk + j * A.nk
                        lhsT = big[a:a + 64, c * GT + j * P:c * GT + (j + 1) * P]
                        rhs = kT[a:a + 64, kc:kc + A.nk]
                    ins = pe.matmul(out, lhsT, rhs, start=True, stop=True)
                ins.then_inc(s_psum, 1)

            def turn(i):
                pe.wait_ge(exp_ready, nb + i + 1)
                if i >= 4 and i % 2 == 0:
                    pe.wait_ge(w_used, tb + (i - 4) // 2 + 1)
                if i:
                    pe.wait_ge(pt_ready, nb + i)
                for u in range(A.jh):
                    e = e_head(A, i, u)
                    if A is HL3:
                        pe.transpose(bank[4][0:KC, u * P:(u + 1) * P], e[:, 0:KC], ident)
                        ins = pe.transpose(bank[5][:, u * P:(u + 1) * P], e[:, KC:K3], ident)
                    else:
                        ins = pe.transpose(bank[4 + u // 4][0:A.nk, (u % 4) * P:(u % 4 + 1) * P], e, ident)
                ins.then_inc(pt_psum, 1)

            def weigh(i):
                j, hh = i // 2, i % 2
                pe.wait_ge(pt_ready, nb + i + 1)
                if i:
                    pe.wait_ge(o_ready, nb + i)
                for u in range(A.jh):
                    h = hh * A.jh + u
                    w = A.d + 1
                    slot = (i % 2) * 1024
                    if A is HL3:
                        at = (j * H3 + h) * w
                        pe.matmul(o_cols(A, u), pT[0:KC, slot + u * P:slot + (u + 1) * P], kv[0:KC, at:at + w],
                                  start=True, stop=False)
                        at += J * H3 * w
                        ins = pe.matmul(o_cols(A, u), pT[:, slot + 512 + u * P:slot + 512 + (u + 1) * P], kv[:, at:at + w],
                                        start=False, stop=True)
                    else:
                        at = (j * A.nh + h) * w
                        ins = pe.matmul(o_cols(A, u), pT[0:A.nk, slot + u * P:slot + (u + 1) * P], kv[0:A.nk, at:at + w],
                                        start=True, stop=True)
                ins.then_inc(o_psum, 1)

            def turn_out(t):
                pe.wait_ge(o_ready, nb + 2 * t + 2)
                for c in range(A.oc):
                    ins = pe.transpose(bank[6 + c // 4][:, (c % 4) * P:(c % 4 + 1) * P], ob[:, c * P:(c + 1) * P], ident)
                ins.then_inc(ot_psum, 1)

            def project(t):
                pe.wait_ge(ot_ready, tb + t + 1)
                pe.wait_ge(pt_ready, nb + min(2 * t + 4, NJ))
                for c in range(A.oc):
                    ins = pe.matmul(bank[4][:, 0:P], oT[:, c * P:(c + 1) * P], A.wo(c), start=(c == 0), stop=(c == A.oc - 1))
                ins.then_inc(w_psum, 1)

            scores(0)
            scores(1)
            for i in range(NJ + 2):
                if i < NJ:
                    turn(i)
                if 1 <= i <= NJ:
                    if i >= 3 and i % 2 == 1:
                        pe.wait_ge(ot_ready, tb + (i - 3) // 2 + 1)
                    weigh(i - 1)
                if i + 2 < NJ:
                    scores(i + 2)
                if i % 2 == 0 and i >= 2:
                    turn_out((i - 2) // 2)
                if i % 2 == 1 and i >= 3:
                    project((i - 3) // 2)
            pe.wait_ge(w_used, tb + J)

        def heads_act(act, A, g):
            nb = NJ * (G * A.k + g)
            tb = J * (G * A.k + g)

            def exps(i):
                act.wait_ge(shift_ready, nb + i + 1)
                act.activation(e_slot(A, i), e_slot(A, i), ACT.Exp, scale=A.scale).then_inc(exp_ready, 1)

            def turned(i):
                slot = (i % 2) * 1024
                act.wait_ge(pt_psum, nb + i + 1)
                if i >= 2:
                    act.wait_ge(o_psum, nb + i - 1)
                if A is HL3:
                    act.copy(pT[0:KC, slot:slot + 512], bank[4][0:KC, :])
                    act.copy(pT[:, slot + 512:slot + 1024], bank[5][:, :]).then_inc(pt_ready, 1)
                else:
                    act.copy(pT[0:A.nk, slot:slot + A.jh * P], psum[0:A.nk, 4 * 512:4 * 512 + A.jh * P]).then_inc(pt_ready, 1)

            exps(0)
            exps(1)
            for i in range(NJ + 1):
                if i < NJ:
                    turned(i)
                if i + 2 < NJ:
                    exps(i + 2)
                if i % 2 == 0 and i >= 2:
                    t = (i - 2) // 2
                    act.wait_ge(ot_psum, tb + t + 1)
                    if t:
                        act.wait_ge(w_psum, tb + t)
                    act.copy(oT[:, 0:A.oc * P], psum[:, 6 * 512:6 * 512 + A.oc * P]).then_inc(ot_ready, 1)

        def heads_dve(dve, ch, A, g):
            nb = NJ * (G * A.k + g)
            tb = J * (G * A.k + g)

            def shift(i):
                dve.wait_ge(s_psum, nb + i + 1)
                if i >= 2:
                    dve.wait_ge(pt_psum, nb + i - 1)
                b = 2 * (i % 2) * 512
                s = banked(A, psum[:, b:b + 1024], A.nk)
                if A is HL3:
                    m = mask3_f[:, bass.ds((g * J + i // 2) * KC, KC)]
                    ch.link(dve.tensor_tensor(s[:, :, :, 0:KC], s[:, :, :, 0:KC],
                                              m[:, None, None, :].to_broadcast((P, 2, A.sl, KC)), ALU.add))
                    ch.after()
                top = mx[:, (i % 2) * 8:(i % 2) * 8 + A.jh].rearrange("p (b s) -> p b s", b=2)
                ch.link(dve.tensor_reduce(top, s, AX.X, ALU.max))
                ch.after()
                dst = e_slot(A, i).rearrange("p (b s k) -> p b s k", b=2, s=A.sl)
                dve.tensor_tensor(dst, s, top[:, :, :, None].to_broadcast((P, 2, A.sl, A.nk)),
                                  ALU.subtract).then_inc(shift_ready, 1)

            def norm(i):
                dve.wait_ge(o_psum, nb + i + 1)
                if i % 2 == 0 and i >= 2:
                    dve.wait_ge(ot_psum, tb + i // 2)
                w = A.d + 1
                if A.ob == 2:
                    o = psum[:, 6 * 512:8 * 512].rearrange("p (b r) -> p b r", b=2)[:, :, 0:A.sl * w]
                    o = o.rearrange("p b (s d) -> p b s d", s=A.sl)
                else:
                    o = bank[6][:, 0:A.jh * w].rearrange("p (b s d) -> p b s d", b=2, s=A.sl)
                r = rs[:, 0:A.jh].rearrange("p (b s) -> p b s", b=2)
                ch.link(dve.reciprocal(r[:, :, :, None], o[:, :, :, A.d:w]))
                ch.after()
                at = (i % 2) * A.jh * A.d
                dst = ob[:, at:at + A.jh * A.d].rearrange("p (s b d) -> p b s d", b=2, s=A.sl)
                dve.tensor_tensor(dst, o[:, :, :, 0:A.d], r[:, :, :, None].to_broadcast((P, 2, A.sl, A.d)),
                                  ALU.mult).then_inc(o_ready, 1)

            def add_x(t):
                dve.wait_ge(w_psum, tb + t + 1)
                res = xl_res if A is HLS else x_res
                x_t = res[:, toks(g * J + t)]
                dve.tensor_tensor(x_t, bank[4][:, 0:P], x_t, ALU.add).then_inc(w_used, 1)

            shift(0)
            shift(1)
            for i in range(NJ + 2):
                if 1 <= i <= NJ:
                    norm(i - 1)
                if i + 2 < NJ:
                    shift(i + 2)
                if i % 2 == 1 and i >= 3:
                    add_x((i - 3) // 2)
            dve.wait_ge(w_used, tb + J)
            if A is HLS:
                xl_g = grp(xl_res[:, toks(g, GT)])
                ch.link(dve.tensor_tensor(xl_g, xl_g, R("s_bo")[:, None, :].to_broadcast((P, J, P)), ALU.add))
                ch.after()

        l1_q_psum, l1_q_ready, l1_k_psum, l1_k_ready = sem("l1_q_psum"), sem("l1_q_ready"), sem("l1_k_psum"), sem("l1_k_ready")
        l1_v_psum, l1_v_ready, l1_ct_ready = sem("l1_v_psum"), sem("l1_v_ready"), sem("l1_ct_ready")
        ct_used = sem("ct_used")
        NV = 2 * J

        def l1_front_pe(pe, g):
            pe.wait_ge(l1_ct_ready, g + 1)
            for c in range(C1):
                pe.wait_ge(l1_q_ready, g * C1 + c + 1)
                pe.matmul(bank[c % 2][:, :], w16_sb[:, c * P:(c + 1) * P], xnT[:, toks(g, GT)],
                          start=True, stop=True).then_inc(l1_q_psum, 1)
                pe.wait_ge(l1_k_ready, g * C1 + c + 1)
                pe.matmul(bank[2 + c % 2][:, 0:J * KC], w16_sb[:, 1024 + c * P:1024 + (c + 1) * P], ctxTg[:, :],
                          start=True, stop=True).then_inc(l1_k_psum, 1)
                i = c
                pe.wait_ge(l1_v_ready, g * NV + i + 1)
                pe.matmul(bank[4 + i % 2][0:KC, :], ctxTg[:, (i // 2) * KC:(i // 2 + 1) * KC],
                          w16_sb[:, 2048 + (i % 2) * 512:2048 + (i % 2 + 1) * 512],
                          start=True, stop=True).then_inc(l1_v_psum, 1)
            pe.wait_ge(l1_q_ready, (g + 1) * C1 + 2)
            pe.wait_ge(l1_k_ready, (g + 1) * C1 + 2)
            pe.wait_ge(l1_v_ready, (g + 1) * NV + 2)

        def l1_front_act(act, g):
            for c in range(C1):
                act.wait_ge(l1_q_psum, g * C1 + c + 1)
                act.activation(big[:, c * GT:(c + 1) * GT], bank[c % 2][:, :], ACT.Identity,
                               bias=W("l1_bq")[:, c:c + 1]).then_inc(l1_q_ready, 1)
                act.wait_ge(l1_k_psum, g * C1 + c + 1)
                act.activation(kT[:, c * J * KC:(c + 1) * J * KC], bank[2 + c % 2][:, 0:J * KC], ACT.Identity,
                               bias=W("l1_bk")[:, c:c + 1]).then_inc(l1_k_ready, 1)

        def l1_front_dve(dve, ch, g):
            v = kv[0:KC, :].rearrange("p (j h d) -> p j h d", j=J, h=H1)
            dve.wait_ge(l1_v_psum, g * NV + 1)
            for j in range(J):
                ch.link(dve.memset(v[:, j, :, D1:D1 + 1], 1.0))
            ch.after()
            for i in range(NV):
                dve.wait_ge(l1_v_psum, g * NV + i + 1)
                a = (i % 2) * 8
                dve.tensor_tensor(v[:, i // 2, a:a + 8, 0:D1], bank[4 + i % 2][0:KC, :].rearrange("p (h d) -> p h d", h=8),
                                  R("l1_bv")[0:KC, a * D1:(a + 8) * D1].rearrange("p (h d) -> p h d", h=8),
                                  ALU.add).then_inc(l1_v_ready, 1)

        def l1_front_pool(pool, g):
            pool.wait_ge(ctl1_used, g + 1)
            pool.tensor_copy(ctxTg[:, :], ctxT_sb[:, bass.ds(g * J * KC, J * KC)]).then_inc(l1_ct_ready, 1)

        ctl1_used = sem("ctl1_used")

        lr_p_psum, lr_p_ready, lr_h_psum, lr_h_ready = sem("lr_p_psum"), sem("lr_p_ready"), sem("lr_h_psum"), sem("lr_h_ready")
        lr_q_psum, lr_q_ready, lr_o_psum = sem("lr_q_psum"), sem("lr_q_ready"), sem("lr_o_psum")

        def lowrank_pe(pe, g):
            pe.matmul(bank[0][0:RANK, :], W("f2_u1"), xnT[:, toks(g, GT)], start=True, stop=True).then_inc(lr_p_psum, 1)
            pe.wait_ge(lr_p_ready, g + 1)
            for c in range(FC):
                pe.matmul(bank[1 + c][:, :], W("f2_v1", RANK)[:, c * P:(c + 1) * P], kT[0:RANK, 0:GT],
                          start=True, stop=True).then_inc(lr_h_psum, 1)
            for c in range(FC):
                pe.wait_ge(lr_h_ready, g * FC + c + 1)
                ins = pe.matmul(bank[5][0:RANK, :], W("f2_u2")[:, c * RANK:(c + 1) * RANK], big[:, c * GT:(c + 1) * GT],
                                start=(c == 0), stop=(c == FC - 1))
            ins.then_inc(lr_q_psum, 1)
            pe.wait_ge(lr_q_ready, g + 1)
            for j in range(J):
                ins = pe.matmul(bank[6][:, j * P:(j + 1) * P], kT[0:RANK, GT + j * P:GT + (j + 1) * P], W("f2_v2", RANK),
                                start=True, stop=True)
            ins.then_inc(lr_o_psum, 1)

        def lowrank_act(act, g):
            act.wait_ge(lr_p_psum, g + 1)
            act.copy(kT[0:RANK, 0:GT], bank[0][0:RANK, :]).then_inc(lr_p_ready, 1)
            for c in range(FC):
                act.wait_ge(lr_h_psum, g * FC + c + 1)
                act.activation(big[:, c * GT:(c + 1) * GT], bank[1 + c][:, :], ACT.Gelu_apprx_tanh,
                               bias=W("f2_b1")[:, c:c + 1]).then_inc(lr_h_ready, 1)
            act.wait_ge(lr_q_psum, g + 1)
            act.copy(kT[0:RANK, GT:2 * GT], bank[5][0:RANK, :]).then_inc(lr_q_ready, 1)

        def lowrank_dve(dve, ch, g):
            x_g = x_res[:, toks(g, GT)]
            dve.wait_ge(lr_o_psum, g + 1)
            ch.link(dve.tensor_tensor(x_g, bank[6][:, :], x_g, ALU.add))
            ch.after()
            ch.link(dve.tensor_tensor(grp(x_g), grp(x_g), R("f2_b2")[:, None, :].to_broadcast((P, J, P)), ALU.add))
            ch.after()

        l3_lg_ready, l3_cn_ready, l3_cn_psum, l3_ct_ready = sem("l3_lg_ready"), sem("l3_cn_ready"), sem("l3_cn_psum"), sem("l3_ct_ready")
        l3_q_psum, l3_q_ready, l3_k_psum, l3_k_ready = sem("l3_q_psum"), sem("l3_q_ready"), sem("l3_k_psum"), sem("l3_k_ready")
        l3_v_psum, l3_v_ready = sem("l3_v_psum"), sem("l3_v_ready")
        latG = big[:, 4 * GT:5 * GT]
        NK3 = 2 * C3

        def l3_front_dve(dve, ch, g):
            dve.wait_ge(xnT_ready, G * 7 + 1)
            dve.wait_ge(s_psum, NJ * (G + g))
            dve.wait_ge(xnt_psum, G * 7 + 1 + g)
            dve.tensor_scalar(latG, xnT[:, toks(g, GT)], W("l3_gate"), None, ALU.mult).then_inc(l3_lg_ready, 1)
            src = ctx_sb[:, bass.ds(g * J * (P + 1), J * (P + 1))].rearrange("p (j d) -> p j d", j=J)
            for j in range(J):
                ch.link(dve.bn_stats(st[0:KC, j, :], src[:, j, 0:P]))
            ch.after()
            for j in range(J):
                ch.link(dve.bn_aggr(mv[0:KC, j, :], st[0:KC, j, :]))
            ch.after()
            dve.tensor_scalar(ve[:, :], mv[:, :, 1], EPS, None, ALU.add).then_inc(cvar_ready, 1)
            dve.wait_ge(crstd_ready, g + 1)
            for j in range(J):
                ch.link(dve.tensor_scalar(tmp[0:KC, j * P:(j + 1) * P], src[:, j, 0:P], mv[0:KC, j, 0:1],
                                          rstd[0:KC, j:j + 1], ALU.subtract, ALU.mult))
            ch.after()
            dve.sem_inc(l3_cn_ready, 1)
            va = kv[0:KC, 0:J * H3 * (D3 + 1)].rearrange("p (j h d) -> p j h d", j=J, h=H3)
            vb = kv[:, J * H3 * (D3 + 1):2 * J * H3 * (D3 + 1)].rearrange("p (j h d) -> p j h d", j=J, h=H3)
            for i in range(2 * J):
                dve.wait_ge(l3_v_psum, g * 2 * J + i + 1)
                if i == 0:
                    for j in range(J):
                        ch.link(dve.memset(va[:, j, :, D3:D3 + 1], 1.0))
                        ch.link(dve.memset(vb[:, j, :, D3:D3 + 1], 1.0))
                    ch.after()
                if i % 2 == 0:
                    ins = dve.tensor_copy(va[:, i // 2, :, 0:D3], bank[4][0:KC, :].rearrange("p (h d) -> p h d", h=H3))
                else:
                    ins = dve.tensor_copy(vb[:, i // 2, :, 0:D3], bank[5][:, :].rearrange("p (h d) -> p h d", h=H3))
                ins.then_inc(l3_v_ready, 1)

        cvar_ready, crstd_ready = sem("cvar_ready"), sem("crstd_ready")

        def l3_front_pool(pool, g):
            pool.wait_ge(cvar_ready, g + 1)
            pool.tensor_tensor(rstd[:, :], ve[:, :], mhalf[:, :], ALU.pow).then_inc(crstd_ready, 1)

        def l3_front_pe(pe, g):
            for c in range(C3):
                pe.matmul(bank[c][:, :], w16_sb[:, c * P:(c + 1) * P], xnT[:, toks(g, GT)],
                          start=True, stop=True).then_inc(l3_q_psum, 1)
            pe.wait_ge(l3_cn_ready, g + 1)
            for j in range(J):
                ins = pe.transpose(bank[4][:, j * KC:(j + 1) * KC], tmp[0:KC, j * P:(j + 1) * P], ident[0:KC, 0:KC])
            ins.then_inc(l3_cn_psum, 1)
            pe.wait_ge(l3_lg_ready, g + 1)
            pe.wait_ge(l3_ct_ready, g + 1)
            pe.wait_ge(l3_q_ready, (g + 1) * C3)
            for c in range(C3):
                w = w16_sb[:, 512 + c * P:512 + (c + 1) * P]
                for half, (keys, n) in enumerate(((ctxTg[:, :], J * KC), (latG, GT))):
                    if c >= 2:
                        pe.wait_ge(l3_k_ready, g * NK3 + 2 * c + half - 3)
                    pe.matmul(bank[(2 * c + half) % 4][:, 0:n], w, keys, start=True, stop=True).then_inc(l3_k_psum, 1)
            for i in range(2 * J):
                if i >= 2:
                    pe.wait_ge(l3_v_ready, g * 2 * J + i - 1)
                j = i // 2
                wv = w16_sb[:, 1024:1536]
                if i % 2 == 0:
                    ins = pe.matmul(bank[4][0:KC, :], ctxTg[:, j * KC:(j + 1) * KC], wv, start=True, stop=True)
                else:
                    ins = pe.matmul(bank[5][:, :], latG[:, j * P:(j + 1) * P], wv, start=True, stop=True)
                ins.then_inc(l3_v_psum, 1)
            pe.wait_ge(l3_k_ready, (g + 1) * NK3)
            pe.wait_ge(l3_v_ready, (g + 1) * 2 * J)

        def l3_front_act(act, g):
            for c in range(C3):
                act.wait_ge(l3_q_psum, g * C3 + c + 1)
                act.copy(big[:, c * GT:(c + 1) * GT], bank[c][:, :]).then_inc(l3_q_ready, 1)
            act.wait_ge(l3_cn_psum, g + 1)
            act.activation(ctxTg[:, :], bank[4][:, 0:J * KC], ACT.Identity, bias=W("l3_bm"), scale=W("l3_gm")).then_inc(l3_ct_ready, 1)
            for c in range(C3):
                dst = kT[:, c * J * K3:(c + 1) * J * K3].rearrange("p (j k) -> p j k", j=J)
                for half, (a, n) in enumerate(((0, KC), (KC, P))):
                    act.wait_ge(l3_k_psum, g * NK3 + 2 * c + half + 1)
                    act.copy(dst[:, :, a:a + n],
                             bank[(2 * c + half) % 4][:, 0:J * n].rearrange("p (j k) -> p j k", j=J)).then_inc(l3_k_ready, 1)

        ls_h_ready, ls_q_psum, ls_q_ready, ls_k_psum, ls_k_ready = [sem("ls_" + n) for n in
                                                                    ("h_ready", "q_psum", "q_ready", "k_psum", "k_ready")]
        ls_v_psum, ls_v_ready, kx_ready, ls_h_used = sem("ls_v_psum"), sem("ls_v_ready"), sem("kx_ready"), sem("ls_h_used")

        def ls_front_pool(pool, g):
            pool.wait_ge(xnT_ready, G * 8 + 1)
            pool.wait_ge(s_psum, NJ * (2 * G + g))
            pool.tensor_copy(kT[:, 2 * GT:3 * GT], xnT[:, toks(g, GT)]).then_inc(ls_h_ready, 1)
            pool.wait_ge(ls_k_ready, g + 1)
            for j in range(J):
                if j >= 2:
                    pool.wait_ge(s_psum, NJ * (2 * G + g) + 2 * (j - 1))
                dst = big[:, (j % 2) * 2048:(j % 2 + 1) * 2048].rearrange("p (h k) -> p h k", h=HS)
                pool.tensor_tensor(dst, kT[:, None, j * P:(j + 1) * P].to_broadcast((P, HS, P)),
                                   W("headmask")[:, :, None].to_broadcast((P, HS, P)), ALU.mult).then_inc(kx_ready, 1)

        def ls_front_pe(pe, g):
            rhs = xnT[:, toks(g, GT)]
            pe.matmul(bank[0][:, :], W("s_wk"), rhs, start=True, stop=True).then_inc(ls_k_psum, 1)
            pe.matmul(bank[1][:, :], W("s_wq"), rhs, start=True, stop=True).then_inc(ls_q_psum, 1)
            pe.wait_ge(ls_h_ready, g + 1)
            for j in range(J):
                ins = pe.matmul(bank[2][:, j * P:(j + 1) * P], kT[:, 2 * GT + j * P:2 * GT + (j + 1) * P], W("s_wv"),
                                start=True, stop=True)
            ins.then_inc(ls_v_psum, 1)
            pe.wait_ge(ls_q_ready, g + 1)
            pe.wait_ge(ls_v_ready, g + 1)

        def ls_front_act(act, g):
            act.wait_ge(ls_k_psum, g + 1)
            act.activation(kT[:, 0:GT], bank[0][:, :], ACT.Identity, bias=W("s_bk")).then_inc(ls_k_ready, 1)
            act.wait_ge(ls_q_psum, g + 1)
            act.activation(kT[:, GT:2 * GT], bank[1][:, :], ACT.Identity, bias=W("s_bq")).then_inc(ls_q_ready, 1)

        def ls_front_dve(dve, ch, g):
            dve.wait_ge(ls_v_psum, g + 1)
            w = DS + 1
            v = kv[:, 0:J * HS * w].rearrange("p (j h d) -> p (j h) d", j=J, h=HS)
            ch.link(dve.memset(v[:, :, DS:w], 1.0))
            ch.after()
            for j in range(J):
                vj = kv[:, j * HS * w:(j + 1) * HS * w].rearrange("p (h d) -> p h d", h=HS)
                ch.link(dve.tensor_tensor(vj[:, :, 0:DS], bank[2][:, j * P:(j + 1) * P].rearrange("p (h d) -> p h d", h=HS),
                                          R("s_bv").rearrange("p (h d) -> p h d", h=HS), ALU.add))
            ch.after()
            dve.sem_inc(ls_v_ready, 1)

        def groups(eng, body):
            with eng.Fori(0, G) as g:
                body(g)

        def by_tile(t):
            return t.rearrange("p (t d) -> p t d", t=T)

        @block.sync
        def _(sp):
            sp.dma_start(small[:, :], small_d).then_inc(in_small, 16)
            for q in range(G):
                sp.dma_start(by_tile(x_res[:, :])[:, q * J:(q + 1) * J, :],
                             x_d[q * J:(q + 1) * J].rearrange("t p d -> p t d")).then_inc(in_x[q], 16)
            sp.dma_start(ctxT_sb[:, :], ctxT_d).then_inc(in_ctx, 16)
            sp.dma_start(by_tile(mask0_sb[:, :]), mask0_d.rearrange("t p k -> p t k")).then_inc(in_masks, 16)
            sp.dma_start(by_tile(ctx_sb[:, :])[:, :, 0:P], ctx_d.rearrange("t k d -> k t d")).then_inc(in_ctx, 16)
            sp.dma_start(rows[:, :], rows_d.to_broadcast((P, N_ROWS))).then_inc(in_rows, 16)
            sp.dma_start(mask3_sb[:, :], mask3_d.to_broadcast((P, T * KC))).then_inc(in_mask3, 16)
            sp.dma_start(f0_sb[:, :], f0_d).then_inc(in_f0, 16)
            sp.dma_start(w16_sb[:, :], l1_d).then_inc(in_w16, 16)
            sp.dma_start(w32_sb[:, :], f1_d).then_inc(in_w32, 16)
            if STOP > 6:
                sp.wait_ge(w_psum, J * G)
                sp.dma_start(w16_sb[:, 0:2048], l3_d).then_inc(in_w16, 16)
            if STOP > 8:
                sp.wait_ge(y_psum, Y_BANKS + 2 * G * YJ)
                sp.dma_start(w32_sb[:, :], f3_d).then_inc(in_w32, 16)
            sp.wait_ge(x_final, G)
            sp.dma_start(out_d.rearrange("t p d -> p t d"), by_tile(x_res[:, :])).then_inc(out_done, 16)
            sp.wait_ge(out_done, 16)

        def run(eng, n, body):
            if STOP >= n:
                groups(eng, body)

        @block.gpsimd
        def _(pool):
            pool.memset(mhalf[:, :], -0.5)
            pool.memset(euler[:, :], float(np.exp(1.0)))
            for e in range(E):
                pool.memset(rank8[:, :].rearrange("p (t e) -> p t e", t=T)[:, :, e:e + 1], float(E - e))
            pool.memset(by_tile(ctx_sb[:, :])[:, :, P:P + 1], 1.0).then_inc(consts_ready, 1)
            pool.memset(mv[:, :, :], 1.0).then_inc(consts_ready, 1)
            pool.wait_ge(consts_ready, 2)
            pool.wait_ge(in_masks, 16)
            pool.tensor_scalar(unmask_f, mask0_sb[:, :], -1.0, 1.0, ALU.mult, ALU.add).then_inc(madd_ready, 1)
            pool.wait_ge(in_mask3, 16)
            pool.tensor_scalar(mask3_f[:, :], mask3_sb[:, :], NEG3, None, ALU.mult).then_inc(madd_ready, 1)
            groups(pool, lambda g: tail_pool(pool, 0, g))

            def copy_l1(g):
                l1_front_pool(pool, g)
                tail_pool(pool, 3, g)

            def copy_l2(g):
                onehead_pool(pool, A2, g)
                tail_pool(pool, 5, g)

            def l3(g):
                l3_front_pool(pool, g)
                tail_pool(pool, 7, g)

            def ls(g):
                ls_front_pool(pool, g)
                tail_pool(pool, 8, g)

            run(pool, 1, lambda g: tail_pool(pool, 1, g))
            run(pool, 2, lambda g: tail_pool(pool, 2, g))
            run(pool, 3, copy_l1)
            if STOP >= 4:
                route_pool(pool)
            run(pool, 4, lambda g: tail_pool(pool, 4, g))
            run(pool, 5, copy_l2)
            run(pool, 6, lambda g: tail_pool(pool, 6, g))
            run(pool, 7, l3)
            run(pool, 8, ls)

        @block.vector
        def _(dve):
            ch = Chain(dve, dve_order)
            dve.sem_inc(y_used, Y_BANKS)
            dve.sem_inc(l1_v_ready, 2)
            dve.wait_ge(consts_ready, 2)
            for g in range(G):
                dve.wait_ge(in_x[g], 16)
                tail_dve(dve, ch, 0, g)
            ch.restart()
            dve.wait_ge(madd_ready, 2)
            dve.wait_ge(in_rows, 16)

            def phase(p, body):
                def whole(g):
                    body(g)
                    if p < 9:
                        tail_dve(dve, ch, p, g)
                    ch.restart()
                run(dve, p, whole)

            def last(g):
                experts_dve(dve, ch, M3, g)
                dve.sem_inc(x_final, 1)

            phase(1, lambda g: onehead_dve(dve, ch, A0, g))
            if STOP >= 2:
                route_dve(dve, ch, M0)
            phase(2, lambda g: experts_dve(dve, ch, M0, g))
            phase(3, lambda g: (l1_front_dve(dve, ch, g), heads_dve(dve, ch, HL1, g)))
            if STOP >= 4:
                route_dve(dve, ch, M1)
            phase(4, lambda g: experts_dve(dve, ch, M1, g))
            phase(5, lambda g: onehead_dve(dve, ch, A2, g))
            phase(6, lambda g: lowrank_dve(dve, ch, g))
            phase(7, lambda g: (l3_front_dve(dve, ch, g), heads_dve(dve, ch, HL3, g)))
            phase(8, lambda g: (ls_front_dve(dve, ch, g), heads_dve(dve, ch, HLS, g)))
            if STOP >= 9:
                route_dve(dve, ch, M3)
            phase(9, last)
            if STOP < 9:
                dve.sem_inc(x_final, G)

        @block.scalar
        def _(act):
            act.sem_inc(xnT_ready, 1)
            act.sem_inc(hT_ready, H_BANKS)
            act.sem_inc(l1_q_ready, 2)
            act.sem_inc(l1_k_ready, 2)
            act.wait_ge(in_small, 16)
            groups(act, lambda g: tail_act(act, 0, g))

            def phase(p, body):
                def whole(g):
                    body(g)
                    if p < 9:
                        tail_act(act, p, g)
                run(act, p, whole)

            phase(1, lambda g: onehead_act(act, A0, g))
            if STOP >= 2:
                route_act(act, M0)
            phase(2, lambda g: experts_act(act, M0, g))
            phase(3, lambda g: (l1_front_act(act, g), heads_act(act, HL1, g)))
            if STOP >= 4:
                route_act(act, M1)
            phase(4, lambda g: experts_act(act, M1, g))
            phase(5, lambda g: onehead_act(act, A2, g))
            phase(6, lambda g: lowrank_act(act, g))
            phase(7, lambda g: (l3_front_act(act, g), heads_act(act, HL3, g)))
            phase(8, lambda g: (ls_front_act(act, g), heads_act(act, HLS, g)))
            if STOP >= 9:
                route_act(act, M3)
            phase(9, lambda g: experts_act(act, M3, g))

        @block.tensor
        def _(pe):
            pe.sem_inc(xnt_psum, 1)
            pe.sem_inc(cwt_psum, 1)
            pe.sem_inc(y_psum, Y_BANKS)
            pe.sem_inc(ct_used, 1)
            pe.sem_inc(ctl1_used, 1)
            pe.wait_ge(in_small, 16)
            groups(pe, lambda g: tail_pe(pe, 0, g))

            def phase(p, body):
                def whole(g):
                    body(g)
                    if p < 9:
                        tail_pe(pe, p, g)
                run(pe, p, whole)

            pe.wait_ge(in_ctx, 32)
            pe.wait_ge(consts_ready, 2)
            enter_phase(pe, 0)
            phase(1, lambda g: onehead_pe(pe, A0, g))
            if STOP >= 2:
                enter_phase(pe, 1)
                route_pe(pe, M0)
                pe.wait_ge(in_f0, 16)
            phase(2, lambda g: experts_pe(pe, M0, g))
            if STOP >= 3:
                enter_phase(pe, 2)
                pe.wait_ge(in_w16, 16)

            def l1(g):
                l1_front_pe(pe, g)
                pe.sem_inc(ctl1_used, 1)
                heads_pe(pe, HL1, g)

            phase(3, l1)
            if STOP >= 4:
                enter_phase(pe, 3)
                route_pe(pe, M1)
                pe.wait_ge(in_w32, 16)
            phase(4, lambda g: experts_pe(pe, M1, g))
            if STOP >= 5:
                enter_phase(pe, 4)

            def l2(g):
                onehead_pe(pe, A2, g)
                pe.sem_inc(ct_used, 1)

            phase(5, l2)
            if STOP >= 6:
                enter_phase(pe, 5)
            phase(6, lambda g: lowrank_pe(pe, g))
            if STOP >= 7:
                enter_phase(pe, 6)
                pe.wait_ge(in_w16, 32)
            phase(7, lambda g: (l3_front_pe(pe, g), heads_pe(pe, HL3, g)))
            if STOP >= 8:
                enter_phase(pe, 7)
            phase(8, lambda g: (ls_front_pe(pe, g), heads_pe(pe, HLS, g)))
            if STOP >= 9:
                enter_phase(pe, 8)
                route_pe(pe, M3)
                pe.wait_ge(in_w32, 32)
            phase(9, lambda g: experts_pe(pe, M3, g))


def kernel(**inputs):
    import concourse.bacc as bacc
    from concourse.bass_utils import run_bass_kernel_spmd

    a = {k: np.asarray(v) for k, v in inputs.items()}

    def pad(m):
        m = m.reshape(m.shape[0], -1)
        return np.concatenate([m, np.zeros((P - m.shape[0], m.shape[1]), m.dtype)], 0)

    def chunks(v):
        return v.reshape(-1, P).T

    head = np.zeros((P, HS), np.float32)
    head[np.arange(P), np.arange(P) // DS] = 1.0
    pieces = {
        "ident": np.eye(P, dtype=np.float32), "headmask": head,
        "l0_w": a["L0_xattn_W"].T, "l0_b": a["L0_xattn_b"][:, None],
        "f0_wg": a["L0_ffn_Wg"], "f0_bg": a["L0_ffn_bg"][:, None], "f0_b1": a["L0_ffn_b1"].T, "f0_b2": a["L0_ffn_b2"],
        "l1_bq": chunks(a["L1_xattn_bq"]), "l1_bk": chunks(a["L1_xattn_bk"]),
        "f1_wr": a["L1_ffn_Wr"].T, "f1_br": a["L1_ffn_br"][:, None], "f1_b1": chunks(a["L1_ffn_b1"].reshape(-1)),
        "f1_b2": a["L1_ffn_b2"],
        "l2_wq": a["L2_xattn_Wq"].T, "l2_bq": a["L2_xattn_bq"][:, None], "l2_wk": a["L2_xattn_Wk"].T,
        "l2_bk": a["L2_xattn_bk"][:, None], "l2_wv": a["L2_xattn_Wv"].T,
        "f2_u1": a["L2_ffn_U1"], "f2_v1": a["L2_ffn_V1"], "f2_b1": chunks(a["L2_ffn_b1"]),
        "f2_u2": a["L2_ffn_U2"].reshape(FC, P, RANK).transpose(1, 0, 2), "f2_v2": a["L2_ffn_V2"],
        "l3_gm": a["L3_xattn_gamma_media"][:, None], "l3_bm": a["L3_xattn_beta_media"][:, None],
        "l3_gl": a["L3_xattn_gamma_lat"][:, None], "l3_bl": a["L3_xattn_beta_lat"][:, None],
        "l3_gate": np.repeat(a["L3_xattn_kv_gate"].reshape(1, 1), P, 0),
        "s_g1": a["L3_ffn_ln1_g"][:, None], "s_b1": a["L3_ffn_ln1_b"][:, None],
        "s_g2": a["L3_ffn_ln2_g"][:, None], "s_b2": a["L3_ffn_ln2_b"][:, None],
        "s_wq": a["L3_ffn_wq"], "s_bq": a["L3_ffn_bq"][:, None], "s_wk": a["L3_ffn_wk"], "s_bk": a["L3_ffn_bk"][:, None],
        "s_wv": a["L3_ffn_wv"], "s_wo": a["L3_ffn_wo"],
        "f3_wg": a["L3_ffn_gate_w"], "f3_bg": a["L3_ffn_gate_b"][:, None], "f3_b1": chunks(a["L3_ffn_b1"].reshape(-1)),
        "f3_b2": a["L3_ffn_b2"],
    }
    small = np.concatenate([pad(pieces[name]) for name, _ in W_SMALL], 1)
    rows = np.concatenate([a[k].reshape(1, -1) for k in ("L1_xattn_bv", "L1_ffn_ln_w", "L1_ffn_ln_b", "L2_xattn_bv",
                                                         "L2_ffn_b2", "L3_ffn_bv", "L3_ffn_bo")], 1)

    def inner(m):
        return m.transpose(1, 0, 2).reshape(P, -1)

    f0 = np.concatenate([inner(a["L0_ffn_W1"]), inner(a["L0_ffn_W2"])], 1)
    l1 = np.concatenate([a["L1_xattn_Wq"].T, a["L1_xattn_Wk"].T, a["L1_xattn_Wv"].T,
                         inner(a["L1_xattn_Wo"].T.reshape(C1, P, P))], 1)
    f1 = np.concatenate([inner(a["L1_ffn_W1"].transpose(0, 2, 1)),
                         inner(a["L1_ffn_W2"].transpose(0, 2, 1).reshape(E * FC, P, P))], 1)
    l3 = np.concatenate([a["L3_xattn_Wq"], a["L3_xattn_Wk"], a["L3_xattn_Wv"],
                         inner(a["L3_xattn_Wout"].reshape(C3, P, P))], 1)
    f3 = np.concatenate([inner(a["L3_ffn_w1"]), inner(a["L3_ffn_w2"].reshape(E * FC, P, P))], 1)
    arrays = {
        "x": a["x"], "ctx": a["ctx_1024"], "ctxT": a["ctx_1024"].transpose(2, 0, 1).reshape(P, T * KC),
        "mask0": a["mask_BxSxS2_ik0"], "mask3": a["mask_BxS2_bk0"].reshape(1, T * KC),
        "small": small, "rows": rows, "f0": f0, "l1": l1, "f1": f1, "l3": l3, "f3": f3,
    }
    nc = bacc.Bacc("TRN2", target_bir_lowering=False, num_devices=1)
    feeds, args = {}, []
    for name, arr in arrays.items():
        arr = np.ascontiguousarray(arr)
        feeds[f"in_{name}"] = arr
        args.append(nc.dram_tensor(f"in_{name}", arr.shape, mybir.dt.from_np(arr.dtype), kind="ExternalInput").ap())
    args.append(nc.dram_tensor("out_x", (T, P, P), F32, kind="ExternalOutput").ap())
    build(nc, *args)
    r = run_bass_kernel_spmd(nc, [feeds], core_ids=[0])
    return r.results[0]["out_x"]
```

```python
from contextlib import ExitStack

import numpy as np

import concourse.bass as bass
from concourse import mybir

F32 = mybir.dt.float32
I32 = mybir.dt.int32
U8 = mybir.dt.uint8
ALU = mybir.AluOpType
ACT = mybir.ActivationFunctionType
AX = mybir.AxisListType

P = 128
T = 16
J = 4
G = T // J
GT = J * P
KC = 77
E = 8
F = 512
FC = F // P
H1, D1 = 16, 64
C1 = H1 * D1 // P
H3, D3 = 8, 64
C3 = H3 * D3 // P
K3 = KC + P
HS, DS = 16, 8
RANK = 32
EPS = 1e-5
EPS_POST = 1e-12
NEG0 = -1000000.0
NEG3 = -1e30
LSW = P + HS

W_SMALL = [("ident", P), ("headmask", HS), ("l0_w", P), ("l0_b", 1), ("f0_wg", E), ("f0_bg", 1), ("f0_b1", E),
           ("f0_b2", P), ("l1_bq", C1), ("l1_bk", C1), ("l1_bv", C1), ("f1_wr", E), ("f1_br", 1), ("f1_b1", E * FC), ("f1_b2", P),
           ("l2_wq", P), ("l2_bq", 1), ("l2_wk", P), ("l2_bk", 1), ("l2_wv", P),
           ("f2_u1", RANK), ("f2_v1", F), ("f2_b1", FC), ("f2_u2", FC * RANK), ("f2_v2", P),
           ("l3_gm", 1), ("l3_bm", 1), ("l3_gl", 1), ("l3_bl", 1), ("l3_gate", 1),
           ("s_g1", 1), ("s_b1", 1), ("s_g2", 1), ("s_b2", 1), ("s_wq", P), ("s_bq", 1), ("s_wk", P), ("s_bk", 1),
           ("s_wv", P), ("s_wo", P), ("f3_wg", E), ("f3_bg", 1), ("f3_b1", E * FC), ("f3_b2", P)]
W_ROWS = [("f1_lnw", P), ("f1_lnb", P), ("l2_bv", P), ("f2_b2", P), ("s_bv", P), ("s_bo", P)]


def columns(table):
    at, out = 0, {}
    for name, width in table:
        out[name] = (at, at + width)
        at += width
    return out, at


SMALL, N_SMALL = columns(W_SMALL)
ROWS, N_ROWS = columns(W_ROWS)


class Chain:

    def __init__(self, eng, sem):
        self.eng, self.sem, self.n = eng, sem, 0

    def link(self, ins):
        ins.then_inc(self.sem, 1)
        self.n += 1

    def after(self):
        self.eng.wait_ge(self.sem, self.n)

    def restart(self):
        self.after()
        self.eng.sem_clear(self.sem)
        self.n = 0


def build(nc, x_d, ctx_d, ctxT_d, mask0_d, mask3_d, small_d, rows_d, f0_d, l1_d, f1_d, l3_d, f3_d, out_d):
    with ExitStack() as ctx:
        def sb(name, shape, dt=F32):
            return ctx.enter_context(nc.sbuf_tensor(name, shape, dt))

        def sem(name):
            return ctx.enter_context(nc.semaphore(name))

        x_res = sb("x_res", [P, T * P])
        xl_res = sb("xl_res", [P, T * P])
        xnT = sb("xnT", [P, T * P])
        ctx_sb = sb("ctx_sb", [KC, T * (P + 1)])
        ctxT_sb = sb("ctxT_sb", [P, T * KC])
        mask0_sb = sb("mask0_sb", [P, T * KC], I32)
        mask3_sb = sb("mask3_sb", [P, T * KC], U8)
        small = sb("small", [P, N_SMALL])
        rows = sb("rows", [P, N_ROWS])
        f0_sb = sb("f0_sb", [P, 2 * E * P])
        w16_sb = sb("w16_sb", [P, 4 * 1024])
        w32_sb = sb("w32_sb", [P, 2 * E * F])
        cw = sb("cw", [P, J * E])

        big = sb("big", [P, 2 * FC * GT])
        kT = sb("kT", [P, C1 * J * 2 * KC])
        kv = sb("kv", [P, 2 * HS * LSW])
        gT_sb = kv[0:E, 0:GT]
        pT = sb("pT", [P, 2 * 1024])
        ebuf = sb("ebuf", [P, 2 * 1024])
        ob = sb("ob", [P, P])
        oT = sb("oT", [P, 1024])
        ctxTg = sb("ctxTg", [P, J * KC])
        xnG = sb("xnG", [P, GT])
        tmp = sb("tmp", [P, GT])
        acc = sb("acc", [P, GT])
        madd = sb("madd", [P, J * KC])
        mask3_f = sb("mask3_f", [P, T * KC])
        cwT = sb("cwT", [E, GT])
        vg = acc
        st = sb("st", [P, J, 6])
        mv = sb("mv", [P, J, 2])
        ve = sb("ve", [P, J])
        rstd = sb("rstd", [P, J])
        mhalf = sb("mhalf", [P, J])
        euler = sb("euler", [P, J])
        mx = sb("mx", [P, 32])
        rs = sb("rs", [P, 32])
        rt = [sb(f"rt{i}", [P, J * E]) for i in range(4)]
        rank8 = sb("rank8", [P, J * E])
        rv = [sb(f"rv{i}", [P, J]) for i in range(4)]

        psum = ctx.enter_context(nc.psum_tensor("psum", [P, 8 * 512], F32))
        bank = [psum[:, i * 512:(i + 1) * 512] for i in range(8)]

        def W(name, rows_=P):
            a, b = SMALL[name]
            return small[0:rows_, a:b]

        def R(name):
            a, b = ROWS[name]
            return rows[:, a:b]

        ident = W("ident")
        unmask_f = mask0_sb[:, :].bitcast(F32)

        in_small, in_ctx, in_rows, in_masks = sem("in_small"), sem("in_ctx"), sem("in_rows"), sem("in_masks")
        in_x = [sem(f"in_x{q}") for q in range(G)]
        in_mask3 = sem("in_mask3")
        in_f0, in_w16, in_w32 = sem("in_f0"), sem("in_w16"), sem("in_w32")
        out_done = sem("out_done")
        consts_ready = sem("consts_ready")
        dve_order = sem("dve_order")
        pool_order = sem("pool_order")
        var_ready, rstd_ready = sem("var_ready"), sem("rstd_ready")
        xn_ready, xnt_psum, xnT_ready = sem("xn_ready"), sem("xnt_psum"), sem("xnT_ready")
        x_final = sem("x_final")
        madd_ready = sem("madd_ready")

        LN_PER = [1, 1, 1, 1, 2, 1, 2, 2, 1]
        LN_BASE = [G * sum(LN_PER[:i]) for i in range(len(LN_PER) + 1)]

        def toks(t, n=P):
            return bass.ds(t * n, n)

        def grp(t):
            return t.rearrange("p (j d) -> p j d", j=J)

        block = ctx.enter_context(nc.Block())

        def ln_dve(dve, ch, src, dst, eps, n, used=None):
            for j in range(J):
                ch.link(dve.bn_stats(st[:, j, :], src[:, j, :]))
            ch.after()
            for j in range(J):
                ch.link(dve.bn_aggr(mv[:, j, :], st[:, j, :]))
            ch.after()
            dve.tensor_scalar(ve[:, :], mv[:, :, 1], eps, None, ALU.add).then_inc(var_ready, 1)
            dve.wait_ge(rstd_ready, n + 1)
            if used is not None:
                dve.wait_ge(xnt_psum, used)
            for j in range(J):
                ch.link(dve.tensor_scalar(dst[:, j, :], src[:, j, :], mv[:, j, 0:1], rstd[:, j:j + 1],
                                          ALU.subtract, ALU.mult))
            ch.after()

        def ln_pool(pool, n):
            pool.wait_ge(var_ready, n + 1)
            pool.tensor_tensor(rstd[:, :], ve[:, :], mhalf[:, :], ALU.pow).then_inc(rstd_ready, 1)

        def tail_dve(dve, ch, p, g):
            x_g = grp(x_res[:, toks(g, GT)])
            xl_g = grp(xl_res[:, toks(g, GT)])
            n = LN_BASE[p] + g * LN_PER[p]
            used = G * p + g + 1
            if p in (6, 7):
                ln_dve(dve, ch, x_g, xl_g, EPS, n)
                ln_dve(dve, ch, xl_g, grp(xnG[:, :]), EPS, n + 1, used)
            elif p == 8:
                ln_dve(dve, ch, xl_g, grp(xnG[:, :]), EPS, n, used)
            else:
                ln_dve(dve, ch, x_g, grp(xnG[:, :]), EPS, n + LN_PER[p] - 1, used)
            if p == 3:
                ch.link(dve.tensor_copy(xl_res[:, toks(g, GT)], xnG[:, :]))
                ch.after()
            dve.sem_inc(xn_ready, 1)

        def tail_pool(pool, p, g):
            for i in range(LN_PER[p]):
                ln_pool(pool, LN_BASE[p] + g * LN_PER[p] + i)

        def tail_pe(pe, p, g):
            pe.wait_ge(xn_ready, G * p + g + 1)
            pe.wait_ge(xnT_ready, G * p + g + 1)
            for j in range(J):
                ins = pe.transpose(bank[7][:, j * P:(j + 1) * P], xnG[:, j * P:(j + 1) * P], ident)
            ins.then_inc(xnt_psum, 1)

        def tail_act(act, p, g):
            act.wait_ge(xnt_psum, G * p + g + 2)
            gain = {6: "l3_gl", 7: "s_g1", 8: "s_g2"}.get(p)
            if gain:
                shift = {6: "l3_bl", 7: "s_b1", 8: "s_b2"}[p]
                ins = act.activation(xnT[:, toks(g, GT)], bank[7][:, :], ACT.Identity, bias=W(shift), scale=W(gain))
            else:
                ins = act.copy(xnT[:, toks(g, GT)], bank[7][:, :])
            ins.then_inc(xnT_ready, 1)

        def input_ready(eng, p, g):
            eng.wait_ge(xnT_ready, G * p + g + 2)

        def after(eng, semaphore, value):
            if not (isinstance(value, int) and value <= 0):
                eng.wait_ge(semaphore, value)

        class OneHead:
            def __init__(s, tag, p):
                s.tag, s.p = tag, p
                s.q_psum, s.q_ready = sem(f"{tag}_q_psum"), sem(f"{tag}_q_ready")
                s.k_psum, s.k_ready = sem(f"{tag}_k_psum"), sem(f"{tag}_k_ready")
                s.v_psum, s.v_ready = sem(f"{tag}_v_psum"), sem(f"{tag}_v_ready")
                s.s_psum, s.shift_ready, s.exp_ready = sem(f"{tag}_s_psum"), sem(f"{tag}_shift_ready"), sem(f"{tag}_exp_ready")
                s.pt_psum, s.pt_ready, s.o_psum = sem(f"{tag}_pt_psum"), sem(f"{tag}_pt_ready"), sem(f"{tag}_o_psum")
                s.ct_ready = sem(f"{tag}_ct_ready")

        A0 = OneHead("l0", 0)
        A2 = OneHead("l2", 4)
        qT1 = big[:, 0:GT]

        def vrow(t, n):
            return ctx_sb[:, bass.ds(t * (P + 1), n)]

        def onehead_pe(pe, A, g, tail):
            first = A is A0
            if g is not G:
                input_ready(pe, A.p, g)
                after(pe, A.q_ready, g)
                pe.matmul(bank[0][:, :], W("l0_w") if first else W("l2_wq"), xnT[:, toks(g, GT)],
                          start=True, stop=True).then_inc(A.q_psum, 1)
                if not first:
                    pe.wait_ge(A.ct_ready, g + 1)
                    pe.matmul(bank[2][:, 0:J * KC], W("l2_wk"), ctxTg[:, :], start=True, stop=True).then_inc(A.k_psum, 1)
            tail()
            if not (isinstance(g, int) and g == 0):
                pe.wait_ge(A.exp_ready, g)
                for j in range(J):
                    ins = pe.transpose(bank[4][0:KC, j * P:(j + 1) * P], ebuf[:, j * KC:(j + 1) * KC], ident)
                ins.then_inc(A.pt_psum, 1)
            if g is not G:
                pe.wait_ge(A.q_ready, g + 1)
                if not first:
                    pe.wait_ge(A.k_ready, g + 1)
                for j in range(J):
                    keys = ctxT_sb[:, bass.ds((g * J + j) * KC, KC)] if first else kT[:, j * KC:(j + 1) * KC]
                    ins = pe.matmul(bank[1][:, j * KC:(j + 1) * KC], qT1[:, j * P:(j + 1) * P], keys, start=True, stop=True)
                ins.then_inc(A.s_psum, 1)
            if not (isinstance(g, int) and g == 0):
                pe.wait_ge(A.pt_ready, g)
                if not first:
                    pe.wait_ge(A.v_ready, g)
                for j in range(J):
                    t = (g - 1) * J + j
                    vals = ctx_sb[0:KC, bass.ds(t * (P + 1), P + 1)] if first else kv[0:KC, j * (P + 1):(j + 1) * (P + 1)]
                    ins = pe.matmul(bank[5 + j // 2][:, (j % 2) * 256:(j % 2) * 256 + P + 1], pT[0:KC, j * P:(j + 1) * P],
                                    vals, start=True, stop=True)
                ins.then_inc(A.o_psum, 1)
            if g is not G and not first:
                after(pe, A.v_ready, g)
                for j in range(J):
                    ins = pe.matmul(bank[3][0:KC, j * P:(j + 1) * P], ctxTg[:, j * KC:(j + 1) * KC], W("l2_wv"),
                                    start=True, stop=True)
                ins.then_inc(A.v_psum, 1)

        def onehead_act(act, A, g, tail):
            first = A is A0
            if g is not G:
                act.wait_ge(A.q_psum, g + 1)
                act.activation(qT1, bank[0][:, :], ACT.Identity, bias=W("l0_b") if first else W("l2_bq")).then_inc(A.q_ready, 1)
                if not first:
                    act.wait_ge(A.k_psum, g + 1)
                    act.activation(kT[:, 0:J * KC], bank[2][:, 0:J * KC], ACT.Identity, bias=W("l2_bk")).then_inc(A.k_ready, 1)
            tail()
            if not (isinstance(g, int) and g == 0):
                act.wait_ge(A.pt_psum, g)
                act.copy(pT[0:KC, 0:GT], bank[4][0:KC, :]).then_inc(A.pt_ready, 1)
            if g is not G:
                act.wait_ge(A.shift_ready, g + 1)
                act.activation(ebuf[:, 0:J * KC], madd[:, :] if first else tmp[:, 0:J * KC], ACT.Exp,
                               scale=1.0 if first else float(P) ** -0.5).then_inc(A.exp_ready, 1)

        def onehead_dve(dve, ch, A, g):
            first = A is A0
            if g is not G:
                dve.wait_ge(A.s_psum, g + 1)
                src = bank[1][:, 0:J * KC]
                if first:
                    ch.link(dve.scalar_tensor_tensor(out=tmp[:, 0:J * KC], in0=unmask_f[:, bass.ds(g * J * KC, J * KC)],
                                                     scalar=NEG0, in1=src, op0=ALU.mult, op1=ALU.add))
                    ch.after()
                    src = tmp[:, 0:J * KC]
                src = src.rearrange("p (j k) -> p j k", j=J)
                ch.link(dve.tensor_reduce(mx[:, 0:J], src, AX.X, ALU.max))
                ch.after()
                dst = (madd[:, :] if first else tmp[:, 0:J * KC]).rearrange("p (j k) -> p j k", j=J)
                dve.tensor_tensor(dst, src, mx[:, 0:J, None].to_broadcast((P, J, KC)), ALU.subtract).then_inc(A.shift_ready, 1)
            if not (isinstance(g, int) and g == 0):
                dve.wait_ge(A.o_psum, g)
                for i in range(2):
                    o = bank[5 + i][:, :].rearrange("p (j d) -> p j d", j=2)
                    ch.link(dve.reciprocal(rs[:, 2 * i:2 * i + 2, None], o[:, :, P:P + 1]))
                ch.after()
                for j in range(J):
                    xt = x_res[:, toks((g - 1) * J + j)]
                    ch.link(dve.scalar_tensor_tensor(out=xt, in0=bank[5 + j // 2][:, (j % 2) * 256:(j % 2) * 256 + P],
                                                     scalar=rs[:, j:j + 1], in1=xt, op0=ALU.mult, op1=ALU.add))
                ch.after()
            if g is not G and not first:
                dve.wait_ge(A.v_psum, g + 1)
                vals = kv[0:KC, 0:J * (P + 1)].rearrange("p (j d) -> p j d", j=J)
                ch.link(dve.memset(vals[:, :, P:P + 1], 1.0))
                dve.tensor_tensor(vals[:, :, 0:P], grp(bank[3][0:KC, :]),
                                  R("l2_bv")[0:KC, None, :].to_broadcast((KC, J, P)), ALU.add).then_inc(A.v_ready, 1)
                ch.after()

        def onehead_pool(pool, g):
            after(pool, A2.v_psum, g)
            pool.tensor_copy(ctxTg[:, :], ctxT_sb[:, bass.ds(g * J * KC, J * KC)]).then_inc(A2.ct_ready, 1)

        gl_psum, gl_ready, g_psum, cw_ready = sem("gl_psum"), sem("gl_ready"), sem("g_psum"), sem("cw_ready")
        gap_ready, gexp_ready = sem("gap_ready"), sem("gexp_ready")
        h_psum, hT_ready, y_psum, y_used = sem("h_psum"), sem("hT_ready"), sem("y_psum"), sem("y_used")
        cwg_ready, cwt_psum, cwT_ready = sem("cwg_ready"), sem("cwt_psum"), sem("cwT_ready")
        H_BANKS = 4

        class Experts:
            def __init__(s, k, p, fc, func, w, wg, bg, b1, b2, top):
                s.k, s.p, s.fc, s.func, s.w, s.wg, s.bg, s.b1, s.b2, s.top = k, p, fc, func, w, wg, bg, b1, b2, top

            def w1(s, e, c):
                return s.w[:, (e * s.fc + c) * P:(e * s.fc + c + 1) * P]

            def w2(s, e, c):
                at = E * s.fc + e * s.fc + c
                return s.w[:, at * P:(at + 1) * P]

        M0 = Experts(0, 1, 1, ACT.Gelu, f0_sb, "f0_wg", "f0_bg", "f0_b1", "f0_b2", 1)
        M1 = Experts(1, 3, FC, ACT.Gelu, w32_sb, "f1_wr", "f1_br", "f1_b1", "f1_b2", 2)
        M3 = Experts(2, 8, FC, ACT.Relu, w32_sb, "f3_wg", "f3_bg", "f3_b1", "f3_b2", 1)
        HT_BASE = {0: H_BANKS, 1: H_BANKS + G * E, 2: H_BANKS + G * E + G * E * FC}
        YJ = E + 1

        def route_pe(pe, M, g):
            input_ready(pe, M.p, g)
            after(pe, r_ready, G * M.k + g)
            pe.matmul(bank[4][0:E, :], W(M.wg), xnT[:, toks(g, GT)], start=True, stop=True).then_inc(gl_psum, 1)

        def route_back_pe(pe, M, g):
            for j in range(J):
                ins = pe.transpose(bank[4][:, j * E:(j + 1) * E], gT_sb[:, j * P:(j + 1) * P], ident[0:E, 0:E])
            ins.then_inc(g_psum, 1)

        def route_act(act, M, g):
            act.wait_ge(gl_psum, G * M.k + g + 1)
            act.activation(gT_sb[:, :], bank[4][0:E, :], ACT.Identity, bias=W(M.bg, E)).then_inc(gl_ready, 1)

        r_ready = sem("r_ready")

        def route_dve(dve, ch, M, g):
            def te(t):
                return t[:, :].rearrange("p (j e) -> p j e", j=J)

            def wide(v):
                return v[:, :, None].to_broadcast((P, J, E))

            def first_of_greatest(src, hot, top, scratch, at):
                ch.link(dve.tensor_reduce(top[:, :], te(src), AX.X, ALU.max))
                ch.after()
                ch.link(dve.tensor_tensor(te(scratch), te(src), wide(top), ALU.is_ge))
                ch.after()
                ch.link(dve.tensor_tensor(te(scratch), te(scratch), te(rank8), ALU.mult))
                ch.after()
                ch.link(dve.tensor_reduce(at[:, :], te(scratch), AX.X, ALU.max))
                ch.after()
                ch.link(dve.tensor_tensor(te(hot), te(scratch), wide(at), ALU.is_equal))
                ch.after()

            dve.wait_ge(g_psum, G * M.k + g + 1)
            dve.tensor_copy(rt[0][:, :], bank[4][:, 0:J * E]).then_inc(r_ready, 1)
            dve.wait_ge(r_ready, G * M.k + g + 1)
            after(dve, cwt_psum, G * M.k + g)
            if M.top == 1:
                first_of_greatest(rt[0], cw, rv[0], rt[1], rv[1])
            else:
                first_of_greatest(rt[0], rt[2], rv[0], rt[1], rv[1])
                ch.link(dve.scalar_tensor_tensor(out=rt[0][:, :], in0=rt[2][:, :], scalar=NEG3, in1=rt[0][:, :],
                                                 op0=ALU.mult, op1=ALU.add))
                ch.after()
                first_of_greatest(rt[0], rt[3], rv[2], rt[1], rv[1])
                dve.tensor_tensor(rv[2][:, :], rv[2][:, :], rv[0][:, :], ALU.subtract).then_inc(gap_ready, 1)
                dve.wait_ge(gexp_ready, g + 1)
                ch.link(dve.tensor_scalar(rv[0][:, :], rv[3][:, :], 1.0, None, ALU.add))
                ch.after()
                ch.link(dve.reciprocal(rv[0][:, :], rv[0][:, :]))
                ch.after()
                ch.link(dve.tensor_tensor(rv[1][:, :], rv[3][:, :], rv[0][:, :], ALU.mult))
                ch.after()
                ch.link(dve.tensor_tensor(te(rt[2]), te(rt[2]), wide(rv[0]), ALU.mult))
                ch.link(dve.tensor_tensor(te(rt[3]), te(rt[3]), wide(rv[1]), ALU.mult))
                ch.after()
                ch.link(dve.tensor_tensor(cw[:, :], rt[2][:, :], rt[3][:, :], ALU.add))
                ch.after()
            dve.sem_inc(cwg_ready, 1)

        def route_pool(pool, g):
            pool.wait_ge(gap_ready, g + 1)
            pool.tensor_tensor(rv[3][:, :], euler[:, :], rv[2][:, :], ALU.pow).then_inc(gexp_ready, 1)

        def experts_pe(pe, M, g, tail):
            rhs = xnT[:, toks(g, GT)]
            n = E * M.fc

            def hidden(e, some=None):
                for c in some or range(M.fc):
                    k = e * M.fc + c
                    pe.wait_ge(hT_ready, HT_BASE[M.k] + g * n + k - H_BANKS + 1)
                    pe.matmul(bank[k % H_BANKS][:, :], M.w1(e, c), rhs, start=True, stop=True).then_inc(h_psum, 1)

            def y_job(i):
                after(pe, y_used, G * YJ * M.k + g * YJ + (i - 1 if i else 0))
                return bank[5 + i % 2]

            def biases():
                y = y_job(E)
                pe.wait_ge(cwT_ready, G * M.k + g + 1)
                for j in range(J):
                    ins = pe.matmul(y[:, j * P:(j + 1) * P], cwT[:, j * P:(j + 1) * P], W(M.b2, E), start=True, stop=True)
                ins.then_inc(y_psum, 1)

            def out(e):
                y = y_job(e)
                pe.wait_ge(hT_ready, HT_BASE[M.k] + g * n + (e + 1) * M.fc)
                for j in range(J):
                    for c in range(M.fc):
                        at = ((e % 2) * M.fc + c) * GT + j * P
                        ins = pe.matmul(y[:, j * P:(j + 1) * P], big[:, at:at + P], M.w2(e, c),
                                        start=(c == 0), stop=(c == M.fc - 1))
                ins.then_inc(y_psum, 1)

            route_pe(pe, M, g)
            hidden(0)
            pe.wait_ge(gl_ready, G * M.k + g + 1)
            hidden(1, [0])
            route_back_pe(pe, M, g)
            if M.fc > 1:
                hidden(1, range(1, M.fc))
            tail()
            for e in range(E):
                out(e)
                if e + 2 < E:
                    hidden(e + 2)
                if e == 3:
                    pe.wait_ge(cwg_ready, G * M.k + g + 1)
                    pe.wait_ge(xnT_ready, G * M.p + G + 1 + (0 if M is M3 else g))
                    for j in range(J):
                        ins = pe.transpose(bank[7][0:E, j * P:(j + 1) * P], cw[:, j * E:(j + 1) * E], ident)
                    ins.then_inc(cwt_psum, 1)
            biases()

        def experts_act(act, M, g, tail):
            n = E * M.fc

            def hidden(e):
                for c in range(M.fc):
                    k = e * M.fc + c
                    act.wait_ge(h_psum, HT_BASE[M.k] - H_BANKS + g * n + k + 1)
                    if c == 0:
                        after(act, y_psum, G * YJ * M.k + g * YJ + (e - 1 if e >= 2 else 0))
                    at = ((e % 2) * M.fc + c) * GT
                    act.activation(big[:, at:at + GT], bank[k % H_BANKS][:, :], M.func,
                                   bias=W(M.b1)[:, k:k + 1]).then_inc(hT_ready, 1)

            route_act(act, M, g)
            hidden(0)
            hidden(1)
            tail()
            for e in range(2, E):
                hidden(e)
                if e == 5:
                    act.wait_ge(cwt_psum, G * M.k + g + 1)
                    act.copy(cwT[:, :], bank[7][0:E, :]).then_inc(cwT_ready, 1)

        def experts_dve(dve, ch, M, g):
            route_dve(dve, ch, M, g)
            w = cw[:, :].rearrange("p (j e) -> p j e", j=J)
            for i in range(YJ):
                n = G * YJ * M.k + g * YJ + i + 1
                dve.wait_ge(y_psum, n)
                y = bank[5 + i % 2]
                if i == 0:
                    dve.tensor_tensor(grp(acc[:, :]), grp(y[:, :]), w[:, :, 0:1].to_broadcast((P, J, P)),
                                      ALU.mult).then_inc(y_used, 1)
                    dve.wait_ge(y_used, n)
                elif i == E:
                    dve.tensor_tensor(acc[:, :], y[:, :], acc[:, :], ALU.add).then_inc(y_used, 1)
                    dve.wait_ge(y_used, n)
                else:
                    dve.tensor_tensor(grp(tmp[:, :]), grp(y[:, :]), w[:, :, i:i + 1].to_broadcast((P, J, P)),
                                      ALU.mult).then_inc(y_used, 1)
                    dve.wait_ge(y_used, n)
                    ch.link(dve.tensor_tensor(acc[:, :], acc[:, :], tmp[:, :], ALU.add))
                    ch.after()
            x_g = x_res[:, toks(g, GT)]
            xl_g = xl_res[:, toks(g, GT)]
            if M is M1:
                ch.link(dve.tensor_tensor(acc[:, :], acc[:, :], xl_g, ALU.add))
                ch.after()
                ln_dve(dve, ch, grp(acc[:, :]), grp(tmp[:, :]), EPS_POST, LN_BASE[4] + g * LN_PER[4])
                for name, op in (("f1_lnw", ALU.mult), ("f1_lnb", ALU.add)):
                    ch.link(dve.tensor_tensor(grp(tmp[:, :]), grp(tmp[:, :]), R(name)[:, None, :].to_broadcast((P, J, P)), op))
                    ch.after()
                ch.link(dve.tensor_tensor(x_g, x_g, tmp[:, :], ALU.add))
                ch.after()
            else:
                ch.link(dve.tensor_tensor(x_g, x_g, acc[:, :], ALU.add))
                ch.after()
                if M is M3:
                    ch.link(dve.tensor_tensor(x_g, x_g, xl_g, ALU.add))
                    ch.after()

        s_psum, shift_ready, exp_ready, p_ready = sem("s_psum"), sem("shift_ready"), sem("exp_ready"), sem("p_ready")
        pt_psum, pt_ready, o_psum, ot_ready = sem("pt_psum"), sem("pt_ready"), sem("o_psum"), sem("ot_ready")
        w_psum, w_used = sem("w_psum"), sem("w_used")
        ls_o_ready, ls_ot_psum, ls_ot_ready = sem("ls_o_ready"), sem("ls_ot_psum"), sem("ls_ot_ready")
        kx_ready, vx_ready = sem("kx_ready"), sem("vx_ready")
        NJ = 2 * J
        LAST = NJ - 1

        class Heads:
            def __init__(s, k, p, nh, d, nk, scale, wo):
                s.k, s.p, s.nh, s.d, s.nk, s.scale, s.wo = k, p, nh, d, nk, scale, wo
                s.jh = nh // 2
                s.sl = s.jh // 2
                s.oc = nh * d // P

        HL1 = Heads(0, 2, H1, D1, KC, D1 ** -0.5, lambda c: w16_sb[:, 3072 + c * P:3072 + (c + 1) * P])
        HL3 = Heads(1, 6, H3, D3, K3, D3 ** -0.5, lambda c: w16_sb[:, 1536 + c * P:1536 + (c + 1) * P])
        HLS = Heads(2, 7, HS, DS, P, DS ** -0.5, lambda c: W("s_wo"))

        def e_slot(A, i):
            return ebuf[:, (i % 2) * 1024:(i % 2) * 1024 + A.jh * A.nk]

        def u_of(A, u):
            return (u % 2) * A.sl + u // 2 if A is HL3 else u

        def e_head(A, i, u):
            at = (i % 2) * 1024 + u_of(A, u) * A.nk
            return ebuf[:, at:at + A.nk]

        class HeadsPE:
            def __init__(s, pe, A, g):
                s.pe, s.A, s.g = pe, A, g
                s.nb = NJ * (G * A.k + g)
                s.tb = J * (G * A.k + g)

            def scores(s, i):
                pe, A, j, hh = s.pe, s.A, i // 2, i % 2
                b = 2 * (i % 2)
                after(pe, shift_ready, s.nb + i - 1)
                if A is HLS:
                    pe.wait_ge(kx_ready, J * s.g + j + 1)
                    for q in range(2):
                        at = (j % 2) * 2048 + (hh * A.jh + q * 4) * P
                        ins = pe.matmul(bank[b + q][:, :], kT[:, GT + j * P:GT + (j + 1) * P], big[:, at:at + 4 * P],
                                        start=True, stop=True)
                elif A is HL1:
                    for q in range(A.sl):
                        c = hh * A.sl + q
                        kc = (c * J + j) * 2 * KC
                        ins = pe.matmul(bank[b + q // 2][:, (q % 2) * 2 * KC:(q % 2 + 1) * 2 * KC],
                                        big[:, c * GT + j * P:c * GT + (j + 1) * P], kT[:, kc:kc + 2 * KC],
                                        start=True, stop=True)
                else:
                    for u in range(A.jh):
                        h = hh * A.jh + u
                        a = (h % 2) * 64
                        c = h // 2
                        kc = (c * J + j) * A.nk
                        ins = pe.matmul(bank[b + u % 2][:, (u // 2) * A.nk:(u // 2 + 1) * A.nk],
                                        big[a:a + 64, c * GT + j * P:c * GT + (j + 1) * P], kT[a:a + 64, kc:kc + A.nk],
                                        start=True, stop=True)
                ins.then_inc(s_psum, 1)

            def turn(s, i):
                pe, A = s.pe, s.A
                if A is HLS:
                    pe.wait_ge(exp_ready, s.nb + i + 1)
                else:
                    pe.wait_ge(p_ready, s.nb + i + 1)
                after(pe, pt_ready, s.nb + i)
                for u in range(A.jh):
                    e = e_head(A, i, u)
                    if A is HL3:
                        pe.transpose(bank[4][0:KC, u * P:(u + 1) * P], e[:, 0:KC], ident)
                        ins = pe.transpose(bank[5][:, u * P:(u + 1) * P], e[:, KC:K3], ident)
                    else:
                        ins = pe.transpose(bank[4 + u // 4][0:A.nk, (u % 4) * P:(u % 4 + 1) * P], e, ident)
                ins.then_inc(pt_psum, 1)

            def weigh(s, i):
                pe, A, j, hh = s.pe, s.A, i // 2, i % 2
                slot = (i % 2) * 1024
                pe.wait_ge(pt_ready, s.nb + i + 1)
                if A is HLS:
                    if i % 2 == 0:
                        after(pe, ls_o_ready, J * s.g + j)
                    pe.wait_ge(vx_ready, J * s.g + j + 1)
                    for u in range(A.jh):
                        h = hh * A.jh + u
                        at = ((j % 2) * HS + h) * LSW
                        ins = pe.matmul(bank[6][:, 0:LSW], pT[:, slot + u * P:slot + (u + 1) * P], kv[:, at:at + LSW],
                                        start=(h == 0), stop=(h == HS - 1))
                else:
                    after(pe, ot_ready, s.nb + i)
                    for u in range(A.jh):
                        h = hh * A.jh + u
                        a = (u % 2) * 64
                        out = bank[6][a:a + 64, (u // 2) * P:(u // 2 + 1) * P]
                        at = (j * A.nh + h) * A.d
                        if A is HL3:
                            pe.matmul(out, kv[0:KC, at:at + A.d], pT[0:KC, slot + u * P:slot + (u + 1) * P],
                                      start=True, stop=False)
                            at += J * A.nh * A.d
                            ins = pe.matmul(out, kv[:, at:at + A.d], pT[:, slot + 512 + u * P:slot + 512 + (u + 1) * P],
                                            start=False, stop=True)
                        else:
                            ins = pe.matmul(out, kv[0:KC, at:at + A.d], pT[0:KC, slot + u * P:slot + (u + 1) * P],
                                            start=True, stop=True)
                ins.then_inc(o_psum, 1)

            def turn_out(s, t):
                pe = s.pe
                pe.wait_ge(ls_o_ready, J * s.g + t + 1)
                after(pe, w_used, s.tb + t)
                pe.transpose(bank[7][:, P:2 * P], ob[:, :], ident).then_inc(ls_ot_psum, 1)

            def project(s, t):
                pe, A = s.pe, s.A
                if A is HLS:
                    pe.wait_ge(ls_ot_ready, J * s.g + t + 1)
                else:
                    pe.wait_ge(ot_ready, s.nb + 2 * t + 2)
                    after(pe, w_used, s.tb + t)
                for c in range(A.oc):
                    ins = pe.matmul(bank[7][:, 0:P], oT[:, c * P:(c + 1) * P], A.wo(c), start=(c == 0), stop=(c == A.oc - 1))
                ins.then_inc(w_psum, 1)

            def step(s, i):
                if i <= LAST:
                    s.turn(i)
                if 1 <= i <= NJ:
                    s.weigh(i - 1)
                if i + 2 <= LAST:
                    s.scores(i + 2)
                if s.A is HLS and i % 2 == 0 and i >= 2:
                    s.turn_out(i // 2 - 1)
                if i % 2 == 1 and i >= 3:
                    s.project(i // 2 - 1)

        class HeadsACT:
            def __init__(s, act, A, g):
                s.act, s.A, s.g = act, A, g
                s.nb = NJ * (G * A.k + g)
                s.tb = J * (G * A.k + g)

            def exps(s, i):
                act, A = s.act, s.A
                act.wait_ge(shift_ready, s.nb + i + 1)
                act.activation(e_slot(A, i), e_slot(A, i), ACT.Exp, scale=A.scale).then_inc(exp_ready, 1)

            def turned(s, i):
                act, A = s.act, s.A
                slot = (i % 2) * 1024
                act.wait_ge(pt_psum, s.nb + i + 1)
                after(act, o_psum, s.nb + i - 1)
                if A is HL3:
                    act.copy(pT[0:KC, slot:slot + 512], bank[4][0:KC, :])
                    act.copy(pT[:, slot + 512:slot + 1024], bank[5][:, :]).then_inc(pt_ready, 1)
                else:
                    act.copy(pT[0:A.nk, slot:slot + A.jh * P], psum[0:A.nk, 4 * 512:4 * 512 + A.jh * P]).then_inc(pt_ready, 1)

            def weighed(s, i):
                act, A, t = s.act, s.A, i // 2
                if A is HLS:
                    if i % 2:
                        act.wait_ge(ls_ot_psum, J * s.g + t + 1)
                        after(act, w_psum, s.tb + t)
                        act.copy(oT[:, 0:P], bank[7][:, P:2 * P]).then_inc(ls_ot_ready, 1)
                    return
                act.wait_ge(o_psum, s.nb + i + 1)
                if i % 2 == 0:
                    after(act, w_psum, s.tb + t)
                n = A.jh // 2
                for q in range(n):
                    c = (i % 2) * n + q
                    if A is HL1:
                        ins = act.activation(oT[:, c * P:(c + 1) * P], bank[6][:, q * P:(q + 1) * P], ACT.Identity,
                                             bias=W("l1_bv")[:, c:c + 1])
                    elif q == 0:
                        ins = act.copy(oT[:, c * P:(c + n) * P], bank[6][:, 0:n * P])
                ins.then_inc(ot_ready, 1)

            def step(s, i):
                if i <= LAST:
                    s.turned(i)
                if s.A is not HLS and 1 <= i <= NJ:
                    s.weighed(i - 1)
                if i + 2 <= LAST:
                    s.exps(i + 2)
                if s.A is HLS and i % 2 == 0 and i >= 2:
                    s.weighed(i - 1)

        class HeadsDVE:
            def __init__(s, dve, ch, A, g):
                s.dve, s.ch, s.A, s.g = dve, ch, A, g
                s.nb = NJ * (G * A.k + g)
                s.tb = J * (G * A.k + g)

            def tops(s, i):
                A = s.A
                return mx[:, (i % 2) * 8:(i % 2) * 8 + A.jh].rearrange("p (b s) -> p b s", b=2)

            def shift(s, i):
                dve, ch, A = s.dve, s.ch, s.A
                dve.wait_ge(s_psum, s.nb + i + 1)
                after(dve, pt_psum, s.nb + i - 1)
                b = 2 * (i % 2) * 512
                sc = psum[:, b:b + 1024].rearrange("p (b r) -> p b r", b=2)[:, :, 0:A.sl * A.nk]
                sc = sc.rearrange("p b (s k) -> p b s k", s=A.sl)
                if A is HL3:
                    m = mask3_f[:, bass.ds((s.g * J + i // 2) * KC, KC)]
                    ch.link(dve.tensor_tensor(sc[:, :, :, 0:KC], sc[:, :, :, 0:KC],
                                              m[:, None, None, :].to_broadcast((P, 2, A.sl, KC)), ALU.add))
                    ch.after()
                top = s.tops(i)
                ch.link(dve.tensor_reduce(top, sc, AX.X, ALU.max))
                ch.after()
                dst = e_slot(A, i).rearrange("p (b s k) -> p b s k", b=2, s=A.sl)
                dve.tensor_tensor(dst, sc, top[:, :, :, None].to_broadcast((P, 2, A.sl, A.nk)),
                                  ALU.subtract).then_inc(shift_ready, 1)

            def normalize(s, i):
                dve, ch, A = s.dve, s.ch, s.A
                if A is HLS:
                    return
                dve.wait_ge(exp_ready, s.nb + i + 1)
                e = e_slot(A, i).rearrange("p (h k) -> p h k", h=A.jh)
                r = rs[:, (i % 2) * 8:(i % 2) * 8 + A.jh]
                ch.link(dve.tensor_reduce(r, e, AX.X, ALU.add))
                ch.after()
                ch.link(dve.reciprocal(r, r))
                ch.after()
                dve.tensor_tensor(e, e, r[:, :, None].to_broadcast((P, A.jh, A.nk)), ALU.mult).then_inc(p_ready, 1)

            def output(s, t):
                dve, ch = s.dve, s.ch
                dve.wait_ge(o_psum, s.nb + 2 * t + 2)
                after(dve, ls_ot_psum, J * s.g + t)
                ch.link(dve.reciprocal(rs[:, 0:HS], bank[6][:, P:LSW]))
                ch.after()
                dve.tensor_tensor(ob[:, :].rearrange("p (h d) -> p h d", h=HS), bank[6][:, 0:P].rearrange("p (h d) -> p h d", h=HS),
                                  rs[:, 0:HS, None].to_broadcast((P, HS, DS)), ALU.mult).then_inc(ls_o_ready, 1)

            def add_x(s, t):
                dve, A = s.dve, s.A
                dve.wait_ge(w_psum, s.tb + t + 1)
                x_t = (xl_res if A is HLS else x_res)[:, toks(s.g * J + t)]
                dve.tensor_tensor(x_t, bank[7][:, 0:P], x_t, ALU.add).then_inc(w_used, 1)

            def step(s, i):
                if i + 1 <= LAST:
                    s.normalize(i + 1)
                if s.A is HLS and i % 2 == 0 and i >= 2:
                    s.output(i // 2 - 1)
                if i + 2 <= LAST:
                    s.shift(i + 2)
                if i % 2 == 1 and i >= 3:
                    s.add_x(i // 2 - 1)

        def heads_begin_pe(pe, A, g):
            h = HeadsPE(pe, A, g)
            h.scores(0)
            h.scores(1)
            for i in range(LAST):
                h.step(i)

        def heads_end_pe(pe, A, g):
            h = HeadsPE(pe, A, g)
            for i in range(LAST, NJ + 2):
                h.step(i)

        def heads_begin_act(act, A, g):
            h = HeadsACT(act, A, g)
            h.exps(0)
            h.exps(1)
            for i in range(LAST):
                h.step(i)

        def heads_end_act(act, A, g):
            h = HeadsACT(act, A, g)
            for i in range(LAST, NJ + 1):
                h.step(i)

        def heads_dve(dve, ch, A, g):
            h = HeadsDVE(dve, ch, A, g)
            h.shift(0)
            h.shift(1)
            h.normalize(0)
            for i in range(NJ + 2):
                h.step(i)
            dve.wait_ge(w_used, h.tb + J)
            if A is HLS:
                xl_g = grp(xl_res[:, toks(g, GT)])
                ch.link(dve.tensor_tensor(xl_g, xl_g, R("s_bo")[:, None, :].to_broadcast((P, J, P)), ALU.add))
                ch.after()

        def between(A, g, front, end, values, tail, begin):
            if g is not G:
                front(g)
            if not (isinstance(g, int) and g == 0):
                end(g - 1)
            if g is not G:
                values(g)
            tail()
            if g is not G:
                begin(g)

        l1_q_psum, l1_q_ready, l1_k_psum, l1_k_ready = sem("l1_q_psum"), sem("l1_q_ready"), sem("l1_k_psum"), sem("l1_k_ready")
        l1_v_psum, l1_v_ready, l1_ct_ready, l1_zero = sem("l1_v_psum"), sem("l1_v_ready"), sem("l1_ct_ready"), sem("l1_zero")
        NV = 2 * J

        def l1_front_pe(pe, g):
            input_ready(pe, 2, g)
            pe.wait_ge(l1_ct_ready, g + 1)
            after(pe, shift_ready, NJ * g)
            for c in range(C1):
                after(pe, l1_q_ready, g * C1 + c - 1)
                pe.matmul(bank[c % 2][:, :], w16_sb[:, c * P:(c + 1) * P], xnT[:, toks(g, GT)],
                          start=True, stop=True).then_inc(l1_q_psum, 1)
                after(pe, l1_k_ready, g * C1 + c - 1)
                pe.matmul(bank[2 + c % 2][:, 0:J * KC], w16_sb[:, 1024 + c * P:1024 + (c + 1) * P], ctxTg[:, :],
                          start=True, stop=True).then_inc(l1_k_psum, 1)

        def l1_values_pe(pe, g):
            after(pe, pt_ready, NJ * g)
            for i in range(NV):
                after(pe, l1_v_ready, g * NV + i - 1)
                pe.matmul(bank[4 + i % 2][0:KC, :], ctxTg[:, (i // 2) * KC:(i // 2 + 1) * KC],
                          w16_sb[:, 2048 + (i % 2) * 512:2048 + (i % 2 + 1) * 512],
                          start=True, stop=True).then_inc(l1_v_psum, 1)
            pe.wait_ge(l1_q_ready, (g + 1) * C1)
            pe.wait_ge(l1_k_ready, (g + 1) * C1)
            pe.wait_ge(l1_v_ready, (g + 1) * NV)

        def l1_front_act(act, g):
            if isinstance(g, int):
                act.wait_ge(l1_zero, 1)
            for c in range(C1):
                act.wait_ge(l1_q_psum, g * C1 + c + 1)
                act.activation(big[:, c * GT:(c + 1) * GT], bank[c % 2][:, :], ACT.Identity,
                               bias=W("l1_bq")[:, c:c + 1]).then_inc(l1_q_ready, 1)
                act.wait_ge(l1_k_psum, g * C1 + c + 1)
                dst = kT[:, c * J * 2 * KC:(c + 1) * J * 2 * KC].rearrange("p (j h k) -> p j h k", j=J, h=2)
                for h in range(2):
                    a = 64 * h
                    ins = act.activation(dst[a:a + 64, :, h, :], bank[2 + c % 2][a:a + 64, 0:J * KC].rearrange("p (j k) -> p j k", j=J),
                                         ACT.Identity, bias=W("l1_bk")[a:a + 64, c:c + 1])
                ins.then_inc(l1_k_ready, 1)

        def l1_values_act(act, g):
            for i in range(NV):
                act.wait_ge(l1_v_psum, g * NV + i + 1)
                act.copy(kv[0:KC, i * 512:(i + 1) * 512], bank[4 + i % 2][0:KC, :]).then_inc(l1_v_ready, 1)

        def l1_front_pool(pool, g):
            after(pool, l1_v_psum, g * NV)
            pool.tensor_copy(ctxTg[:, :], ctxT_sb[:, bass.ds(g * J * KC, J * KC)]).then_inc(l1_ct_ready, 1)

        lr_p_psum, lr_p_ready, lr_h_psum, lr_h_ready = sem("lr_p_psum"), sem("lr_p_ready"), sem("lr_h_psum"), sem("lr_h_ready")
        lr_q_psum, lr_q_ready, lr_o_psum = sem("lr_q_psum"), sem("lr_q_ready"), sem("lr_o_psum")

        def lowrank_pe(pe, g, tail):
            if g is not G:
                input_ready(pe, 5, g)
                pe.matmul(bank[0][0:RANK, :], W("f2_u1"), xnT[:, toks(g, GT)], start=True, stop=True).then_inc(lr_p_psum, 1)
            if not (isinstance(g, int) and g == 0):
                pe.wait_ge(lr_h_ready, g * FC)
                for c in range(FC):
                    ins = pe.matmul(bank[5][0:RANK, :], W("f2_u2")[:, c * RANK:(c + 1) * RANK], big[:, c * GT:(c + 1) * GT],
                                    start=(c == 0), stop=(c == FC - 1))
                ins.then_inc(lr_q_psum, 1)
            tail()
            if g is not G:
                pe.wait_ge(lr_p_ready, g + 1)
                for c in range(FC):
                    pe.matmul(bank[1 + c][:, :], W("f2_v1", RANK)[:, c * P:(c + 1) * P], kT[0:RANK, 0:GT],
                              start=True, stop=True).then_inc(lr_h_psum, 1)
            if not (isinstance(g, int) and g == 0):
                pe.wait_ge(lr_q_ready, g)
                for j in range(J):
                    ins = pe.matmul(bank[6][:, j * P:(j + 1) * P], kT[0:RANK, GT + j * P:GT + (j + 1) * P], W("f2_v2", RANK),
                                    start=True, stop=True)
                ins.then_inc(lr_o_psum, 1)

        def lowrank_act(act, g, tail):
            if g is not G:
                act.wait_ge(lr_p_psum, g + 1)
                act.copy(kT[0:RANK, 0:GT], bank[0][0:RANK, :]).then_inc(lr_p_ready, 1)
            if not (isinstance(g, int) and g == 0):
                act.wait_ge(lr_q_psum, g)
                act.copy(kT[0:RANK, GT:2 * GT], bank[5][0:RANK, :]).then_inc(lr_q_ready, 1)
            tail()
            if g is not G:
                for c in range(FC):
                    act.wait_ge(lr_h_psum, g * FC + c + 1)
                    act.activation(big[:, c * GT:(c + 1) * GT], bank[1 + c][:, :], ACT.Gelu_apprx_tanh,
                                   bias=W("f2_b1")[:, c:c + 1]).then_inc(lr_h_ready, 1)

        def lowrank_dve(dve, ch, g):
            x_g = x_res[:, toks(g, GT)]
            dve.wait_ge(lr_o_psum, g + 1)
            ch.link(dve.tensor_tensor(x_g, bank[6][:, :], x_g, ALU.add))
            ch.after()
            ch.link(dve.tensor_tensor(grp(x_g), grp(x_g), R("f2_b2")[:, None, :].to_broadcast((P, J, P)), ALU.add))
            ch.after()

        l3_lg_ready, l3_cn_ready, l3_cn_psum, l3_ct_ready = sem("l3_lg_ready"), sem("l3_cn_ready"), sem("l3_cn_psum"), sem("l3_ct_ready")
        l3_q_psum, l3_q_ready, l3_k_psum, l3_k_ready = sem("l3_q_psum"), sem("l3_q_ready"), sem("l3_k_psum"), sem("l3_k_ready")
        l3_v_psum, l3_v_ready = sem("l3_v_psum"), sem("l3_v_ready")
        latG = big[:, 4 * GT:5 * GT]
        NK3 = 2 * C3

        def l3_front_dve(dve, ch, g):
            dve.wait_ge(xnT_ready, G * 6 + g + 2)
            after(dve, l3_v_psum, g * 2 * J)
            dve.tensor_scalar(latG, xnT[:, toks(g, GT)], W("l3_gate"), None, ALU.mult).then_inc(l3_lg_ready, 1)
            src = ctx_sb[:, bass.ds(g * J * (P + 1), J * (P + 1))].rearrange("p (j d) -> p j d", j=J)
            for j in range(J):
                ch.link(dve.bn_stats(st[0:KC, j, :], src[:, j, 0:P]))
            ch.after()
            for j in range(J):
                ch.link(dve.bn_aggr(mv[0:KC, j, :], st[0:KC, j, :]))
            ch.after()
            dve.tensor_scalar(ve[:, :], mv[:, :, 1], EPS, None, ALU.add).then_inc(cvar_ready, 1)
            dve.wait_ge(crstd_ready, g + 1)
            for j in range(J):
                ch.link(dve.tensor_scalar(tmp[0:KC, j * P:(j + 1) * P], src[:, j, 0:P], mv[0:KC, j, 0:1],
                                          rstd[0:KC, j:j + 1], ALU.subtract, ALU.mult))
            ch.after()
            dve.sem_inc(l3_cn_ready, 1)

        cvar_ready, crstd_ready = sem("cvar_ready"), sem("crstd_ready")

        def l3_front_pool(pool, g):
            pool.wait_ge(cvar_ready, g + 1)
            pool.tensor_tensor(rstd[:, :], ve[:, :], mhalf[:, :], ALU.pow).then_inc(crstd_ready, 1)

        def l3_front_pe(pe, g):
            input_ready(pe, 6, g)
            after(pe, shift_ready, NJ * (G + g))
            for c in range(C3):
                pe.matmul(bank[c][:, :], w16_sb[:, c * P:(c + 1) * P], xnT[:, toks(g, GT)],
                          start=True, stop=True).then_inc(l3_q_psum, 1)

        def l3_values_pe(pe, g):
            after(pe, pt_ready, NJ * (G + g))
            pe.wait_ge(l3_cn_ready, g + 1)
            for j in range(J):
                ins = pe.transpose(bank[4][:, j * KC:(j + 1) * KC], tmp[0:KC, j * P:(j + 1) * P], ident[0:KC, 0:KC])
            ins.then_inc(l3_cn_psum, 1)
            pe.wait_ge(l3_lg_ready, g + 1)
            pe.wait_ge(l3_q_ready, (g + 1) * C3)
            for c in range(C3):
                w = w16_sb[:, 512 + c * P:512 + (c + 1) * P]
                for half, n in enumerate((GT, J * KC)):
                    if half and c == 0:
                        pe.wait_ge(l3_ct_ready, g + 1)
                    if c >= 2:
                        pe.wait_ge(l3_k_ready, g * NK3 + 2 * c + half - 3)
                    pe.matmul(bank[(2 * c + half) % 4][:, 0:n], w, ctxTg[:, :] if half else latG,
                              start=True, stop=True).then_inc(l3_k_psum, 1)
            for i in range(2 * J):
                if i >= 2:
                    pe.wait_ge(l3_v_ready, g * 2 * J + i - 1)
                j = i // 2
                wv = w16_sb[:, 1024:1536]
                if i % 2 == 0:
                    ins = pe.matmul(bank[4][0:KC, :], ctxTg[:, j * KC:(j + 1) * KC], wv, start=True, stop=True)
                else:
                    ins = pe.matmul(bank[5][:, :], latG[:, j * P:(j + 1) * P], wv, start=True, stop=True)
                ins.then_inc(l3_v_psum, 1)
            pe.wait_ge(l3_k_ready, (g + 1) * NK3)
            pe.wait_ge(l3_v_ready, (g + 1) * 2 * J)

        def l3_front_act(act, g):
            for c in range(C3):
                act.wait_ge(l3_q_psum, g * C3 + c + 1)
                act.copy(big[:, c * GT:(c + 1) * GT], bank[c][:, :]).then_inc(l3_q_ready, 1)

        def l3_values_act(act, g):
            act.wait_ge(l3_cn_psum, g + 1)
            act.activation(ctxTg[:, :], bank[4][:, 0:J * KC], ACT.Identity, bias=W("l3_bm"), scale=W("l3_gm")).then_inc(l3_ct_ready, 1)
            for c in range(C3):
                dst = kT[:, c * J * K3:(c + 1) * J * K3].rearrange("p (j k) -> p j k", j=J)
                for half, (a, n) in enumerate(((KC, P), (0, KC))):
                    act.wait_ge(l3_k_psum, g * NK3 + 2 * c + half + 1)
                    act.copy(dst[:, :, a:a + n],
                             bank[(2 * c + half) % 4][:, 0:J * n].rearrange("p (j k) -> p j k", j=J)).then_inc(l3_k_ready, 1)
            for i in range(2 * J):
                act.wait_ge(l3_v_psum, g * 2 * J + i + 1)
                at = (i // 2) * 512 + (i % 2) * J * 512
                if i % 2 == 0:
                    act.copy(kv[0:KC, at:at + 512], bank[4][0:KC, :]).then_inc(l3_v_ready, 1)
                else:
                    act.copy(kv[:, at:at + 512], bank[5][:, :]).then_inc(l3_v_ready, 1)

        ls_h_ready, ls_q_psum, ls_q_ready, ls_k_psum, ls_k_ready = [sem("ls_" + n) for n in
                                                                    ("h_ready", "q_psum", "q_ready", "k_psum", "k_ready")]
        ls_v_psum, ls_v_used, ls_zero = sem("ls_v_psum"), sem("ls_v_used"), sem("ls_zero")

        def ls_front_pool(pool, g):
            pool.wait_ge(xnT_ready, G * 7 + g + 2)
            after(pool, ls_v_psum, g)
            pool.tensor_copy(kT[:, 2 * GT:3 * GT], xnT[:, toks(g, GT)]).then_inc(ls_h_ready, 1)
            if isinstance(g, int):
                pool.wait_ge(o_psum, NJ * 2 * G)
                pool.memset(kv[:, :], 0.0).then_inc(ls_zero, 1)
                pool.wait_ge(ls_zero, 1)
                v = kv[:, :].rearrange("p (b h w) -> p b h w", b=2, h=HS)
                for h in range(HS):
                    ins = pool.memset(v[:, :, h, P + h:P + h + 1], 1.0)
                ins.then_inc(ls_zero, 1)
            pool.wait_ge(ls_k_ready, g + 1)

        def ls_kx_pool(pool, g, tiles):
            for j in tiles:
                pool.wait_ge(s_psum, NJ * (2 * G + g) + 2 * (j - 1))
                dst = big[:, (j % 2) * 2048:(j % 2 + 1) * 2048].rearrange("p (h k) -> p h k", h=HS)
                pool.tensor_tensor(dst, kT[:, None, j * P:(j + 1) * P].to_broadcast((P, HS, P)),
                                   W("headmask")[:, :, None].to_broadcast((P, HS, P)), ALU.mult).then_inc(kx_ready, 1)

        def ls_front_pe(pe, g):
            rhs = xnT[:, toks(g, GT)]
            input_ready(pe, 7, g)
            after(pe, shift_ready, NJ * (2 * G + g))
            pe.matmul(bank[0][:, :], W("s_wk"), rhs, start=True, stop=True).then_inc(ls_k_psum, 1)
            pe.matmul(bank[1][:, :], W("s_wq"), rhs, start=True, stop=True).then_inc(ls_q_psum, 1)

        def ls_values_pe(pe, g):
            pe.wait_ge(pt_ready, NJ * (2 * G + g))
            pe.wait_ge(ls_h_ready, g + 1)
            after(pe, ls_v_used, g)
            for j in range(J):
                ins = pe.matmul(bank[5][:, j * P:(j + 1) * P], kT[:, 2 * GT + j * P:2 * GT + (j + 1) * P], W("s_wv"),
                                start=True, stop=True)
            ins.then_inc(ls_v_psum, 1)
            pe.wait_ge(ls_q_ready, g + 1)
            pe.wait_ge(ls_k_ready, g + 1)
            pe.wait_ge(ls_v_used, g + 1)

        def ls_front_act(act, g):
            act.wait_ge(ls_k_psum, g + 1)
            after(act, kx_ready, J * g)
            act.activation(kT[:, 0:GT], bank[0][:, :], ACT.Identity, bias=W("s_bk")).then_inc(ls_k_ready, 1)
            act.wait_ge(ls_q_psum, g + 1)
            act.activation(kT[:, GT:2 * GT], bank[1][:, :], ACT.Identity, bias=W("s_bq")).then_inc(ls_q_ready, 1)

        def ls_values_act(act, g):
            act.wait_ge(ls_v_psum, g + 1)
            after(act, vx_ready, J * g)
            act.copy(vg[:, :], bank[5][:, :]).then_inc(ls_v_used, 1)

        def ls_spread_dve(dve, g, j):
            if j == 0:
                dve.wait_ge(ls_v_used, g + 1)
                if isinstance(g, int):
                    dve.wait_ge(ls_zero, 2)
            after(dve, o_psum, NJ * (2 * G + g) + 2 * (j - 1))
            b = (j % 2) * HS * LSW
            dst = kv[:, b:b + HS * LSW]
            dst = spread(dst)
            dve.tensor_tensor(dst, vg[:, j * P:(j + 1) * P].rearrange("p (h d) -> p h d", h=HS),
                              R("s_bv").rearrange("p (h d) -> p h d", h=HS), ALU.add).then_inc(vx_ready, 1)

        def spread(slot):
            pitch = LSW + DS
            return bass.AP(slot.tensor, slot.offset, [list(slot.ap[0]), [pitch, HS], [1, DS]])

        def by_tile(t):
            return t.rearrange("p (t d) -> p t d", t=T)

        @block.sync
        def _(sp):
            sp.dma_start(small[:, :], small_d).then_inc(in_small, 16)
            for q in range(G):
                sp.dma_start(by_tile(x_res[:, :])[:, q * J:(q + 1) * J, :],
                             x_d[q * J:(q + 1) * J].rearrange("t p d -> p t d")).then_inc(in_x[q], 16)
            sp.dma_start(ctxT_sb[:, :], ctxT_d).then_inc(in_ctx, 16)
            sp.dma_start(by_tile(mask0_sb[:, :]), mask0_d.rearrange("t p k -> p t k")).then_inc(in_masks, 16)
            sp.dma_start(by_tile(ctx_sb[:, :])[:, :, 0:P], ctx_d.rearrange("t k d -> k t d")).then_inc(in_ctx, 16)
            sp.dma_start(rows[:, :], rows_d.to_broadcast((P, N_ROWS))).then_inc(in_rows, 16)
            sp.dma_start(mask3_sb[:, :], mask3_d.to_broadcast((P, T * KC))).then_inc(in_mask3, 16)
            sp.dma_start(f0_sb[:, :], f0_d).then_inc(in_f0, 16)
            sp.dma_start(w16_sb[:, :], l1_d).then_inc(in_w16, 16)
            sp.dma_start(w32_sb[:, :], f1_d).then_inc(in_w32, 16)
            sp.wait_ge(w_psum, J * G)
            sp.dma_start(w16_sb[:, 0:2048], l3_d).then_inc(in_w16, 16)
            sp.wait_ge(y_psum, 2 * G * YJ)
            sp.dma_start(w32_sb[:, :], f3_d).then_inc(in_w32, 16)
            for q in range(G):
                sp.wait_ge(x_final, q + 1)
                sp.dma_start(out_d[q * J:(q + 1) * J].rearrange("t p d -> p t d"),
                             by_tile(x_res[:, :])[:, q * J:(q + 1) * J, :]).then_inc(out_done, 16)
            sp.wait_ge(out_done, 16 * G)

        def groups(eng, body):
            body(0)
            with eng.Fori(1, G) as g:
                body(g)

        @block.gpsimd
        def _(pool):
            pool.memset(mhalf[:, :], -0.5)
            pool.memset(euler[:, :], float(np.exp(1.0)))
            for e in range(E):
                pool.memset(rank8[:, :].rearrange("p (t e) -> p t e", t=J)[:, :, e:e + 1], float(E - e))
            pool.memset(by_tile(ctx_sb[:, :])[:, :, P:P + 1], 1.0).then_inc(consts_ready, 1)
            pool.memset(mv[:, :, :], 1.0).then_inc(consts_ready, 1)
            pool.wait_ge(consts_ready, 2)
            for g in range(G):
                tail_pool(pool, 0, g)
            pool.wait_ge(in_masks, 16)
            pool.tensor_scalar(unmask_f, mask0_sb[:, :], -1.0, 1.0, ALU.mult, ALU.add).then_inc(madd_ready, 1)
            pool.wait_ge(in_mask3, 16)
            pool.tensor_scalar(mask3_f[:, :], mask3_sb[:, :], NEG3, None, ALU.mult).then_inc(madd_ready, 1)
            pool.memset(kT[:, :], 0.0).then_inc(l1_zero, 1)

            def ahead(p, front):
                front(pool, 0)
                front(pool, 1)
                with pool.Fori(0, G - 2) as g:
                    tail_pool(pool, p, g)
                    front(pool, g + 2)
                tail_pool(pool, p, G - 2)
                tail_pool(pool, p, G - 1)

            def ls_pool(pool):
                ls_front_pool(pool, 0)
                ls_kx_pool(pool, 0, range(J))
                with pool.Fori(1, G) as g:
                    ls_front_pool(pool, g)
                    ls_kx_pool(pool, g, range(2))
                    tail_pool(pool, 8, g - 1)
                    ls_kx_pool(pool, g, range(2, J))
                tail_pool(pool, 8, G - 1)

            groups(pool, lambda g: tail_pool(pool, 1, g))
            groups(pool, lambda g: tail_pool(pool, 2, g))
            ahead(3, l1_front_pool)
            groups(pool, lambda g: (route_pool(pool, g), tail_pool(pool, 4, g)))
            ahead(5, onehead_pool)
            groups(pool, lambda g: tail_pool(pool, 6, g))
            groups(pool, lambda g: (l3_front_pool(pool, g), tail_pool(pool, 7, g)))
            ls_pool(pool)

        @block.vector
        def _(dve):
            ch = Chain(dve, dve_order)
            dve.wait_ge(consts_ready, 2)
            for g in range(G):
                dve.wait_ge(in_x[g], 16)
                tail_dve(dve, ch, 0, g)
            ch.restart()
            dve.wait_ge(madd_ready, 2)
            dve.wait_ge(in_rows, 16)

            def phase(p, body):
                def whole(g):
                    body(g)
                    if p < 9:
                        tail_dve(dve, ch, p, g)
                    ch.restart()
                groups(dve, whole)

            def phase_behind(p, body):
                body(0)
                ch.restart()
                with dve.Fori(1, G) as g:
                    body(g)
                    tail_dve(dve, ch, p, g - 1)
                    ch.restart()
                body(G)
                tail_dve(dve, ch, p, G - 1)
                ch.restart()

            def last(g):
                experts_dve(dve, ch, M3, g)
                dve.sem_inc(x_final, 1)

            def self_attention(g):
                h = HeadsDVE(dve, ch, HLS, g)
                ls_spread_dve(dve, g, 0)
                h.shift(0)
                h.shift(1)
                for i in range(NJ + 2):
                    if i % 2 == 0 and i // 2 + 1 < J:
                        ls_spread_dve(dve, g, i // 2 + 1)
                    h.step(i)
                dve.wait_ge(w_used, h.tb + J)
                xl_g = grp(xl_res[:, toks(g, GT)])
                ch.link(dve.tensor_tensor(xl_g, xl_g, R("s_bo")[:, None, :].to_broadcast((P, J, P)), ALU.add))
                ch.after()

            phase_behind(1, lambda g: onehead_dve(dve, ch, A0, g))
            phase(2, lambda g: experts_dve(dve, ch, M0, g))
            phase(3, lambda g: heads_dve(dve, ch, HL1, g))
            phase(4, lambda g: experts_dve(dve, ch, M1, g))
            phase_behind(5, lambda g: onehead_dve(dve, ch, A2, g))
            phase(6, lambda g: lowrank_dve(dve, ch, g))
            phase(7, lambda g: (l3_front_dve(dve, ch, g), heads_dve(dve, ch, HL3, g)))
            phase(8, self_attention)
            phase(9, last)

        def late_tails(eng, tail_of, pending, p, body, behind):

            def tail(g):
                return lambda: tail_of(eng, p, g)

            def none():
                pass

            body(0, pending)
            if behind:
                body(1, none)
                with eng.Fori(2, G) as g:
                    body(g, tail(g - 2))
                body(G, tail(G - 2))
                return tail(G - 1)
            with eng.Fori(1, G) as g:
                body(g, tail(g - 1))
            return tail(G - 1)

        @block.scalar
        def _(act):
            act.sem_inc(xnT_ready, 1)
            act.sem_inc(hT_ready, H_BANKS)
            act.wait_ge(in_small, 16)
            for g in range(G - 1):
                tail_act(act, 0, g)

            def heads(A, front, values):
                def body(g, tail):
                    between(A, g, lambda g: front(act, g), lambda g: heads_end_act(act, A, g), lambda g: values(act, g), tail,
                            lambda g: heads_begin_act(act, A, g))
                return body

            def run(pending, p, body, behind=False, ends=None):
                pending = late_tails(act, tail_act, pending, p, body, behind)
                if ends:
                    ends()
                return pending

            t = lambda: tail_act(act, 0, G - 1)
            t = run(t, 1, lambda g, tail: onehead_act(act, A0, g, tail), True)
            t = run(t, 2, lambda g, tail: experts_act(act, M0, g, tail))
            t = run(t, 3, heads(HL1, l1_front_act, l1_values_act), ends=lambda: heads_end_act(act, HL1, G - 1))
            t = run(t, 4, lambda g, tail: experts_act(act, M1, g, tail))
            t = run(t, 5, lambda g, tail: onehead_act(act, A2, g, tail), True)
            t = run(t, 6, lambda g, tail: lowrank_act(act, g, tail), True)
            t = run(t, 7, heads(HL3, l3_front_act, l3_values_act), ends=lambda: heads_end_act(act, HL3, G - 1))
            t = run(t, 8, heads(HLS, ls_front_act, ls_values_act), ends=lambda: heads_end_act(act, HLS, G - 1))
            t = run(t, 9, lambda g, tail: experts_act(act, M3, g, tail if isinstance(g, int) else lambda: None))

        @block.tensor
        def _(pe):
            pe.sem_inc(xnt_psum, 1)
            pe.wait_ge(in_small, 16)
            for g in range(G - 1):
                tail_pe(pe, 0, g)
            pe.wait_ge(in_ctx, 32)
            pe.wait_ge(consts_ready, 2)

            def heads(A, front, values):
                def body(g, tail):
                    between(A, g, lambda g: front(pe, g), lambda g: heads_end_pe(pe, A, g), lambda g: values(pe, g), tail,
                            lambda g: heads_begin_pe(pe, A, g))
                return body

            def run(pending, p, body, behind=False, ends=None, needs=None):
                if needs:
                    pe.wait_ge(*needs)
                pending = late_tails(pe, tail_pe, pending, p, body, behind)
                if ends:
                    ends()
                return pending

            t = lambda: tail_pe(pe, 0, G - 1)
            t = run(t, 1, lambda g, tail: onehead_pe(pe, A0, g, tail), True)
            t = run(t, 2, lambda g, tail: experts_pe(pe, M0, g, tail), needs=(in_f0, 16))
            t = run(t, 3, heads(HL1, l1_front_pe, l1_values_pe), ends=lambda: heads_end_pe(pe, HL1, G - 1), needs=(in_w16, 16))
            t = run(t, 4, lambda g, tail: experts_pe(pe, M1, g, tail), needs=(in_w32, 16))
            t = run(t, 5, lambda g, tail: onehead_pe(pe, A2, g, tail), True)
            t = run(t, 6, lambda g, tail: lowrank_pe(pe, g, tail), True)
            t = run(t, 7, heads(HL3, l3_front_pe, l3_values_pe), ends=lambda: heads_end_pe(pe, HL3, G - 1), needs=(in_w16, 32))
            t = run(t, 8, heads(HLS, ls_front_pe, ls_values_pe), ends=lambda: heads_end_pe(pe, HLS, G - 1))
            t = run(t, 9, lambda g, tail: experts_pe(pe, M3, g, tail if isinstance(g, int) else lambda: None), needs=(in_w32, 32))


def kernel(**inputs):
    import concourse.bacc as bacc
    from concourse.bass_utils import run_bass_kernel_spmd

    a = {k: np.asarray(v) for k, v in inputs.items()}

    def pad(m):
        m = m.reshape(m.shape[0], -1)
        return np.concatenate([m, np.zeros((P - m.shape[0], m.shape[1]), m.dtype)], 0)

    def chunks(v):
        return v.reshape(-1, P).T

    head = np.zeros((P, HS), np.float32)
    head[np.arange(P), np.arange(P) // DS] = 1.0
    pieces = {
        "ident": np.eye(P, dtype=np.float32), "headmask": head,
        "l0_w": a["L0_xattn_W"].T, "l0_b": a["L0_xattn_b"][:, None],
        "f0_wg": a["L0_ffn_Wg"], "f0_bg": a["L0_ffn_bg"][:, None], "f0_b1": a["L0_ffn_b1"].T, "f0_b2": a["L0_ffn_b2"],
        "l1_bq": chunks(a["L1_xattn_bq"]), "l1_bk": chunks(a["L1_xattn_bk"]), "l1_bv": chunks(a["L1_xattn_bv"]),
        "f1_wr": a["L1_ffn_Wr"].T, "f1_br": a["L1_ffn_br"][:, None], "f1_b1": chunks(a["L1_ffn_b1"].reshape(-1)),
        "f1_b2": a["L1_ffn_b2"],
        "l2_wq": a["L2_xattn_Wq"].T, "l2_bq": a["L2_xattn_bq"][:, None], "l2_wk": a["L2_xattn_Wk"].T,
        "l2_bk": a["L2_xattn_bk"][:, None], "l2_wv": a["L2_xattn_Wv"].T,
        "f2_u1": a["L2_ffn_U1"], "f2_v1": a["L2_ffn_V1"], "f2_b1": chunks(a["L2_ffn_b1"]),
        "f2_u2": a["L2_ffn_U2"].reshape(FC, P, RANK).transpose(1, 0, 2), "f2_v2": a["L2_ffn_V2"],
        "l3_gm": a["L3_xattn_gamma_media"][:, None], "l3_bm": a["L3_xattn_beta_media"][:, None],
        "l3_gl": a["L3_xattn_gamma_lat"][:, None], "l3_bl": a["L3_xattn_beta_lat"][:, None],
        "l3_gate": np.repeat(a["L3_xattn_kv_gate"].reshape(1, 1), P, 0),
        "s_g1": a["L3_ffn_ln1_g"][:, None], "s_b1": a["L3_ffn_ln1_b"][:, None],
        "s_g2": a["L3_ffn_ln2_g"][:, None], "s_b2": a["L3_ffn_ln2_b"][:, None],
        "s_wq": a["L3_ffn_wq"], "s_bq": a["L3_ffn_bq"][:, None], "s_wk": a["L3_ffn_wk"], "s_bk": a["L3_ffn_bk"][:, None],
        "s_wv": a["L3_ffn_wv"], "s_wo": a["L3_ffn_wo"],
        "f3_wg": a["L3_ffn_gate_w"], "f3_bg": a["L3_ffn_gate_b"][:, None], "f3_b1": chunks(a["L3_ffn_b1"].reshape(-1)),
        "f3_b2": a["L3_ffn_b2"],
    }
    small = np.concatenate([pad(pieces[name]) for name, _ in W_SMALL], 1)
    rows = np.concatenate([a[k].reshape(1, -1) for k in ("L1_ffn_ln_w", "L1_ffn_ln_b", "L2_xattn_bv",
                                                         "L2_ffn_b2", "L3_ffn_bv", "L3_ffn_bo")], 1)

    def inner(m):
        return m.transpose(1, 0, 2).reshape(P, -1)

    f0 = np.concatenate([inner(a["L0_ffn_W1"]), inner(a["L0_ffn_W2"])], 1)
    l1 = np.concatenate([a["L1_xattn_Wq"].T, a["L1_xattn_Wk"].T, a["L1_xattn_Wv"].T,
                         inner(a["L1_xattn_Wo"].T.reshape(C1, P, P))], 1)
    f1 = np.concatenate([inner(a["L1_ffn_W1"].transpose(0, 2, 1)),
                         inner(a["L1_ffn_W2"].transpose(0, 2, 1).reshape(E * FC, P, P))], 1)
    l3 = np.concatenate([a["L3_xattn_Wq"], a["L3_xattn_Wk"], a["L3_xattn_Wv"],
                         inner(a["L3_xattn_Wout"].reshape(C3, P, P))], 1)
    f3 = np.concatenate([inner(a["L3_ffn_w1"]), inner(a["L3_ffn_w2"].reshape(E * FC, P, P))], 1)
    arrays = {
        "x": a["x"], "ctx": a["ctx_1024"], "ctxT": a["ctx_1024"].transpose(2, 0, 1).reshape(P, T * KC),
        "mask0": a["mask_BxSxS2_ik0"], "mask3": a["mask_BxS2_bk0"].reshape(1, T * KC),
        "small": small, "rows": rows, "f0": f0, "l1": l1, "f1": f1, "l3": l3, "f3": f3,
    }
    nc = bacc.Bacc("TRN2", target_bir_lowering=False, num_devices=1)
    feeds, args = {}, []
    for name, arr in arrays.items():
        arr = np.ascontiguousarray(arr)
        feeds[f"in_{name}"] = arr
        args.append(nc.dram_tensor(f"in_{name}", arr.shape, mybir.dt.from_np(arr.dtype), kind="ExternalInput").ap())
    args.append(nc.dram_tensor("out_x", (T, P, P), F32, kind="ExternalOutput").ap())
    build(nc, *args)
    r = run_bass_kernel_spmd(nc, [feeds], core_ids=[0])
    return r.results[0]["out_x"]
```

```python
from contextlib import ExitStack

import numpy as np

import concourse.bass as bass
from concourse import mybir

F32 = mybir.dt.float32
F32R = mybir.dt.float32r
I32 = mybir.dt.int32
U8 = mybir.dt.uint8
ALU = mybir.AluOpType
ACT = mybir.ActivationFunctionType
AX = mybir.AxisListType

P = 128
T = 16
J = 4
G = T // J
GT = J * P
KC = 77
E = 8
F = 512
FC = F // P
H1, D1 = 16, 64
C1 = H1 * D1 // P
H3, D3 = 8, 64
C3 = H3 * D3 // P
K3 = KC + P
HS, DS = 16, 8
RANK = 32
EPS = 1e-5
EPS_POST = 1e-12
NEG0 = -1000000.0
NEG3 = -1e30
LSW = P + HS

W_SMALL = [("ident", P), ("headmask", HS), ("l0_w", P), ("l0_b", 1), ("f0_wg", E), ("f0_bg", 1), ("f0_b1", E),
           ("f0_b2", P), ("l1_bq", C1), ("l1_bk", C1), ("l1_bv", C1), ("f1_wr", E), ("f1_br", 1), ("f1_b1", E * FC), ("f1_b2", P),
           ("l2_wq", P), ("l2_bq", 1), ("l2_wk", P), ("l2_bk", 1), ("l2_wv", P),
           ("f2_u1", RANK), ("f2_v1", F), ("f2_b1", FC), ("f2_u2", FC * RANK), ("f2_v2", P),
           ("l3_gm", 1), ("l3_bm", 1), ("l3_gl", 1), ("l3_bl", 1), ("l3_gate", 1),
           ("s_g1", 1), ("s_b1", 1), ("s_g2", 1), ("s_b2", 1), ("s_wq", P), ("s_bq", 1), ("s_wk", P), ("s_bk", 1),
           ("s_wv", P), ("s_wo", P), ("f3_wg", E), ("f3_bg", 1), ("f3_b1", E * FC), ("f3_b2", P)]
W_ROWS = [("f1_lnw", P), ("f1_lnb", P), ("l2_bv", P), ("f2_b2", P), ("s_bv", P), ("s_bo", P)]


def columns(table):
    at, out = 0, {}
    for name, width in table:
        out[name] = (at, at + width)
        at += width
    return out, at


SMALL, N_SMALL = columns(W_SMALL)
ROWS, N_ROWS = columns(W_ROWS)
N_FIRST = SMALL["f0_wg"][0]


class Chain:

    def __init__(self, eng, sem):
        self.eng, self.sem, self.n = eng, sem, 0

    def link(self, ins):
        ins.then_inc(self.sem, 1)
        self.n += 1

    def after(self):
        self.eng.wait_ge(self.sem, self.n)

    def restart(self):
        self.after()
        self.eng.sem_clear(self.sem)
        self.n = 0


def build(nc, x_d, ctx_d, ctxT_d, mask0_d, mask3_d, small_d, rows_d, f0_d, l1_d, f1_d, l3_d, f3_d, out_d):
    with ExitStack() as ctx:
        def sb(name, shape, dt=F32):
            return ctx.enter_context(nc.sbuf_tensor(name, shape, dt))

        def sem(name):
            return ctx.enter_context(nc.semaphore(name))

        x_res = sb("x_res", [P, T * P])
        xl_res = sb("xl_res", [P, T * P])
        xnT = sb("xnT", [P, T * P])
        ctx_sb = sb("ctx_sb", [KC, T * (P + 1)])
        ctxT_sb = sb("ctxT_sb", [P, T * KC])
        mask0_sb = sb("mask0_sb", [P, T * KC], I32)
        mask3_sb = sb("mask3_sb", [P, T * KC], U8)
        small = sb("small", [P, N_SMALL])
        rows = sb("rows", [P, N_ROWS])
        w32_sb = sb("w32_sb", [P, 2 * E * F])
        cw = sb("cw", [P, J * E])

        big = sb("big", [P, 2 * FC * GT])
        kv = sb("kv", [P, 2 * HS * LSW])
        with ExitStack() as first_use:
            def over(name, shape):
                return first_use.enter_context(nc.sbuf_tensor(name, shape, F32))

            f0_sb = over("f0_sb", [P, 2 * E * P])
            w16_sb = over("w16_sb", [P, 4 * 1024])
            kT = over("kT", [P, C1 * J * 2 * KC])
        x_half = sb("x_half", [P, 2 * E * P], F32R)
        w1_lo = sb("w1_lo", [P, 4 * 1024], F32R)
        w1_hi = sb("w1_hi", [P, C1 * J * 2 * KC], F32R)
        gT_sb = kv[0:E, 0:GT]
        pT = sb("pT", [P, 2 * 1024])
        ebuf = sb("ebuf", [P, 2 * 1024])
        ob = sb("ob", [P, P])
        oT = sb("oT", [P, 1024])
        ctxTg = sb("ctxTg", [P, J * KC])
        xnG = sb("xnG", [P, GT])
        tmp = sb("tmp", [P, GT])
        acc = sb("acc", [P, GT])
        madd = sb("madd", [P, J * KC])
        mask3_f = sb("mask3_f", [P, T * KC])
        cwT = sb("cwT", [E, GT])
        vg = acc
        st = sb("st", [P, J, 6])
        mv = sb("mv", [P, J, 2])
        ve = sb("ve", [P, J])
        rstd = sb("rstd", [P, J])
        mhalf = sb("mhalf", [P, J])
        euler = sb("euler", [P, J])
        mx = sb("mx", [P, 32])
        rs = sb("rs", [P, 32])
        rt = [sb(f"rt{i}", [P, J * E]) for i in range(4)]
        rank8 = sb("rank8", [P, J * E])
        rv = [sb(f"rv{i}", [P, J]) for i in range(4)]

        psum = ctx.enter_context(nc.psum_tensor("psum", [P, 8 * 512], F32))
        bank = [psum[:, i * 512:(i + 1) * 512] for i in range(8)]

        def W(name, rows_=P):
            a, b = SMALL[name]
            return small[0:rows_, a:b]

        def R(name):
            a, b = ROWS[name]
            return rows[:, a:b]

        ident = W("ident")
        unmask_f = mask0_sb[:, :].bitcast(F32)

        in_small, in_rest, in_ctxT = sem("in_small"), sem("in_rest"), sem("in_ctxT")
        in_ctx, in_rows, in_masks = sem("in_ctx"), sem("in_rows"), sem("in_masks")
        in_x = [sem(f"in_x{q}") for q in range(G)]
        in_mask3 = sem("in_mask3")
        in_f0, in_w16, in_w32 = sem("in_f0"), sem("in_w16"), sem("in_w32")
        out_done = sem("out_done")
        consts_ready = sem("consts_ready")
        dve_order = sem("dve_order")
        pool_order = sem("pool_order")
        var_ready, rstd_ready = sem("var_ready"), sem("rstd_ready")
        xn_ready, xnt_psum, xnT_ready = sem("xn_ready"), sem("xnt_psum"), sem("xnT_ready")
        x_final = sem("x_final")
        madd_ready = sem("madd_ready")

        LN_PER = [1, 1, 1, 1, 2, 1, 2, 2, 1]
        LN_BASE = [G * sum(LN_PER[:i]) for i in range(len(LN_PER) + 1)]

        def toks(t, n=P):
            return bass.ds(t * n, n)

        def grp(t):
            return t.rearrange("p (j d) -> p j d", j=J)

        block = ctx.enter_context(nc.Block())

        def ln_stats_dve(dve, ch, src, eps):
            for j in range(J):
                ch.link(dve.bn_stats(st[:, j, :], src[:, j, :]))
            ch.after()
            for j in range(J):
                ch.link(dve.bn_aggr(mv[:, j, :], st[:, j, :]))
            ch.after()
            dve.tensor_scalar(ve[:, :], mv[:, :, 1], eps, None, ALU.add).then_inc(var_ready, 1)

        def ln_apply_dve(dve, ch, src, dst, n, used=None):
            dve.wait_ge(rstd_ready, n + 1)
            if used is not None:
                dve.wait_ge(xnt_psum, used)
            for j in range(J):
                ch.link(dve.tensor_scalar(dst[:, j, :], src[:, j, :], mv[:, j, 0:1], rstd[:, j:j + 1],
                                          ALU.subtract, ALU.mult))
            ch.after()

        def ln_pool(pool, n):
            pool.wait_ge(var_ready, n + 1)
            pool.tensor_tensor(rstd[:, :], ve[:, :], mhalf[:, :], ALU.pow).then_inc(rstd_ready, 1)

        def tail_parts_dve(dve, ch, p, g):
            x_g = grp(x_res[:, toks(g, GT)])
            xl_g = grp(xl_res[:, toks(g, GT)])
            n = LN_BASE[p] + g * LN_PER[p]
            used = G * p + g + 1
            out = grp(xnG[:, :])

            def x_stats():
                ln_stats_dve(dve, ch, x_g, EPS)

            def x_apply():
                ln_apply_dve(dve, ch, x_g, out, n + LN_PER[p] - 1, used)
                if p == 3:
                    ch.link(dve.tensor_copy(xl_res[:, toks(g, GT)], xnG[:, :]))
                    ch.after()
                dve.sem_inc(xn_ready, 1)

            def xl_stats():
                if p != 8:
                    ln_apply_dve(dve, ch, x_g, xl_g, n)
                ln_stats_dve(dve, ch, xl_g, EPS)

            def xl_apply():
                ln_apply_dve(dve, ch, xl_g, out, n + LN_PER[p] - 1, used)
                dve.sem_inc(xn_ready, 1)

            if p in (6, 7):
                return [x_stats, xl_stats, xl_apply]
            return [xl_stats, xl_apply] if p == 8 else [x_stats, x_apply]

        def tail_dve(dve, ch, p, g):
            for part in tail_parts_dve(dve, ch, p, g):
                part()

        def tail_pool(pool, p, g):
            for i in range(LN_PER[p]):
                ln_pool(pool, LN_BASE[p] + g * LN_PER[p] + i)

        def tail_pe(pe, p, g):
            pe.wait_ge(xn_ready, G * p + g + 1)
            pe.wait_ge(xnT_ready, G * p + g + 1)
            for j in range(J):
                ins = pe.transpose(bank[7][:, j * P:(j + 1) * P], xnG[:, j * P:(j + 1) * P], ident)
            ins.then_inc(xnt_psum, 1)

        def tail_act(act, p, g):
            act.wait_ge(xnt_psum, G * p + g + 2)
            gain = {6: "l3_gl", 7: "s_g1", 8: "s_g2"}.get(p)
            if gain:
                shift = {6: "l3_bl", 7: "s_b1", 8: "s_b2"}[p]
                ins = act.activation(xnT[:, toks(g, GT)], bank[7][:, :], ACT.Identity, bias=W(shift), scale=W(gain))
            else:
                ins = act.copy(xnT[:, toks(g, GT)], bank[7][:, :])
            ins.then_inc(xnT_ready, 1)

        def input_ready(eng, p, g):
            eng.wait_ge(xnT_ready, G * p + g + 2)

        def after(eng, semaphore, value):
            if not (isinstance(value, int) and value <= 0):
                eng.wait_ge(semaphore, value)

        class OneHead:
            def __init__(s, tag, p):
                s.tag, s.p = tag, p
                s.q_psum, s.q_ready = sem(f"{tag}_q_psum"), sem(f"{tag}_q_ready")
                s.k_psum, s.k_ready = sem(f"{tag}_k_psum"), sem(f"{tag}_k_ready")
                s.v_psum, s.v_ready = sem(f"{tag}_v_psum"), sem(f"{tag}_v_ready")
                s.s_psum, s.shift_ready, s.exp_ready = sem(f"{tag}_s_psum"), sem(f"{tag}_shift_ready"), sem(f"{tag}_exp_ready")
                s.pt_psum, s.pt_ready, s.o_psum = sem(f"{tag}_pt_psum"), sem(f"{tag}_pt_ready"), sem(f"{tag}_o_psum")
                s.ct_ready, s.o_used = sem(f"{tag}_ct_ready"), sem(f"{tag}_o_used")

        A0 = OneHead("l0", 0)
        A2 = OneHead("l2", 4)
        qT1 = big[:, 0:GT]

        def ctxT_of(g):
            return madd if isinstance(g, int) and g == 1 else ctxTg

        def onehead_pe(pe, A, g, tail):
            first = A is A0
            if g is not G:
                input_ready(pe, A.p, g)
                after(pe, A.q_ready, g)
                pe.matmul(bank[0][:, :], W("l0_w") if first else W("l2_wq"), xnT[:, toks(g, GT)],
                          start=True, stop=True).then_inc(A.q_psum, 1)
                if not first:
                    pe.wait_ge(A.ct_ready, g + 1)
                    pe.matmul(bank[2][:, 0:J * KC], W("l2_wk"), ctxT_of(g)[:, :], start=True, stop=True).then_inc(A.k_psum, 1)
            if not (isinstance(g, int) and g == 0):
                pe.wait_ge(A.exp_ready, g)
                for j in range(J):
                    ins = pe.transpose(bank[4][0:KC, j * P:(j + 1) * P], ebuf[:, j * KC:(j + 1) * KC], ident)
                ins.then_inc(A.pt_psum, 1)
            if g is not G:
                pe.wait_ge(A.q_ready, g + 1)
                if not first:
                    pe.wait_ge(A.k_ready, g + 1)
                for j in range(J):
                    keys = ctxT_sb[:, bass.ds((g * J + j) * KC, KC)] if first else kT[:, j * KC:(j + 1) * KC]
                    ins = pe.matmul(bank[1][:, j * KC:(j + 1) * KC], qT1[:, j * P:(j + 1) * P], keys, start=True, stop=True)
                ins.then_inc(A.s_psum, 1)
            if not (isinstance(g, int) and g == 0):
                pe.wait_ge(A.pt_ready, g)
                if not first:
                    pe.wait_ge(A.v_ready, g)
                elif isinstance(g, int) and g == 1:
                    pe.wait_ge(in_ctx, 16)
                    pe.wait_ge(consts_ready, 2)
                after(pe, A.o_used, g - 1)
                for j in range(J):
                    t = (g - 1) * J + j
                    vals = ctx_sb[0:KC, bass.ds(t * (P + 1), P + 1)] if first else kv[0:KC, j * (P + 1):(j + 1) * (P + 1)]
                    ins = pe.matmul(bank[5 + j // 2][:, (j % 2) * 256:(j % 2) * 256 + P + 1], pT[0:KC, j * P:(j + 1) * P],
                                    vals, start=True, stop=True)
                ins.then_inc(A.o_psum, 1)
            if g is not G and not first:
                after(pe, A.v_ready, g)
                for j in range(J):
                    ins = pe.matmul(bank[3][0:KC, j * P:(j + 1) * P], ctxT_of(g)[:, j * KC:(j + 1) * KC], W("l2_wv"),
                                    start=True, stop=True)
                ins.then_inc(A.v_psum, 1)
            tail()

        def onehead_act(act, A, g, tail):
            first = A is A0
            if g is not G:
                act.wait_ge(A.q_psum, g + 1)
                act.activation(qT1, bank[0][:, :], ACT.Identity, bias=W("l0_b") if first else W("l2_bq")).then_inc(A.q_ready, 1)
                if not first:
                    act.wait_ge(A.k_psum, g + 1)
                    act.activation(kT[:, 0:J * KC], bank[2][:, 0:J * KC], ACT.Identity, bias=W("l2_bk")).then_inc(A.k_ready, 1)
            if not (isinstance(g, int) and g == 0):
                act.wait_ge(A.pt_psum, g)
                act.copy(pT[0:KC, 0:GT], bank[4][0:KC, :]).then_inc(A.pt_ready, 1)
            if g is not G:
                act.wait_ge(A.shift_ready, g + 1)
                act.activation(ebuf[:, 0:J * KC], madd[:, :] if first else tmp[:, 0:J * KC], ACT.Exp,
                               scale=1.0 if first else float(P) ** -0.5).then_inc(A.exp_ready, 1)
            tail()

        def onehead_dve(dve, ch, A, g):
            first = A is A0
            if g is not G:
                dve.wait_ge(A.s_psum, g + 1)
                src = bank[1][:, 0:J * KC]
                if first:
                    ch.link(dve.scalar_tensor_tensor(out=tmp[:, 0:J * KC], in0=unmask_f[:, bass.ds(g * J * KC, J * KC)],
                                                     scalar=NEG0, in1=src, op0=ALU.mult, op1=ALU.add))
                    ch.after()
                    src = tmp[:, 0:J * KC]
                src = src.rearrange("p (j k) -> p j k", j=J)
                ch.link(dve.tensor_reduce(mx[:, 0:J], src, AX.X, ALU.max))
                ch.after()
                dst = (madd[:, :] if first else tmp[:, 0:J * KC]).rearrange("p (j k) -> p j k", j=J)
                dve.tensor_tensor(dst, src, mx[:, 0:J, None].to_broadcast((P, J, KC)), ALU.subtract).then_inc(A.shift_ready, 1)
            if not (isinstance(g, int) and g == 0):
                dve.wait_ge(A.o_psum, g)
                for i in range(2):
                    o = bank[5 + i][:, :].rearrange("p (j d) -> p j d", j=2)
                    ch.link(dve.reciprocal(rs[:, 2 * i:2 * i + 2, None], o[:, :, P:P + 1]))
                ch.after()
                for j in range(J):
                    xt = x_res[:, toks((g - 1) * J + j)]
                    ch.link(dve.scalar_tensor_tensor(out=xt, in0=bank[5 + j // 2][:, (j % 2) * 256:(j % 2) * 256 + P],
                                                     scalar=rs[:, j:j + 1], in1=xt, op0=ALU.mult, op1=ALU.add))
                ch.after()
                dve.sem_inc(A.o_used, 1)
            if g is not G and not first:
                dve.wait_ge(A.v_psum, g + 1)
                vals = kv[0:KC, 0:J * (P + 1)].rearrange("p (j d) -> p j d", j=J)
                ch.link(dve.memset(vals[:, :, P:P + 1], 1.0))
                dve.tensor_tensor(vals[:, :, 0:P], grp(bank[3][0:KC, :]),
                                  R("l2_bv")[0:KC, None, :].to_broadcast((KC, J, P)), ALU.add).then_inc(A.v_ready, 1)
                ch.after()

        def onehead_pool(pool, g):
            if not isinstance(g, int):
                pool.wait_ge(A2.v_psum, g)
            pool.tensor_copy(ctxT_of(g)[:, :], ctxT_sb[:, bass.ds(g * J * KC, J * KC)]).then_inc(A2.ct_ready, 1)

        gl_psum, gl_ready, g_psum = sem("gl_psum"), sem("gl_ready"), sem("g_psum")
        gap_ready, gexp_ready = sem("gap_ready"), sem("gexp_ready")
        h_psum, hT_ready, y_psum, y_used = sem("h_psum"), sem("hT_ready"), sem("y_psum"), sem("y_used")
        cwg_ready, cwt_psum, cwT_ready = sem("cwg_ready"), sem("cwt_psum"), sem("cwT_ready")
        H_BANKS = 4

        class Experts:
            def __init__(s, k, p, fc, func, w, wg, bg, b1, b2, top):
                s.k, s.p, s.fc, s.func, s.w, s.wg, s.bg, s.b1, s.b2, s.top = k, p, fc, func, w, wg, bg, b1, b2, top

            def w1(s, e, c):
                return s.w[:, (e * s.fc + c) * P:(e * s.fc + c + 1) * P]

            def w2(s, e, c):
                at = E * s.fc + e * s.fc + c
                return s.w[:, at * P:(at + 1) * P]

        M0 = Experts(0, 1, 1, ACT.Gelu, f0_sb, "f0_wg", "f0_bg", "f0_b1", "f0_b2", 1)
        M1 = Experts(1, 3, FC, ACT.Gelu, w32_sb, "f1_wr", "f1_br", "f1_b1", "f1_b2", 2)
        M3 = Experts(2, 8, FC, ACT.Relu, w32_sb, "f3_wg", "f3_bg", "f3_b1", "f3_b2", 1)
        split_ready, x_split_ready = sem("split_ready"), sem("x_split_ready")
        x_hi, x_lo = x_half[:, 0:GT], x_half[:, GT:2 * GT]

        def split_dve(dve, ch, M, e):
            w, hi, lo = [t[:, e * F:(e + 1) * F] for t in (M.w, w1_hi, w1_lo)]
            ch.link(dve.tensor_copy(hi, w))
            ch.after()
            dve.tensor_tensor(lo, w, hi.bitcast(F32), ALU.subtract).then_inc(split_ready, 1)

        def x_split_pool(pool, order, M, g):
            pool.wait_ge(xnT_ready, G * M.p + g + 2)
            pool.wait_ge(h_psum, G * E + (M.k - 1) * G * E * FC + g * E * FC)
            x = xnT[:, toks(g, GT)]
            order.link(pool.tensor_copy(x_hi, x))
            order.after()
            pool.tensor_tensor(x_lo, x, x_hi.bitcast(F32), ALU.subtract).then_inc(x_split_ready, 1)
            order.restart()

        HT_BASE = {0: H_BANKS, 1: H_BANKS + G * E, 2: H_BANKS + G * E + G * E * FC}
        YJ = E + 1

        def route_pe(pe, M, g):
            input_ready(pe, M.p, g)
            after(pe, r_ready, G * M.k + g)
            pe.matmul(bank[4][0:E, :], W(M.wg), xnT[:, toks(g, GT)], start=True, stop=True).then_inc(gl_psum, 1)

        def route_back_pe(pe, M, g):
            for j in range(J):
                ins = pe.transpose(bank[4][:, j * E:(j + 1) * E], gT_sb[:, j * P:(j + 1) * P], ident[0:E, 0:E])
            ins.then_inc(g_psum, 1)

        def route_act(act, M, g):
            act.wait_ge(gl_psum, G * M.k + g + 1)
            act.activation(gT_sb[:, :], bank[4][0:E, :], ACT.Identity, bias=W(M.bg, E)).then_inc(gl_ready, 1)

        r_ready = sem("r_ready")

        def route_dve(dve, ch, M, g):
            def te(t):
                return t[:, :].rearrange("p (j e) -> p j e", j=J)

            def wide(v):
                return v[:, :, None].to_broadcast((P, J, E))

            def first_of_greatest(src, hot, top, scratch, at):
                ch.link(dve.tensor_reduce(top[:, :], te(src), AX.X, ALU.max))
                ch.after()
                ch.link(dve.tensor_tensor(te(scratch), te(src), wide(top), ALU.is_ge))
                ch.after()
                ch.link(dve.tensor_tensor(te(scratch), te(scratch), te(rank8), ALU.mult))
                ch.after()
                ch.link(dve.tensor_reduce(at[:, :], te(scratch), AX.X, ALU.max))
                ch.after()
                ch.link(dve.tensor_tensor(te(hot), te(scratch), wide(at), ALU.is_equal))
                ch.after()

            dve.wait_ge(g_psum, G * M.k + g + 1)
            dve.tensor_copy(rt[0][:, :], bank[4][:, 0:J * E]).then_inc(r_ready, 1)
            dve.wait_ge(r_ready, G * M.k + g + 1)
            after(dve, cwt_psum, G * M.k + g)
            if M.top == 1:
                first_of_greatest(rt[0], cw, rv[0], rt[1], rv[1])
            else:
                first_of_greatest(rt[0], rt[2], rv[0], rt[1], rv[1])
                ch.link(dve.scalar_tensor_tensor(out=rt[0][:, :], in0=rt[2][:, :], scalar=NEG3, in1=rt[0][:, :],
                                                 op0=ALU.mult, op1=ALU.add))
                ch.after()
                first_of_greatest(rt[0], rt[3], rv[2], rt[1], rv[1])
                dve.tensor_tensor(rv[2][:, :], rv[2][:, :], rv[0][:, :], ALU.subtract).then_inc(gap_ready, 1)
                dve.wait_ge(gexp_ready, g + 1)
                ch.link(dve.tensor_scalar(rv[0][:, :], rv[3][:, :], 1.0, None, ALU.add))
                ch.after()
                ch.link(dve.reciprocal(rv[0][:, :], rv[0][:, :]))
                ch.after()
                ch.link(dve.tensor_tensor(rv[1][:, :], rv[3][:, :], rv[0][:, :], ALU.mult))
                ch.after()
                ch.link(dve.tensor_tensor(te(rt[2]), te(rt[2]), wide(rv[0]), ALU.mult))
                ch.link(dve.tensor_tensor(te(rt[3]), te(rt[3]), wide(rv[1]), ALU.mult))
                ch.after()
                ch.link(dve.tensor_tensor(cw[:, :], rt[2][:, :], rt[3][:, :], ALU.add))
                ch.after()
            dve.sem_inc(cwg_ready, 1)

        def route_pool(pool, g):
            pool.wait_ge(gap_ready, g + 1)
            pool.tensor_tensor(rv[3][:, :], euler[:, :], rv[2][:, :], ALU.pow).then_inc(gexp_ready, 1)

        def experts_pe(pe, M, g, tail):
            rhs = xnT[:, toks(g, GT)]
            n = E * M.fc

            def hidden(e, some=None):
                halves = M.fc > 1 and not isinstance(g, int)
                if halves and e == 0:
                    pe.wait_ge(x_split_ready, (G - 1) * (M.k - 1) + g)
                    pe.wait_ge(split_ready, E * M.k)
                for c in some or range(M.fc):
                    k = e * M.fc + c
                    if halves:
                        at = (e * M.fc + c) * P
                        pe.wait_ge(hT_ready, HT_BASE[M.k] + g * n + k - H_BANKS + 1)
                        for i, (w, x) in enumerate(((w1_hi, x_hi), (w1_hi, x_lo), (w1_lo, x_hi))):
                            ins = pe.matmul(bank[k % H_BANKS][:, :], w[:, at:at + P], x,
                                            start=(i == 0), stop=(i == 2))
                        ins.then_inc(h_psum, 1)
                        continue
                    pe.wait_ge(hT_ready, HT_BASE[M.k] + g * n + k - H_BANKS + 1)
                    pe.matmul(bank[k % H_BANKS][:, :], M.w1(e, c), rhs, start=True, stop=True).then_inc(h_psum, 1)

            def y_job(i):
                after(pe, y_used, G * YJ * M.k + g * YJ + (i - 1 if i else 0))
                return bank[5 + i % 2]

            def biases():
                y = y_job(E)
                pe.wait_ge(cwT_ready, G * M.k + g + 1)
                for j in range(J):
                    ins = pe.matmul(y[:, j * P:(j + 1) * P], cwT[:, j * P:(j + 1) * P], W(M.b2, E), start=True, stop=True)
                ins.then_inc(y_psum, 1)

            def out(e):
                if M is M0 and e == 0 and isinstance(g, int):
                    pe.wait_ge(A0.o_used, G)
                y = y_job(e)
                pe.wait_ge(hT_ready, HT_BASE[M.k] + g * n + (e + 1) * M.fc)
                for j in range(J):
                    for c in range(M.fc):
                        at = ((e % 2) * M.fc + c) * GT + j * P
                        ins = pe.matmul(y[:, j * P:(j + 1) * P], big[:, at:at + P], M.w2(e, c),
                                        start=(c == 0), stop=(c == M.fc - 1))
                ins.then_inc(y_psum, 1)

            route_pe(pe, M, g)
            hidden(0)
            pe.wait_ge(gl_ready, G * M.k + g + 1)
            hidden(1, [0])
            route_back_pe(pe, M, g)
            if M.fc > 1:
                hidden(1, range(1, M.fc))
            for e in range(E):
                out(e)
                if e + 2 < E:
                    hidden(e + 2)
                if e == 2:
                    tail()
                if e == 3:
                    pe.wait_ge(cwg_ready, G * M.k + g + 1)
                    pe.wait_ge(xnT_ready, G * M.p + G + 1 + (0 if M is M3 else g))
                    for j in range(J):
                        ins = pe.transpose(bank[7][0:E, j * P:(j + 1) * P], cw[:, j * E:(j + 1) * E], ident)
                    ins.then_inc(cwt_psum, 1)
            biases()

        def experts_act(act, M, g, tail):
            n = E * M.fc

            def hidden(e):
                for c in range(M.fc):
                    k = e * M.fc + c
                    act.wait_ge(h_psum, HT_BASE[M.k] - H_BANKS + g * n + k + 1)
                    if c == 0:
                        after(act, y_psum, G * YJ * M.k + g * YJ + (e - 1 if e >= 2 else 0))
                    at = ((e % 2) * M.fc + c) * GT
                    act.activation(big[:, at:at + GT], bank[k % H_BANKS][:, :], M.func,
                                   bias=W(M.b1)[:, k:k + 1]).then_inc(hT_ready, 1)

            route_act(act, M, g)
            hidden(0)
            hidden(1)
            for e in range(2, E):
                hidden(e)
                if e == 4:
                    tail()
                if e == 5:
                    act.wait_ge(cwt_psum, G * M.k + g + 1)
                    act.copy(cwT[:, :], bank[7][0:E, :]).then_inc(cwT_ready, 1)

        def experts_dve(dve, ch, M, g):
            splits = M.fc > 1 and isinstance(g, int)
            if splits:
                dve.wait_ge(in_w32, 16 * M.k)
            route_dve(dve, ch, M, g)
            w = cw[:, :].rearrange("p (j e) -> p j e", j=J)
            for i in range(YJ):
                n = G * YJ * M.k + g * YJ + i + 1
                dve.wait_ge(y_psum, n)
                y = bank[5 + i % 2]
                if i == 0:
                    dve.tensor_tensor(grp(acc[:, :]), grp(y[:, :]), w[:, :, 0:1].to_broadcast((P, J, P)),
                                      ALU.mult).then_inc(y_used, 1)
                    dve.wait_ge(y_used, n)
                elif i == E:
                    dve.tensor_tensor(acc[:, :], y[:, :], acc[:, :], ALU.add).then_inc(y_used, 1)
                    dve.wait_ge(y_used, n)
                else:
                    dve.tensor_tensor(grp(tmp[:, :]), grp(y[:, :]), w[:, :, i:i + 1].to_broadcast((P, J, P)),
                                      ALU.mult).then_inc(y_used, 1)
                    dve.wait_ge(y_used, n)
                    ch.link(dve.tensor_tensor(acc[:, :], acc[:, :], tmp[:, :], ALU.add))
                    ch.after()
                if M is M1 and i == 5:
                    context_dve(dve, ch, g)
                if splits and i < E:
                    split_dve(dve, ch, M, i)
            x_g = x_res[:, toks(g, GT)]
            xl_g = xl_res[:, toks(g, GT)]
            if M is M1:
                ch.link(dve.tensor_tensor(acc[:, :], acc[:, :], xl_g, ALU.add))
                ch.after()
                ln_stats_dve(dve, ch, grp(acc[:, :]), EPS_POST)
                ln_apply_dve(dve, ch, grp(acc[:, :]), grp(tmp[:, :]), LN_BASE[4] + g * LN_PER[4])
                for name, op in (("f1_lnw", ALU.mult), ("f1_lnb", ALU.add)):
                    ch.link(dve.tensor_tensor(grp(tmp[:, :]), grp(tmp[:, :]), R(name)[:, None, :].to_broadcast((P, J, P)), op))
                    ch.after()
                ch.link(dve.tensor_tensor(x_g, x_g, tmp[:, :], ALU.add))
                ch.after()
            else:
                ch.link(dve.tensor_tensor(x_g, x_g, acc[:, :], ALU.add))
                ch.after()
                if M is M3:
                    ch.link(dve.tensor_tensor(x_g, x_g, xl_g, ALU.add))
                    ch.after()

        s_psum, shift_ready, exp_ready, p_ready = sem("s_psum"), sem("shift_ready"), sem("exp_ready"), sem("p_ready")
        pt_psum, pt_ready, o_psum, ot_ready = sem("pt_psum"), sem("pt_ready"), sem("o_psum"), sem("ot_ready")
        w_psum, w_used = sem("w_psum"), sem("w_used")
        ls_o_ready, ls_ot_psum, ls_ot_ready = sem("ls_o_ready"), sem("ls_ot_psum"), sem("ls_ot_ready")
        kx_ready, vx_ready = sem("kx_ready"), sem("vx_ready")
        NJ = 2 * J
        LAST = NJ - 1

        class Heads:
            def __init__(s, k, p, nh, d, nk, scale, wo):
                s.k, s.p, s.nh, s.d, s.nk, s.scale, s.wo = k, p, nh, d, nk, scale, wo
                s.jh = nh // 2
                s.sl = s.jh // 2
                s.oc = nh * d // P
                s.slot = 1 if nk == P else 2
                s.scores_first = nk != P
                s.shift_first = nk == K3

        HL1 = Heads(0, 2, H1, D1, KC, D1 ** -0.5, lambda c: w16_sb[:, 3072 + c * P:3072 + (c + 1) * P])
        HL3 = Heads(1, 6, H3, D3, K3, D3 ** -0.5, lambda c: w16_sb[:, 1536 + c * P:1536 + (c + 1) * P])
        HLS = Heads(2, 7, HS, DS, P, DS ** -0.5, lambda c: W("s_wo"))

        def e_slot(A, i):
            return ebuf[:, (i % 2) * 1024:(i % 2) * 1024 + A.jh * A.nk]

        def u_of(A, u):
            return (u % 2) * A.sl + u // 2 if A is HL3 else u

        def e_head(A, i, u):
            at = (i % 2) * 1024 + u_of(A, u) * A.nk
            return ebuf[:, at:at + A.nk]

        class HeadsPE:
            def __init__(s, pe, A, g):
                s.pe, s.A, s.g = pe, A, g
                s.nb = NJ * (G * A.k + g)
                s.tb = J * (G * A.k + g)

            def scores(s, i):
                pe, A, j, hh = s.pe, s.A, i // 2, i % 2
                b = 2 * (i % 2)
                if A is HL3:
                    after(pe, exp_ready, s.nb + i - 1)
                else:
                    after(pe, shift_ready, s.nb + i - 1)
                if A is HLS:
                    pe.wait_ge(kx_ready, J * s.g + j + 1)
                    for q in range(2):
                        at = (j % 2) * 2048 + (hh * A.jh + q * 4) * P
                        ins = pe.matmul(bank[b + q][:, :], lsQ[:, j * P:(j + 1) * P], big[:, at:at + 4 * P],
                                        start=True, stop=True)
                elif A is HL1:
                    for q in range(A.sl):
                        c = hh * A.sl + q
                        kc = (c * J + j) * 2 * KC
                        ins = pe.matmul(bank[b + q // 2][:, (q % 2) * 2 * KC:(q % 2 + 1) * 2 * KC],
                                        big[:, c * GT + j * P:c * GT + (j + 1) * P], kT[:, kc:kc + 2 * KC],
                                        start=True, stop=True)
                else:
                    for u in range(A.jh):
                        h = hh * A.jh + u
                        a = (h % 2) * 64
                        c = h // 2
                        kc = (c * J + j) * A.nk
                        ins = pe.matmul(bank[b + u % 2][:, (u // 2) * A.nk:(u // 2 + 1) * A.nk],
                                        big[a:a + 64, c * GT + j * P:c * GT + (j + 1) * P], kT[a:a + 64, kc:kc + A.nk],
                                        start=True, stop=True)
                ins.then_inc(s_psum, 1)

            def turn(s, i):
                pe, A = s.pe, s.A
                if A is HLS:
                    pe.wait_ge(exp_ready, s.nb + i + 1)
                else:
                    pe.wait_ge(p_ready, s.nb + i + 1)
                after(pe, pt_ready, s.nb + i)
                for u in range(A.jh):
                    e = e_head(A, i, u)
                    if A is HL3:
                        pe.transpose(bank[4][0:KC, u * P:(u + 1) * P], e[:, 0:KC], ident)
                        ins = pe.transpose(bank[5][:, u * P:(u + 1) * P], e[:, KC:K3], ident)
                    else:
                        ins = pe.transpose(bank[4 + u // 4][0:A.nk, (u % 4) * P:(u % 4 + 1) * P], e, ident)
                ins.then_inc(pt_psum, 1)

            def weigh(s, i):
                pe, A, j, hh = s.pe, s.A, i // 2, i % 2
                slot = (i % 2) * 1024
                pe.wait_ge(pt_ready, s.nb + i + 1)
                if A is HLS:
                    if i % 2 == 0:
                        after(pe, ls_o_ready, J * s.g + j)
                    pe.wait_ge(vx_ready, J * s.g + j + 1)
                    for u in range(A.jh):
                        h = hh * A.jh + u
                        at = ((j % 2) * HS + h) * LSW
                        ins = pe.matmul(bank[6][:, 0:LSW], pT[:, slot + u * P:slot + (u + 1) * P], kv[:, at:at + LSW],
                                        start=(h == 0), stop=(h == HS - 1))
                else:
                    after(pe, ot_ready, s.nb + i)
                    for u in range(A.jh):
                        h = hh * A.jh + u
                        a = (u % 2) * 64
                        out = bank[6][a:a + 64, (u // 2) * P:(u // 2 + 1) * P]
                        at = (j * A.nh + h) * A.d
                        if A is HL3:
                            pe.matmul(out, kv[0:KC, at:at + A.d], pT[0:KC, slot + u * P:slot + (u + 1) * P],
                                      start=True, stop=False)
                            at += J * A.nh * A.d
                            ins = pe.matmul(out, kv[:, at:at + A.d], pT[:, slot + 512 + u * P:slot + 512 + (u + 1) * P],
                                            start=False, stop=True)
                        else:
                            ins = pe.matmul(out, kv[0:KC, at:at + A.d], pT[0:KC, slot + u * P:slot + (u + 1) * P],
                                            start=True, stop=True)
                ins.then_inc(o_psum, 1)

            def tail_done(s):
                s.pe.wait_ge(xnT_ready, G * s.A.p + G + s.g + 1)

            def turn_out(s, t):
                pe = s.pe
                pe.wait_ge(ls_o_ready, J * s.g + t + 1)
                if t == 0:
                    s.tail_done()
                after(pe, w_used, s.tb + t)
                pe.transpose(bank[7][:, P:2 * P], ob[:, :], ident).then_inc(ls_ot_psum, 1)

            def project(s, t):
                pe, A = s.pe, s.A
                if A is HLS:
                    pe.wait_ge(ls_ot_ready, J * s.g + t + 1)
                else:
                    if t == 0:
                        s.tail_done()
                    pe.wait_ge(ot_ready, s.nb + 2 * t + 2)
                    after(pe, w_used, s.tb + t)
                for c in range(A.oc):
                    ins = pe.matmul(bank[7][:, 0:P], oT[:, c * P:(c + 1) * P], A.wo(c), start=(c == 0), stop=(c == A.oc - 1))
                ins.then_inc(w_psum, 1)

            def step(s, i):
                if s.A.scores_first and i + 2 <= LAST:
                    s.scores(i + 2)
                if i <= LAST:
                    s.turn(i)
                if 1 <= i <= NJ:
                    s.weigh(i - 1)
                if not s.A.scores_first and i + 2 <= LAST:
                    s.scores(i + 2)
                if s.A is HLS and i % 2 == 0 and i >= 2:
                    s.turn_out(i // 2 - 1)
                if i % 2 == 1 and i >= 3:
                    s.project(i // 2 - 1)

        class HeadsACT:
            def __init__(s, act, A, g):
                s.act, s.A, s.g = act, A, g
                s.nb = NJ * (G * A.k + g)
                s.tb = J * (G * A.k + g)

            def exps(s, i):
                act, A = s.act, s.A
                act.wait_ge(shift_ready, s.nb + i + 1)
                if A is HL3:
                    for q in range(A.jh):
                        at = (2 * (i % 2) + q // A.sl) * 512 + (q % A.sl) * A.nk
                        m = (i % 2) * 8 + q
                        ins = act.activation(e_slot(A, i)[:, q * A.nk:(q + 1) * A.nk], psum[:, at:at + A.nk], ACT.Exp,
                                             bias=mx[:, m:m + 1], scale=A.scale, accum_out=rs[:, m:m + 1])
                    ins.then_inc(exp_ready, 1)
                    return
                act.activation(e_slot(A, i), e_slot(A, i), ACT.Exp, scale=A.scale).then_inc(exp_ready, 1)

            def turned(s, i):
                act, A = s.act, s.A
                slot = (i % 2) * 1024
                act.wait_ge(pt_psum, s.nb + i + 1)
                after(act, o_psum, s.nb + i - 1)
                if A is HL3:
                    act.copy(pT[0:KC, slot:slot + 512], bank[4][0:KC, :])
                    act.copy(pT[:, slot + 512:slot + 1024], bank[5][:, :]).then_inc(pt_ready, 1)
                else:
                    act.copy(pT[0:A.nk, slot:slot + A.jh * P], psum[0:A.nk, 4 * 512:4 * 512 + A.jh * P]).then_inc(pt_ready, 1)

            def weighed(s, i):
                act, A, t = s.act, s.A, i // 2
                if A is HLS:
                    if i % 2:
                        act.wait_ge(ls_ot_psum, J * s.g + t + 1)
                        after(act, w_psum, s.tb + t)
                        act.copy(oT[:, 0:P], bank[7][:, P:2 * P]).then_inc(ls_ot_ready, 1)
                    return
                act.wait_ge(o_psum, s.nb + i + 1)
                if i % 2 == 0:
                    after(act, w_psum, s.tb + t)
                n = A.jh // 2
                for q in range(n):
                    c = (i % 2) * n + q
                    if A is HL1:
                        ins = act.activation(oT[:, c * P:(c + 1) * P], bank[6][:, q * P:(q + 1) * P], ACT.Identity,
                                             bias=W("l1_bv")[:, c:c + 1])
                    elif q == 0:
                        ins = act.copy(oT[:, c * P:(c + n) * P], bank[6][:, 0:n * P])
                ins.then_inc(ot_ready, 1)

            def step(s, i):
                if i <= LAST:
                    s.turned(i)
                if s.A is not HLS and 1 <= i <= NJ:
                    s.weighed(i - 1)
                if i + 2 <= LAST:
                    s.exps(i + 2)
                if s.A is HLS and i % 2 == 0 and i >= 2:
                    s.weighed(i - 1)

        class HeadsDVE:
            def __init__(s, dve, ch, A, g):
                s.dve, s.ch, s.A, s.g = dve, ch, A, g
                s.nb = NJ * (G * A.k + g)
                s.tb = J * (G * A.k + g)

            def tops(s, i):
                A = s.A
                return mx[:, (i % 2) * 8:(i % 2) * 8 + A.jh].rearrange("p (b s) -> p b s", b=2)

            def shift(s, i):
                dve, ch, A = s.dve, s.ch, s.A
                dve.wait_ge(s_psum, s.nb + i + 1)
                b = 2 * (i % 2) * 512
                sc = psum[:, b:b + 1024].rearrange("p (b r) -> p b r", b=2)[:, :, 0:A.sl * A.nk]
                sc = sc.rearrange("p b (s k) -> p b s k", s=A.sl)
                if A is HL3:
                    m = mask3_f[:, bass.ds((s.g * J + i // 2) * KC, KC)]
                    ch.link(dve.tensor_tensor(sc[:, :, :, 0:KC], sc[:, :, :, 0:KC],
                                              m[:, None, None, :].to_broadcast((P, 2, A.sl, KC)), ALU.add))
                    ch.after()
                top = s.tops(i)
                ch.link(dve.tensor_reduce(top, sc, AX.X, ALU.max))
                ch.after()
                if A is HL3:
                    dve.tensor_scalar(top, top, -A.scale, None, ALU.mult).then_inc(shift_ready, 1)
                    return
                after(dve, pt_psum, s.nb + i - 1)
                dst = e_slot(A, i).rearrange("p (b s k) -> p b s k", b=2, s=A.sl)
                dve.tensor_tensor(dst, sc, top[:, :, :, None].to_broadcast((P, 2, A.sl, A.nk)),
                                  ALU.subtract).then_inc(shift_ready, 1)

            def normalize(s, i):
                dve, ch, A = s.dve, s.ch, s.A
                if A is HLS:
                    return
                dve.wait_ge(exp_ready, s.nb + i + 1)
                e = e_slot(A, i).rearrange("p (h k) -> p h k", h=A.jh)
                r = rs[:, (i % 2) * 8:(i % 2) * 8 + A.jh]
                if A is not HL3:
                    ch.link(dve.tensor_reduce(r, e, AX.X, ALU.add))
                    ch.after()
                ch.link(dve.reciprocal(r, r))
                ch.after()
                dve.tensor_tensor(e, e, r[:, :, None].to_broadcast((P, A.jh, A.nk)), ALU.mult).then_inc(p_ready, 1)

            def output(s, t):
                dve, ch = s.dve, s.ch
                dve.wait_ge(o_psum, s.nb + 2 * t + 2)
                after(dve, ls_ot_psum, J * s.g + t)
                ch.link(dve.reciprocal(rs[:, 0:HS], bank[6][:, P:LSW]))
                ch.after()
                dve.tensor_tensor(ob[:, :].rearrange("p (h d) -> p h d", h=HS), bank[6][:, 0:P].rearrange("p (h d) -> p h d", h=HS),
                                  rs[:, 0:HS, None].to_broadcast((P, HS, DS)), ALU.mult).then_inc(ls_o_ready, 1)

            def add_x(s, t):
                dve, A = s.dve, s.A
                dve.wait_ge(w_psum, s.tb + t + 1)
                x_t = (xl_res if A is HLS else x_res)[:, toks(s.g * J + t)]
                dve.tensor_tensor(x_t, bank[7][:, 0:P], x_t, ALU.add).then_inc(w_used, 1)

            def step(s, i):
                if s.A.shift_first and i + 2 <= LAST:
                    s.shift(i + 2)
                if 2 <= i + 1 <= LAST:
                    s.normalize(i + 1)
                if s.A is HLS and i % 2 == 0 and i >= 2:
                    s.output(i // 2 - 1)
                if not s.A.shift_first and i + 2 <= LAST:
                    s.shift(i + 2)
                if i % 2 == 1 and i >= 3:
                    s.add_x(i // 2 - 1)

        def heads_pe(pe, A, g, tail, front, keys, values):
            for part in range(3):
                front(pe, g, part)
                if not (isinstance(g, int) and g == 0):
                    HeadsPE(pe, A, g - 1).step(LAST + part)
                elif A is HLS:
                    HeadsPE(pe, HL3, G - 1).step(LAST + part)
            keys(pe, g)
            h = HeadsPE(pe, A, g)
            h.scores(0)
            h.scores(1)
            values(pe, g)
            for i in range(LAST):
                h.step(i)
                if i == A.slot:
                    after(pe, w_used, h.tb)
                    tail()

        def heads_act(act, A, g, tail, front, keys, values):
            for part in range(3):
                front(act, g, part)
                if not (isinstance(g, int) and g == 0):
                    HeadsACT(act, A, g - 1).step(LAST + part)
                elif A is HLS:
                    HeadsACT(act, HL3, G - 1).step(LAST + part)
            keys(act, g)
            h = HeadsACT(act, A, g)
            values(act, g, h)
            for i in range(LAST):
                h.step(i)
                if i == A.slot:
                    tail()

        def heads_end(h):
            for i in range(LAST, NJ + 2):
                h.step(i)

        def heads_dve(dve, ch, A, g, tail, l3_ahead):
            h = HeadsDVE(dve, ch, A, g)
            h.shift(0)
            h.shift(1)
            parts = tail()
            if A is HLS:
                ls_spread_dve(dve, g, 0)
            if parts:
                parts[0]()
            h.normalize(0)
            late = A is HLS and len(parts) == 2
            if parts and not late:
                parts[1]()
            h.normalize(1)
            if parts[2:]:
                parts[2]()
            for i in range(NJ + 2):
                if A is HLS and i % 2 == 0 and i // 2 + 1 < J:
                    ls_spread_dve(dve, g, i // 2 + 1)
                if A is HL3 and i == 4:
                    l3_ahead(g)
                h.step(i)
                if i == 0 and late:
                    parts[1]()
            if A is HLS:
                dve.wait_ge(w_used, h.tb + J)
                xl_g = grp(xl_res[:, toks(g, GT)])
                ch.link(dve.tensor_tensor(xl_g, xl_g, R("s_bo")[:, None, :].to_broadcast((P, J, P)), ALU.add))
                ch.after()

        def no_keys(act, g):
            pass

        l1_q_psum, l1_q_ready, l1_k_psum, l1_k_ready = sem("l1_q_psum"), sem("l1_q_ready"), sem("l1_k_psum"), sem("l1_k_ready")
        l1_v_psum, l1_v_ready, l1_ct_ready, l1_zero = sem("l1_v_psum"), sem("l1_v_ready"), sem("l1_ct_ready"), sem("l1_zero")
        NV = 2 * J

        L1_PARTS = [range(0, 4), range(4, 6), range(6, C1)]
        L3_PARTS = [range(0, 2), range(2, 3), range(3, C3)]

        def l1_front_pe(pe, g, part):
            if part == 0:
                input_ready(pe, 2, g)
                pe.wait_ge(l1_ct_ready, g + 1)
                after(pe, shift_ready, NJ * g)
            for c in L1_PARTS[part]:
                after(pe, l1_q_ready, g * C1 + c - 1)
                pe.matmul(bank[c % 2][:, :], w16_sb[:, c * P:(c + 1) * P], xnT[:, toks(g, GT)],
                          start=True, stop=True).then_inc(l1_q_psum, 1)
                after(pe, l1_k_ready, g * C1 + c - 1)
                pe.matmul(bank[2 + c % 2][:, 0:J * KC], w16_sb[:, 1024 + c * P:1024 + (c + 1) * P], ctxTg[:, :],
                          start=True, stop=True).then_inc(l1_k_psum, 1)

        def l1_keys_pe(pe, g):
            pe.wait_ge(l1_q_ready, (g + 1) * C1)
            pe.wait_ge(l1_k_ready, (g + 1) * C1)

        def l1_values_pe(pe, g):
            after(pe, pt_ready, NJ * g)
            if isinstance(g, int):
                pe.wait_ge(y_used, G * YJ)
            for i in range(NV):
                after(pe, l1_v_ready, g * NV + i - 1)
                pe.matmul(bank[4 + i % 2][0:KC, :], ctxTg[:, (i // 2) * KC:(i // 2 + 1) * KC],
                          w16_sb[:, 2048 + (i % 2) * 512:2048 + (i % 2 + 1) * 512],
                          start=True, stop=True).then_inc(l1_v_psum, 1)
            pe.wait_ge(l1_v_ready, (g + 1) * NV)

        def l1_front_act(act, g, part):
            if part == 0 and isinstance(g, int):
                act.wait_ge(l1_zero, 1)
            for c in L1_PARTS[part]:
                act.wait_ge(l1_q_psum, g * C1 + c + 1)
                act.activation(big[:, c * GT:(c + 1) * GT], bank[c % 2][:, :], ACT.Identity,
                               bias=W("l1_bq")[:, c:c + 1]).then_inc(l1_q_ready, 1)
                act.wait_ge(l1_k_psum, g * C1 + c + 1)
                dst = kT[:, c * J * 2 * KC:(c + 1) * J * 2 * KC].rearrange("p (j h k) -> p j h k", j=J, h=2)
                for h in range(2):
                    a = 64 * h
                    ins = act.activation(dst[a:a + 64, :, h, :], bank[2 + c % 2][a:a + 64, 0:J * KC].rearrange("p (j k) -> p j k", j=J),
                                         ACT.Identity, bias=W("l1_bk")[a:a + 64, c:c + 1])
                ins.then_inc(l1_k_ready, 1)

        def l1_values_act(act, g, h):
            for i in range(NV):
                if i == NV // 2 - 1:
                    h.exps(0)
                if i == NV - 2:
                    h.exps(1)
                act.wait_ge(l1_v_psum, g * NV + i + 1)
                act.copy(kv[0:KC, i * 512:(i + 1) * 512], bank[4 + i % 2][0:KC, :]).then_inc(l1_v_ready, 1)

        def l1_front_pool(pool, g):
            after(pool, l1_v_psum, g * NV)
            pool.tensor_copy(ctxTg[:, :], ctxT_sb[:, bass.ds(g * J * KC, J * KC)]).then_inc(l1_ct_ready, 1)

        lr_p_psum, lr_p_ready, lr_h_psum, lr_h_ready = sem("lr_p_psum"), sem("lr_p_ready"), sem("lr_h_psum"), sem("lr_h_ready")
        lr_o_used = sem("lr_o_used")
        lr_q_psum, lr_q_ready, lr_o_psum = sem("lr_q_psum"), sem("lr_q_ready"), sem("lr_o_psum")

        def lowrank_pe(pe, g, tail):
            if g is not G:
                input_ready(pe, 5, g)
                pe.matmul(bank[0][0:RANK, :], W("f2_u1"), xnT[:, toks(g, GT)], start=True, stop=True).then_inc(lr_p_psum, 1)
            if not (isinstance(g, int) and g == 0):
                if isinstance(g, int) and g == 1:
                    pe.wait_ge(A2.o_used, G)
                pe.wait_ge(lr_h_ready, g * FC)
                for c in range(FC):
                    ins = pe.matmul(bank[5][0:RANK, :], W("f2_u2")[:, c * RANK:(c + 1) * RANK], big[:, c * GT:(c + 1) * GT],
                                    start=(c == 0), stop=(c == FC - 1))
                ins.then_inc(lr_q_psum, 1)
            if g is not G:
                pe.wait_ge(lr_p_ready, g + 1)
                for c in range(FC):
                    pe.matmul(bank[1 + c][:, :], W("f2_v1", RANK)[:, c * P:(c + 1) * P], kT[0:RANK, 0:GT],
                              start=True, stop=True).then_inc(lr_h_psum, 1)
            if not (isinstance(g, int) and g == 0):
                pe.wait_ge(lr_q_ready, g)
                after(pe, lr_o_used, g - 1)
                for j in range(J):
                    ins = pe.matmul(bank[6][:, j * P:(j + 1) * P], kT[0:RANK, GT + j * P:GT + (j + 1) * P], W("f2_v2", RANK),
                                    start=True, stop=True)
                ins.then_inc(lr_o_psum, 1)
            tail()

        def lowrank_act(act, g, tail):
            if g is not G:
                act.wait_ge(lr_p_psum, g + 1)
                act.copy(kT[0:RANK, 0:GT], bank[0][0:RANK, :]).then_inc(lr_p_ready, 1)
            if not (isinstance(g, int) and g == 0):
                act.wait_ge(lr_q_psum, g)
                act.copy(kT[0:RANK, GT:2 * GT], bank[5][0:RANK, :]).then_inc(lr_q_ready, 1)
            if g is not G:
                for c in range(FC):
                    act.wait_ge(lr_h_psum, g * FC + c + 1)
                    act.activation(big[:, c * GT:(c + 1) * GT], bank[1 + c][:, :], ACT.Gelu_apprx_tanh,
                                   bias=W("f2_b1")[:, c:c + 1]).then_inc(lr_h_ready, 1)
            tail()

        def lowrank_dve(dve, ch, g):
            x_g = x_res[:, toks(g, GT)]
            dve.wait_ge(lr_o_psum, g + 1)
            dve.tensor_tensor(x_g, bank[6][:, :], x_g, ALU.add).then_inc(lr_o_used, 1)
            dve.wait_ge(lr_o_used, g + 1)
            ch.link(dve.tensor_tensor(grp(x_g), grp(x_g), R("f2_b2")[:, None, :].to_broadcast((P, J, P)), ALU.add))
            ch.after()

        l3_lg_ready, l3_cn_ready, l3_cn_psum, l3_ct_ready = sem("l3_lg_ready"), sem("l3_cn_ready"), sem("l3_cn_psum"), sem("l3_ct_ready")
        l3_q_psum, l3_q_ready, l3_k_psum, l3_k_ready = sem("l3_q_psum"), sem("l3_q_ready"), sem("l3_k_psum"), sem("l3_k_ready")
        l3_v_psum, l3_v_ready = sem("l3_v_psum"), sem("l3_v_ready")
        latG = big[:, 4 * GT:5 * GT]
        NK3 = 2 * C3

        def context_dve(dve, ch, g):
            src = ctx_sb[0:KC, bass.ds(g * J * (P + 1), J * (P + 1))].rearrange("p (j d) -> p j d", j=J)
            for j in range(J):
                ch.link(dve.bn_stats(st[0:KC, j, :], src[:, j, 0:P]))
            ch.after()
            for j in range(J):
                ch.link(dve.bn_aggr(mv[0:KC, j, :], st[0:KC, j, :]))
            ch.after()
            dve.tensor_scalar(ve[:, :], mv[:, :, 1], EPS, None, ALU.add).then_inc(cvar_ready, 1)
            dve.wait_ge(crstd_ready, g + 1)
            for j in range(J):
                ch.link(dve.tensor_scalar(src[:, j, 0:P], src[:, j, 0:P], mv[0:KC, j, 0:1], rstd[0:KC, j:j + 1],
                                          ALU.subtract, ALU.mult))
            ch.after()

        def l3_context_dve(dve, g):
            src = ctx_sb[0:KC, bass.ds(g * J * (P + 1), J * (P + 1))].rearrange("p (j d) -> p j d", j=J)
            dve.tensor_copy(grp(tmp[0:KC, :]), src[:, :, 0:P]).then_inc(l3_cn_ready, 1)

        def l3_gate_dve(dve, g):
            dve.wait_ge(xnT_ready, G * 6 + g + 2)
            after(dve, l3_v_psum, g * 2 * J)
            dve.tensor_scalar(latG, xnT[:, toks(g, GT)], W("l3_gate"), None, ALU.mult).then_inc(l3_lg_ready, 1)

        cvar_ready, crstd_ready = sem("cvar_ready"), sem("crstd_ready")

        def context_pool(pool, g):
            pool.wait_ge(cvar_ready, g + 1)
            pool.tensor_tensor(rstd[:, :], ve[:, :], mhalf[:, :], ALU.pow).then_inc(crstd_ready, 1)

        def l3_front_pe(pe, g, part):
            if part == 0:
                input_ready(pe, 6, g)
                after(pe, exp_ready, NJ * (G + g))
            for c in L3_PARTS[part]:
                pe.matmul(bank[c][:, :], w16_sb[:, c * P:(c + 1) * P], xnT[:, toks(g, GT)],
                          start=True, stop=True).then_inc(l3_q_psum, 1)

        def l3_keys_pe(pe, g):
            after(pe, pt_ready, NJ * (G + g))
            pe.wait_ge(l3_cn_ready, g + 1)
            for j in range(J):
                ins = pe.transpose(bank[4][:, j * KC:(j + 1) * KC], tmp[0:KC, j * P:(j + 1) * P], ident[0:KC, 0:KC])
            ins.then_inc(l3_cn_psum, 1)
            pe.wait_ge(l3_lg_ready, g + 1)
            pe.wait_ge(l3_q_ready, (g + 1) * C3)
            for c in range(C3):
                w = w16_sb[:, 512 + c * P:512 + (c + 1) * P]
                for half, n in enumerate((GT, J * KC)):
                    if half and c == 0:
                        pe.wait_ge(l3_ct_ready, g + 1)
                    if c >= 2:
                        pe.wait_ge(l3_k_ready, g * NK3 + 2 * c + half - 3)
                    pe.matmul(bank[(2 * c + half) % 4][:, 0:n], w, ctxTg[:, :] if half else latG,
                              start=True, stop=True).then_inc(l3_k_psum, 1)
            pe.wait_ge(l3_k_ready, (g + 1) * NK3)

        def l3_values_pe(pe, g):
            for i in range(2 * J):
                if i >= 2:
                    pe.wait_ge(l3_v_ready, g * 2 * J + i - 1)
                j = i // 2
                wv = w16_sb[:, 1024:1536]
                if i % 2 == 0:
                    ins = pe.matmul(bank[4][0:KC, :], ctxTg[:, j * KC:(j + 1) * KC], wv, start=True, stop=True)
                else:
                    ins = pe.matmul(bank[5][:, :], latG[:, j * P:(j + 1) * P], wv, start=True, stop=True)
                ins.then_inc(l3_v_psum, 1)
            pe.wait_ge(l3_v_ready, (g + 1) * 2 * J)

        def l3_front_act(act, g, part):
            for c in L3_PARTS[part]:
                act.wait_ge(l3_q_psum, g * C3 + c + 1)
                act.copy(big[:, c * GT:(c + 1) * GT], bank[c][:, :]).then_inc(l3_q_ready, 1)

        def l3_keys_act(act, g):
            act.wait_ge(l3_cn_psum, g + 1)
            act.activation(ctxTg[:, :], bank[4][:, 0:J * KC], ACT.Identity, bias=W("l3_bm"), scale=W("l3_gm")).then_inc(l3_ct_ready, 1)
            for c in range(C3):
                dst = kT[:, c * J * K3:(c + 1) * J * K3].rearrange("p (j k) -> p j k", j=J)
                for half, (a, n) in enumerate(((KC, P), (0, KC))):
                    act.wait_ge(l3_k_psum, g * NK3 + 2 * c + half + 1)
                    act.copy(dst[:, :, a:a + n],
                             bank[(2 * c + half) % 4][:, 0:J * n].rearrange("p (j k) -> p j k", j=J)).then_inc(l3_k_ready, 1)

        def l3_values_act(act, g, h):
            for i in range(2 * J):
                if i == J - 1:
                    h.exps(0)
                if i == 2 * J - 2:
                    h.exps(1)
                act.wait_ge(l3_v_psum, g * 2 * J + i + 1)
                at = (i // 2) * 512 + (i % 2) * J * 512
                if i % 2 == 0:
                    act.copy(kv[0:KC, at:at + 512], bank[4][0:KC, :]).then_inc(l3_v_ready, 1)
                else:
                    act.copy(kv[:, at:at + 512], bank[5][:, :]).then_inc(l3_v_ready, 1)

        ls_h_ready, ls_q_psum, ls_q_ready, ls_k_psum, ls_k_ready = [sem("ls_" + n) for n in
                                                                    ("h_ready", "q_psum", "q_ready", "k_psum", "k_ready")]
        lsK, lsQ, lsH = [kT[:, C3 * J * K3 + i * GT:C3 * J * K3 + (i + 1) * GT] for i in range(3)]
        ls_v_psum, ls_v_used, ls_zero = sem("ls_v_psum"), sem("ls_v_used"), sem("ls_zero")

        def ls_front_pool(pool, g):
            pool.wait_ge(xnT_ready, G * 7 + g + 2)
            after(pool, ls_v_psum, g)
            pool.tensor_copy(lsH, xnT[:, toks(g, GT)]).then_inc(ls_h_ready, 1)
            pool.wait_ge(ls_k_ready, g + 1)

        def ls_zero_pool(pool):
            pool.wait_ge(o_psum, NJ * 2 * G)
            pool.memset(kv[:, :], 0.0).then_inc(ls_zero, 1)
            pool.wait_ge(ls_zero, 1)
            ones = bass.AP(kv[:, :].tensor, kv[:, :].offset + P, [list(kv[:, :].ap[0]), [HS * LSW, 2], [LSW + 1, HS]])
            pool.memset(ones, 1.0).then_inc(ls_zero, 1)

        def ls_kx_pool(pool, g, tiles):
            for j in tiles:
                pool.wait_ge(s_psum, NJ * 2 * G if isinstance(g, int) and j < 2 else NJ * (2 * G + g) + 2 * (j - 1))
                dst = big[:, (j % 2) * 2048:(j % 2 + 1) * 2048].rearrange("p (h k) -> p h k", h=HS)
                pool.tensor_tensor(dst, lsK[:, None, j * P:(j + 1) * P].to_broadcast((P, HS, P)),
                                   W("headmask")[:, :, None].to_broadcast((P, HS, P)), ALU.mult).then_inc(kx_ready, 1)

        def ls_front_pe(pe, g, part):
            if part:
                return
            rhs = xnT[:, toks(g, GT)]
            input_ready(pe, 7, g)
            after(pe, shift_ready, NJ * (2 * G + g))
            pe.matmul(bank[0][:, :], W("s_wk"), rhs, start=True, stop=True).then_inc(ls_k_psum, 1)
            pe.matmul(bank[1][:, :], W("s_wq"), rhs, start=True, stop=True).then_inc(ls_q_psum, 1)

        def ls_keys_pe(pe, g):
            pe.wait_ge(ls_q_ready, g + 1)
            pe.wait_ge(ls_k_ready, g + 1)

        def ls_values_pe(pe, g):
            pe.wait_ge(pt_ready, NJ * (2 * G + g))
            pe.wait_ge(ls_h_ready, g + 1)
            after(pe, ls_v_used, g)
            for j in range(J):
                ins = pe.matmul(bank[5][:, j * P:(j + 1) * P], lsH[:, j * P:(j + 1) * P], W("s_wv"),
                                start=True, stop=True)
            ins.then_inc(ls_v_psum, 1)
            pe.wait_ge(ls_v_used, g + 1)

        def ls_front_act(act, g, part):
            if part:
                return
            act.wait_ge(ls_k_psum, g + 1)
            after(act, kx_ready, J * g)
            act.activation(lsK, bank[0][:, :], ACT.Identity, bias=W("s_bk")).then_inc(ls_k_ready, 1)
            act.wait_ge(ls_q_psum, g + 1)
            act.activation(lsQ, bank[1][:, :], ACT.Identity, bias=W("s_bq")).then_inc(ls_q_ready, 1)

        def ls_values_act(act, g, h):
            act.wait_ge(ls_v_psum, g + 1)
            after(act, vx_ready, J * g)
            act.copy(vg[:, :], bank[5][:, :]).then_inc(ls_v_used, 1)
            h.exps(0)
            h.exps(1)

        def ls_spread_dve(dve, g, j):
            if j == 0:
                dve.wait_ge(ls_v_used, g + 1)
                if isinstance(g, int):
                    dve.wait_ge(ls_zero, 2)
            after(dve, o_psum, NJ * (2 * G + g) + 2 * (j - 1))
            b = (j % 2) * HS * LSW
            dst = kv[:, b:b + HS * LSW]
            dst = spread(dst)
            dve.tensor_tensor(dst, vg[:, j * P:(j + 1) * P].rearrange("p (h d) -> p h d", h=HS),
                              R("s_bv").rearrange("p (h d) -> p h d", h=HS), ALU.add).then_inc(vx_ready, 1)

        def spread(slot):
            pitch = LSW + DS
            return bass.AP(slot.tensor, slot.offset, [list(slot.ap[0]), [pitch, HS], [1, DS]])

        def by_tile(t):
            return t.rearrange("p (t d) -> p t d", t=T)

        @block.sync
        def _(sp):
            for q in range(G):
                sp.dma_start(by_tile(x_res[:, :])[:, q * J:(q + 1) * J, :],
                             x_d[q * J:(q + 1) * J].rearrange("t p d -> p t d")).then_inc(in_x[q], 16)
                if q == 0:
                    sp.dma_start(by_tile(mask0_sb[:, :]), mask0_d.rearrange("t p k -> p t k")).then_inc(in_masks, 16)
            sp.dma_start(small[:, N_FIRST:], small_d[:, N_FIRST:]).then_inc(in_rest, 16)
            sp.dma_start(rows[:, :], rows_d.to_broadcast((P, N_ROWS))).then_inc(in_rows, 16)
            sp.dma_start(f0_sb[:, :], f0_d).then_inc(in_f0, 16)
            sp.dma_start(mask3_sb[:, :], mask3_d.to_broadcast((P, T * KC))).then_inc(in_mask3, 16)
            sp.dma_start(w16_sb[:, :], l1_d).then_inc(in_w16, 16)
            sp.dma_start(w32_sb[:, :], f1_d).then_inc(in_w32, 16)
            sp.wait_ge(y_psum, 2 * G * YJ)
            sp.dma_start(w16_sb[:, 0:2048], l3_d).then_inc(in_w16, 16)
            sp.dma_start(w32_sb[:, :], f3_d).then_inc(in_w32, 16)
            for q in range(G):
                sp.wait_ge(x_final, q + 1)
                sp.dma_start(out_d[q * J:(q + 1) * J].rearrange("t p d -> p t d"),
                             by_tile(x_res[:, :])[:, q * J:(q + 1) * J, :]).then_inc(out_done, 16)
            sp.wait_ge(out_done, 16 * G)

        def groups(eng, body):
            body(0)
            with eng.Fori(1, G) as g:
                body(g)

        @block.gpsimd
        def _(pool):
            order = Chain(pool, pool_order)
            pool.memset(mhalf[:, :], -0.5)
            pool.memset(euler[:, :], float(np.exp(1.0)))
            for e in range(E):
                pool.memset(rank8[:, :].rearrange("p (t e) -> p t e", t=J)[:, :, e:e + 1], float(E - e))
            pool.memset(by_tile(ctx_sb[:, :])[:, :, P:P + 1], 1.0).then_inc(consts_ready, 1)
            pool.memset(mv[:, :, :], 1.0).then_inc(consts_ready, 1)
            pool.wait_ge(consts_ready, 2)
            for g in range(G):
                tail_pool(pool, 0, g)
            pool.wait_ge(in_masks, 16)
            pool.tensor_scalar(unmask_f, mask0_sb[:, :], -1.0, 1.0, ALU.mult, ALU.add).then_inc(madd_ready, 1)
            pool.wait_ge(in_mask3, 16)
            pool.tensor_scalar(mask3_f[:, :], mask3_sb[:, :], NEG3, None, ALU.mult).then_inc(madd_ready, 1)
            pool.memset(kT[:, :], 0.0).then_inc(l1_zero, 1)

            def ahead(p, front):
                if p == 3:
                    front(pool, 1)
                with pool.Fori(0, G - 2) as g:
                    if p == 3:
                        tail_pool(pool, p, g)
                    front(pool, g + 2)
                    if p != 3:
                        tail_pool(pool, p, g)
                tail_pool(pool, p, G - 2)
                tail_pool(pool, p, G - 1)

            def ls_pool(pool):
                ls_front_pool(pool, 0)
                ls_kx_pool(pool, 0, range(2))
                ls_zero_pool(pool)
                tail_pool(pool, 7, G - 1)
                ls_kx_pool(pool, 0, range(2, J))
                with pool.Fori(1, G) as g:
                    ls_front_pool(pool, g)
                    ls_kx_pool(pool, g, range(2))
                    tail_pool(pool, 8, g - 1)
                    ls_kx_pool(pool, g, range(2, J))
                tail_pool(pool, 8, G - 1)

            pool.wait_ge(in_ctxT, 16)
            l1_front_pool(pool, 0)
            groups(pool, lambda g: tail_pool(pool, 1, g))
            groups(pool, lambda g: tail_pool(pool, 2, g))
            ahead(3, l1_front_pool)
            pool.wait_ge(l1_v_psum, G * NV)
            onehead_pool(pool, 0)
            onehead_pool(pool, 1)
            route_pool(pool, 0)
            context_pool(pool, 0)
            x_split_pool(pool, order, M1, 1)
            tail_pool(pool, 4, 0)
            with pool.Fori(1, G - 1) as g:
                route_pool(pool, g)
                context_pool(pool, g)
                x_split_pool(pool, order, M1, g + 1)
                tail_pool(pool, 4, g)
            route_pool(pool, G - 1)
            context_pool(pool, G - 1)
            tail_pool(pool, 4, G - 1)
            ahead(5, onehead_pool)
            groups(pool, lambda g: tail_pool(pool, 6, g))
            tail_pool(pool, 7, 0)
            with pool.Fori(1, G - 1) as g:
                tail_pool(pool, 7, g)
            ls_pool(pool)
            with pool.Fori(1, G) as g:
                x_split_pool(pool, order, M3, g)

        @block.vector
        def _(dve):
            ch = Chain(dve, dve_order)
            dve.wait_ge(consts_ready, 2)
            for g in range(G):
                dve.wait_ge(in_x[g], 16)
                tail_dve(dve, ch, 0, g)
            ch.restart()
            dve.wait_ge(madd_ready, 1)

            def phase(p, body):
                def whole(g):
                    body(g)
                    if p < 9:
                        tail_dve(dve, ch, p, g)
                    ch.restart()
                groups(dve, whole)

            def phase_behind(p, body):
                body(0)
                ch.restart()
                with dve.Fori(1, G) as g:
                    body(g)
                    tail_dve(dve, ch, p, g - 1)
                    ch.restart()
                body(G)
                tail_dve(dve, ch, p, G - 1)
                ch.restart()

            def last(g):
                experts_dve(dve, ch, M3, g)
                dve.sem_inc(x_final, 1)

            def phase_heads(p, A, pending=None):
                def none():
                    return []

                def tail(g):
                    if A is not HLS:
                        dve.wait_ge(w_used, J * (G * A.k + g + 1))
                    return tail_parts_dve(dve, ch, p, g)

                def ahead(g):
                    l3_gate_dve(dve, g + 1)
                    l3_context_dve(dve, g + 1)

                def nothing_ahead(g):
                    pass

                heads_dve(dve, ch, A, 0, pending or none, ahead)
                ch.restart()
                with dve.Fori(1, G - 1) as g:
                    heads_dve(dve, ch, A, g, lambda: tail(g - 1), ahead)
                    ch.restart()
                heads_dve(dve, ch, A, G - 1, lambda: tail(G - 2), nothing_ahead)
                if A is HL3:
                    ch.restart()
                    return lambda: tail(G - 1)
                for part in tail(G - 1):
                    part()
                ch.restart()

            phase_behind(1, lambda g: onehead_dve(dve, ch, A0, g))
            phase(2, lambda g: experts_dve(dve, ch, M0, g))
            phase_heads(3, HL1)
            dve.wait_ge(in_rows, 16)
            phase(4, lambda g: experts_dve(dve, ch, M1, g))
            phase_behind(5, lambda g: onehead_dve(dve, ch, A2, g))
            lowrank_dve(dve, ch, 0)
            tail_dve(dve, ch, 6, 0)
            ch.restart()
            with dve.Fori(1, G - 1) as g:
                lowrank_dve(dve, ch, g)
                tail_dve(dve, ch, 6, g)
                ch.restart()
            lowrank_dve(dve, ch, G - 1)
            l3_gate_dve(dve, 0)
            l3_context_dve(dve, 0)
            tail_dve(dve, ch, 6, G - 1)
            ch.restart()
            dve.wait_ge(madd_ready, 2)
            phase_heads(8, HLS, phase_heads(7, HL3))
            phase(9, last)

        def late_tails(eng, tail_of, pending, p, body, behind):

            def tail(g):
                return lambda: tail_of(eng, p, g)

            def none():
                pass

            if behind:
                body(0, none)
                body(1, pending)
                with eng.Fori(2, G) as g:
                    body(g, tail(g - 2))
                body(G, tail(G - 2))
                return tail(G - 1)
            body(0, pending)
            with eng.Fori(1, G) as g:
                body(g, tail(g - 1))
            return tail(G - 1)

        @block.scalar
        def _(act):
            act.dma_start(small[:, 0:N_FIRST], small_d[:, 0:N_FIRST]).then_inc(in_small, 16)
            act.dma_start(ctxT_sb[:, :], ctxT_d).then_inc(in_ctxT, 16)
            act.dma_start(by_tile(ctx_sb[:, :])[:, :, 0:P], ctx_d.rearrange("t k d -> k t d")).then_inc(in_ctx, 16)
            act.sem_inc(xnT_ready, 1)
            act.sem_inc(hT_ready, H_BANKS)
            act.wait_ge(in_small, 16)
            for g in range(G - 1):
                tail_act(act, 0, g)

            def heads(A, front, keys, values):
                return lambda g, tail: heads_act(act, A, g, tail, front, keys, values)

            def run(pending, p, body, behind=False, ends=None):
                pending = late_tails(act, tail_act, pending, p, body, behind)
                if ends:
                    ends()
                return pending

            t = lambda: tail_act(act, 0, G - 1)
            t = run(t, 1, lambda g, tail: onehead_act(act, A0, g, tail), True)
            act.wait_ge(in_rest, 16)
            t = run(t, 2, lambda g, tail: experts_act(act, M0, g, tail))
            t = run(t, 3, heads(HL1, l1_front_act, no_keys, l1_values_act), ends=lambda: heads_end(HeadsACT(act, HL1, G - 1)))
            t = run(t, 4, lambda g, tail: experts_act(act, M1, g, tail))
            t = run(t, 5, lambda g, tail: onehead_act(act, A2, g, tail), True)
            t = run(t, 6, lambda g, tail: lowrank_act(act, g, tail), True)
            t = run(t, 7, heads(HL3, l3_front_act, l3_keys_act, l3_values_act))
            t = run(t, 8, heads(HLS, ls_front_act, no_keys, ls_values_act), ends=lambda: heads_end(HeadsACT(act, HLS, G - 1)))
            t = run(t, 9, lambda g, tail: experts_act(act, M3, g, tail if isinstance(g, int) else lambda: None))

        @block.tensor
        def _(pe):
            pe.sem_inc(xnt_psum, 1)
            pe.wait_ge(in_small, 16)
            for g in range(G - 1):
                tail_pe(pe, 0, g)
            pe.wait_ge(in_ctxT, 16)

            def heads(A, front, keys, values):
                return lambda g, tail: heads_pe(pe, A, g, tail, front, keys, values)

            def run(pending, p, body, behind=False, ends=None, needs=()):
                for semaphore, value in needs:
                    pe.wait_ge(semaphore, value)
                pending = late_tails(pe, tail_pe, pending, p, body, behind)
                if ends:
                    ends()
                return pending

            t = lambda: tail_pe(pe, 0, G - 1)
            t = run(t, 1, lambda g, tail: onehead_pe(pe, A0, g, tail), True)
            t = run(t, 2, lambda g, tail: experts_pe(pe, M0, g, tail), needs=[(in_rest, 16), (in_f0, 16)])
            t = run(t, 3, heads(HL1, l1_front_pe, l1_keys_pe, l1_values_pe), ends=lambda: heads_end(HeadsPE(pe, HL1, G - 1)), needs=[(in_w16, 16)])
            t = run(t, 4, lambda g, tail: experts_pe(pe, M1, g, tail), needs=[(in_w32, 16)])
            t = run(t, 5, lambda g, tail: onehead_pe(pe, A2, g, tail), True)
            t = run(t, 6, lambda g, tail: lowrank_pe(pe, g, tail), True)
            t = run(t, 7, heads(HL3, l3_front_pe, l3_keys_pe, l3_values_pe), needs=[(in_w16, 32)])
            t = run(t, 8, heads(HLS, ls_front_pe, ls_keys_pe, ls_values_pe), ends=lambda: heads_end(HeadsPE(pe, HLS, G - 1)))
            t = run(t, 9, lambda g, tail: experts_pe(pe, M3, g, tail if isinstance(g, int) else lambda: None), needs=[(in_w32, 32)])


def kernel(**inputs):
    import concourse.bacc as bacc
    from concourse.bass_utils import run_bass_kernel_spmd

    a = {k: np.asarray(v) for k, v in inputs.items()}

    def pad(m):
        m = m.reshape(m.shape[0], -1)
        return np.concatenate([m, np.zeros((P - m.shape[0], m.shape[1]), m.dtype)], 0)

    def chunks(v):
        return v.reshape(-1, P).T

    head = np.zeros((P, HS), np.float32)
    head[np.arange(P), np.arange(P) // DS] = 1.0
    pieces = {
        "ident": np.eye(P, dtype=np.float32), "headmask": head,
        "l0_w": a["L0_xattn_W"].T, "l0_b": a["L0_xattn_b"][:, None],
        "f0_wg": a["L0_ffn_Wg"], "f0_bg": a["L0_ffn_bg"][:, None], "f0_b1": a["L0_ffn_b1"].T, "f0_b2": a["L0_ffn_b2"],
        "l1_bq": chunks(a["L1_xattn_bq"]), "l1_bk": chunks(a["L1_xattn_bk"]), "l1_bv": chunks(a["L1_xattn_bv"]),
        "f1_wr": a["L1_ffn_Wr"].T, "f1_br": a["L1_ffn_br"][:, None], "f1_b1": chunks(a["L1_ffn_b1"].reshape(-1)),
        "f1_b2": a["L1_ffn_b2"],
        "l2_wq": a["L2_xattn_Wq"].T, "l2_bq": a["L2_xattn_bq"][:, None], "l2_wk": a["L2_xattn_Wk"].T,
        "l2_bk": a["L2_xattn_bk"][:, None], "l2_wv": a["L2_xattn_Wv"].T,
        "f2_u1": a["L2_ffn_U1"], "f2_v1": a["L2_ffn_V1"], "f2_b1": chunks(a["L2_ffn_b1"]),
        "f2_u2": a["L2_ffn_U2"].reshape(FC, P, RANK).transpose(1, 0, 2), "f2_v2": a["L2_ffn_V2"],
        "l3_gm": a["L3_xattn_gamma_media"][:, None], "l3_bm": a["L3_xattn_beta_media"][:, None],
        "l3_gl": a["L3_xattn_gamma_lat"][:, None], "l3_bl": a["L3_xattn_beta_lat"][:, None],
        "l3_gate": np.repeat(a["L3_xattn_kv_gate"].reshape(1, 1), P, 0),
        "s_g1": a["L3_ffn_ln1_g"][:, None], "s_b1": a["L3_ffn_ln1_b"][:, None],
        "s_g2": a["L3_ffn_ln2_g"][:, None], "s_b2": a["L3_ffn_ln2_b"][:, None],
        "s_wq": a["L3_ffn_wq"], "s_bq": a["L3_ffn_bq"][:, None], "s_wk": a["L3_ffn_wk"], "s_bk": a["L3_ffn_bk"][:, None],
        "s_wv": a["L3_ffn_wv"], "s_wo": a["L3_ffn_wo"],
        "f3_wg": a["L3_ffn_gate_w"], "f3_bg": a["L3_ffn_gate_b"][:, None], "f3_b1": chunks(a["L3_ffn_b1"].reshape(-1)),
        "f3_b2": a["L3_ffn_b2"],
    }
    small = np.concatenate([pad(pieces[name]) for name, _ in W_SMALL], 1)
    rows = np.concatenate([a[k].reshape(1, -1) for k in ("L1_ffn_ln_w", "L1_ffn_ln_b", "L2_xattn_bv",
                                                         "L2_ffn_b2", "L3_ffn_bv", "L3_ffn_bo")], 1)

    def inner(m):
        return m.transpose(1, 0, 2).reshape(P, -1)

    f0 = np.concatenate([inner(a["L0_ffn_W1"]), inner(a["L0_ffn_W2"])], 1)
    l1 = np.concatenate([a["L1_xattn_Wq"].T, a["L1_xattn_Wk"].T, a["L1_xattn_Wv"].T,
                         inner(a["L1_xattn_Wo"].T.reshape(C1, P, P))], 1)
    f1 = np.concatenate([inner(a["L1_ffn_W1"].transpose(0, 2, 1)),
                         inner(a["L1_ffn_W2"].transpose(0, 2, 1).reshape(E * FC, P, P))], 1)
    l3 = np.concatenate([a["L3_xattn_Wq"], a["L3_xattn_Wk"], a["L3_xattn_Wv"],
                         inner(a["L3_xattn_Wout"].reshape(C3, P, P))], 1)
    f3 = np.concatenate([inner(a["L3_ffn_w1"]), inner(a["L3_ffn_w2"].reshape(E * FC, P, P))], 1)
    arrays = {
        "x": a["x"], "ctx": a["ctx_1024"], "ctxT": a["ctx_1024"].transpose(2, 0, 1).reshape(P, T * KC),
        "mask0": a["mask_BxSxS2_ik0"], "mask3": a["mask_BxS2_bk0"].reshape(1, T * KC),
        "small": small, "rows": rows, "f0": f0, "l1": l1, "f1": f1, "l3": l3, "f3": f3,
    }
    nc = bacc.Bacc("TRN2", target_bir_lowering=False, num_devices=1)
    feeds, args = {}, []
    for name, arr in arrays.items():
        arr = np.ascontiguousarray(arr)
        feeds[f"in_{name}"] = arr
        args.append(nc.dram_tensor(f"in_{name}", arr.shape, mybir.dt.from_np(arr.dtype), kind="ExternalInput").ap())
    args.append(nc.dram_tensor("out_x", (T, P, P), F32, kind="ExternalOutput").ap())
    build(nc, *args)
    r = run_bass_kernel_spmd(nc, [feeds], core_ids=[0])
    return r.results[0]["out_x"]
```
